# Optimizing a Trainium2 kernel written in Bass

```python
import numpy as np
import jax
import jax.numpy as jnp

def _softmax(x, axis=-1):
    return jax.nn.softmax(x, axis=axis)

def _gelu(x):
    return jax.nn.gelu(x, approximate=True)

def _silu(x):
    return jax.nn.silu(x)

def _sigmoid(x):
    return jax.nn.sigmoid(x)

def _layernorm(x, axis=-1, eps=1e-05):
    m = jnp.mean(x, axis=axis, keepdims=True)
    v = jnp.var(x, axis=axis, keepdims=True)
    return (x - m) / jnp.sqrt(v + eps)

def _scatter_add(tgt, idx, src, axis=0):
    return tgt.at[idx].add(src)

def _segment_sum(src, seg, n):
    return jax.ops.segment_sum(src, seg, n)
kernel_name = 'mk_sandwich_d2_jaxref_r8_ab2011'

def setup_inputs(seed: int=0):
    np.random.seed(seed)
    _w = jnp.asarray

    def _L0_attn_setup():
        import jax, jax.numpy as jnp
        import numpy as np
        B, T, C = (64, 32, 128)
        N_HEAD, HEAD_SIZE, KV_RANK = (16, 64, 128)
        BLOCK_SIZE = 32
        key = jax.random.key(seed)
        ks = jax.random.split(key, 5)
        HD = N_HEAD * HEAD_SIZE

        def init(k, shape):
            fan_in = shape[0]
            bound = 1.0 / np.sqrt(fan_in)
            return jax.random.uniform(k, shape, jnp.float32, -bound, bound)
        return {'x': jax.random.normal(ks[0], (B, T, C), jnp.float32), 'w_kv_down': init(ks[1], (C, KV_RANK)), 'w_kv_up': init(ks[2], (KV_RANK, 2 * HD)), 'w_q': init(ks[3], (C, HD)), 'w_out': init(ks[4], (HD, C))}
    _L0_attn_in = _L0_attn_setup()

    def _L0_ffn_setup():
        import jax, jax.numpy as jnp
        import numpy as np
        B, S, D, H, F = (4, 512, 128, 16, 512)
        CAP = 0.125
        ROPE_BASE = 10000.0

        def rmsnorm(x, g):
            return x * jax.lax.rsqrt(jnp.mean(x * x, -1, keepdims=True) + 1e-06) * g

        def rope(t, pos):
            hd = t.shape[-1]
            inv = 1.0 / ROPE_BASE ** (jnp.arange(0, hd, 2, dtype=jnp.float32) / hd)
            f = pos[:, None, :, None].astype(jnp.float32) * inv
            emb = jnp.concatenate([f, f], axis=-1)
            cos, sin = (jnp.cos(emb), jnp.sin(emb))
            rot = jnp.concatenate([-t[..., hd // 2:], t[..., :hd // 2]], axis=-1)
            return t * cos + rot * sin
        key = jax.random.key(seed)
        ks = jax.random.split(key, 9)
        scale = 0.02
        x = jax.random.normal(ks[0], (B, S, D), jnp.float32)
        causal = jnp.where(jnp.tril(jnp.ones((S, S), bool)), 0.0, -1000000000.0).astype(jnp.float32)
        attention_mask = jnp.broadcast_to(causal[None, None], (B, 1, S, S))
        position_ids = jnp.broadcast_to(jnp.arange(S, dtype=jnp.int32), (B, S))
        return {'x': x, 'attention_mask': attention_mask, 'position_ids': position_ids, 'router_w': jax.random.normal(ks[1], (D, 1), jnp.float32) * scale, 'router_b': jnp.zeros((1,), jnp.float32), 'wq': jax.random.normal(ks[2], (D, D), jnp.float32) * scale, 'wk': jax.random.normal(ks[3], (D, D), jnp.float32) * scale, 'wv': jax.random.normal(ks[4], (D, D), jnp.float32) * scale, 'wo': jax.random.normal(ks[5], (D, D), jnp.float32) * scale, 'w1': jax.random.normal(ks[6], (D, F), jnp.float32) * scale, 'w2': jax.random.normal(ks[7], (F, D), jnp.float32) * scale, 'ln1': jnp.ones((D,), jnp.float32), 'ln2': jnp.ones((D,), jnp.float32)}
    _L0_ffn_in = _L0_ffn_setup()

    def _L1_attn_setup():
        import math
        import jax, jax.numpy as jnp
        import numpy as np
        D_MODEL = 128
        N_HEADS = 16
        D_K = D_MODEL // N_HEADS
        EPS = 1e-06

        def _kernel_feats(data, P):
            norm = 1.0 / math.sqrt(math.sqrt(D_K))
            proj = jnp.einsum('bhnd,fd->bhnf', data * norm, P)
            return jax.nn.relu(proj) + 1e-06
        key = jax.random.key(seed)
        ks = jax.random.split(key, 10)
        B, N = (4, 1024)
        s = 1.0 / math.sqrt(D_MODEL)
        inp = {'x': jax.random.normal(ks[0], (B, N, D_MODEL), jnp.float32), 'Wq': jax.random.normal(ks[1], (D_MODEL, D_MODEL), jnp.float32) * s, 'bq': jnp.zeros((D_MODEL,), jnp.float32), 'Wk': jax.random.normal(ks[2], (D_MODEL, D_MODEL), jnp.float32) * s, 'bk': jnp.zeros((D_MODEL,), jnp.float32), 'Wv': jax.random.normal(ks[3], (D_MODEL, D_MODEL), jnp.float32) * s, 'bv': jnp.zeros((D_MODEL,), jnp.float32), 'Wo': jax.random.normal(ks[4], (D_MODEL, D_MODEL), jnp.float32) * s, 'bo': jnp.zeros((D_MODEL,), jnp.float32), 'P': jax.random.normal(ks[5], (D_K, D_K), jnp.float32)}
        return inp
    _L1_attn_in = _L1_attn_setup()

    def _L1_ffn_setup():
        import jax, jax.numpy as jnp
        import numpy as np
        DIM = 128
        DEPTH = 6
        HEADS = 16
        DIM_HEAD = 64
        WINDOW = 32
        INNER = HEADS * DIM_HEAD
        DIM_INNER = int(DIM * 4 * 2 / 3)
        QK_SCALE = 8.0

        def shift_tokens(t):
            a, s = jnp.split(t, 2, -1)
            s = jnp.pad(s, ((0, 0), (1, 0), (0, 0)))[:, :-1]
            return jnp.concatenate([a, s], -1)

        def l2norm(t):
            return t / jnp.maximum(jnp.linalg.norm(t, axis=-1, keepdims=True), 1e-12)

        def rotate_half(x):
            x1, x2 = jnp.split(x, 2, -1)
            return jnp.concatenate([-x2, x1], -1)

        def rotary_tables(n):
            half = jnp.arange(0, DIM_HEAD, 2, dtype=jnp.float32)
            inv_freq = 1.0 / 10000.0 ** (half / DIM_HEAD)
            t = jnp.arange(n, dtype=jnp.float32)
            freqs = t[:, None] * inv_freq[None, :]
            freqs = jnp.concatenate([freqs, freqs], -1)
            base_scale = (half + 0.4 * DIM_HEAD) / (1.4 * DIM_HEAD)
            power = (t - n // 2) / (WINDOW // 2)
            scale = base_scale[None, :] ** power[:, None]
            scale = jnp.concatenate([scale, scale], -1)
            return (freqs, scale)

        def local_attention(q, k, v):
            b, h, n, d = q.shape
            w = WINDOW
            nw = n // w
            bq = q.reshape(b, h, nw, w, d)
            bk = k.reshape(b, h, nw, w, d)
            bv = v.reshape(b, h, nw, w, d)

            def look(t):
                p = jnp.pad(t, ((0, 0), (0, 0), (1, 0), (0, 0), (0, 0)))
                return jnp.concatenate([p[:, :, :nw], p[:, :, 1:]], axis=3)
            bk2, bv2 = (look(bk), look(bv))
            seq = jnp.arange(n).reshape(nw, w)
            seq_p = jnp.pad(seq, ((1, 0), (0, 0)), constant_values=-1)
            jt = jnp.concatenate([seq_p[:nw], seq_p[1:]], axis=1)
            it = seq[:, :, None]
            jb = jt[:, None, :]
            mask = (it < jb) | (it > jb + w) | (jb == -1)
            sim = jnp.einsum('bhwie,bhwje->bhwij', bq, bk2) * QK_SCALE
            sim = jnp.where(mask, -jnp.finfo(sim.dtype).max, sim)
            attn = jax.nn.softmax(sim, -1)
            out = jnp.einsum('bhwij,bhwje->bhwie', attn, bv2)
            return out.reshape(b, h, n, d)

        def attn_layer(x, Wqkv, qs, ksc, Wo):
            b, n, _ = x.shape
            qkv = x @ Wqkv
            q, k, v = jnp.split(qkv, 3, -1)
            sh = lambda t: t.reshape(b, n, HEADS, DIM_HEAD).transpose(0, 2, 1, 3)
            q, k, v = (sh(q), sh(k), sh(v))
            q = l2norm(q) * qs
            k = l2norm(k) * ksc
            freqs, scale = rotary_tables(n)
            cos, sin = (jnp.cos(freqs), jnp.sin(freqs))
            q = q * cos * scale + rotate_half(q) * sin * scale
            inv = 1.0 / scale
            k = k * cos * inv + rotate_half(k) * sin * inv
            out = local_attention(q, k, v)
            out = out.transpose(0, 2, 1, 3).reshape(b, n, INNER)
            return out @ Wo

        def ffn_layer(x, g, bln, W1, b1, W2, b2):
            mu = x.mean(-1, keepdims=True)
            var = ((x - mu) ** 2).mean(-1, keepdims=True)
            xn = (x - mu) / jnp.sqrt(var + 1e-05) * g + bln
            hg = xn @ W1 + b1
            a, gate = jnp.split(hg, 2, -1)
            return a * jax.nn.gelu(gate, approximate=False) @ W2 + b2
        key = jax.random.key(seed)
        ks = jax.random.split(key, 8)
        B, N = (2, 256)
        init = lambda k, shape: jax.random.normal(k, shape, jnp.float32) * 0.02
        return {'x': jax.random.normal(ks[0], (B, N, DIM), jnp.float32), 'Wqkv': init(ks[1], (DEPTH, DIM, 3 * INNER)), 'q_scale': jnp.ones((DEPTH, DIM_HEAD), jnp.float32), 'k_scale': jnp.ones((DEPTH, DIM_HEAD), jnp.float32), 'Wo': init(ks[2], (DEPTH, INNER, DIM)), 'ln_g': jnp.ones((DEPTH, DIM), jnp.float32), 'ln_b': jnp.zeros((DEPTH, DIM), jnp.float32), 'W1': init(ks[3], (DEPTH, DIM, 2 * DIM_INNER)), 'b1': jnp.zeros((DEPTH, 2 * DIM_INNER), jnp.float32), 'W2': init(ks[4], (DEPTH, DIM_INNER, DIM)), 'b2': jnp.zeros((DEPTH, DIM), jnp.float32)}
    _L1_ffn_in = _L1_ffn_setup()
    _d = {'L0_attn_x': _L0_attn_in['x'], 'L0_attn_w_kv_down': _L0_attn_in['w_kv_down'], 'L0_attn_w_kv_up': _L0_attn_in['w_kv_up'], 'L0_attn_w_q': _L0_attn_in['w_q'], 'L0_attn_w_out': _L0_attn_in['w_out'], 'L0_ffn_attention_mask': _L0_ffn_in['attention_mask'], 'L0_ffn_position_ids': _L0_ffn_in['position_ids'], 'L0_ffn_router_w': _L0_ffn_in['router_w'], 'L0_ffn_router_b': _L0_ffn_in['router_b'], 'L0_ffn_wq': _L0_ffn_in['wq'], 'L0_ffn_wk': _L0_ffn_in['wk'], 'L0_ffn_wv': _L0_ffn_in['wv'], 'L0_ffn_wo': _L0_ffn_in['wo'], 'L0_ffn_w1': _L0_ffn_in['w1'], 'L0_ffn_w2': _L0_ffn_in['w2'], 'L0_ffn_ln1': _L0_ffn_in['ln1'], 'L0_ffn_ln2': _L0_ffn_in['ln2'], 'L1_attn_Wq': _L1_attn_in['Wq'], 'L1_attn_bq': _L1_attn_in['bq'], 'L1_attn_Wk': _L1_attn_in['Wk'], 'L1_attn_bk': _L1_attn_in['bk'], 'L1_attn_Wv': _L1_attn_in['Wv'], 'L1_attn_bv': _L1_attn_in['bv'], 'L1_attn_Wo': _L1_attn_in['Wo'], 'L1_attn_bo': _L1_attn_in['bo'], 'L1_attn_P': _L1_attn_in['P'], 'L1_ffn_Wqkv': _L1_ffn_in['Wqkv'], 'L1_ffn_q_scale': _L1_ffn_in['q_scale'], 'L1_ffn_k_scale': _L1_ffn_in['k_scale'], 'L1_ffn_Wo': _L1_ffn_in['Wo'], 'L1_ffn_ln_g': _L1_ffn_in['ln_g'], 'L1_ffn_ln_b': _L1_ffn_in['ln_b'], 'L1_ffn_W1': _L1_ffn_in['W1'], 'L1_ffn_b1': _L1_ffn_in['b1'], 'L1_ffn_W2': _L1_ffn_in['W2'], 'L1_ffn_b2': _L1_ffn_in['b2']}
    _x0 = _d['L0_attn_x']
    _d['L0_attn_x'] = jax.random.normal(jax.random.fold_in(jax.random.key(seed), 1), (4, 1024, 128), dtype=_x0.dtype)
    del _x0
    return _d

def reference(L0_attn_x, L0_attn_w_kv_down, L0_attn_w_kv_up, L0_attn_w_q, L0_attn_w_out, L0_ffn_attention_mask, L0_ffn_position_ids, L0_ffn_router_w, L0_ffn_router_b, L0_ffn_wq, L0_ffn_wk, L0_ffn_wv, L0_ffn_wo, L0_ffn_w1, L0_ffn_w2, L0_ffn_ln1, L0_ffn_ln2, L1_attn_Wq, L1_attn_bq, L1_attn_Wk, L1_attn_bk, L1_attn_Wv, L1_attn_bv, L1_attn_Wo, L1_attn_bo, L1_attn_P, L1_ffn_Wqkv, L1_ffn_q_scale, L1_ffn_k_scale, L1_ffn_Wo, L1_ffn_ln_g, L1_ffn_ln_b, L1_ffn_W1, L1_ffn_b1, L1_ffn_W2, L1_ffn_b2):

    def _L0_attn_ref(x, w_kv_down, w_kv_up, w_q, w_out):
        import jax, jax.numpy as jnp
        import numpy as np
        B, T, C = (64, 32, 128)
        N_HEAD, HEAD_SIZE, KV_RANK = (16, 64, 128)
        BLOCK_SIZE = 32
        Bx, Tx, Cx = x.shape
        HD = N_HEAD * HEAD_SIZE
        latent_kv = x @ w_kv_down
        kv = latent_kv @ w_kv_up
        k, v = (kv[..., :HD], kv[..., HD:])
        k = k.reshape(Bx, Tx, N_HEAD, HEAD_SIZE)
        v = v.reshape(Bx, Tx, N_HEAD, HEAD_SIZE)
        q = (x @ w_q).reshape(Bx, Tx, N_HEAD, HEAD_SIZE)
        scale = HEAD_SIZE ** (-0.5)
        att = jnp.einsum('bqhd,bkhd->bhqk', q, k) * scale
        causal = jnp.tril(jnp.ones((Tx, Tx), dtype=bool))
        att = jnp.where(causal, att, -jnp.inf)
        att = jax.nn.softmax(att, axis=-1)
        y = jnp.einsum('bhqk,bkhd->bqhd', att, v)
        y = y.reshape(Bx, Tx, HD)
        return y @ w_out

    def _L0_ffn_ref(x, attention_mask, position_ids, router_w, router_b, wq, wk, wv, wo, w1, w2, ln1, ln2):
        import jax, jax.numpy as jnp
        import numpy as np
        B, S, D, H, F = (4, 512, 128, 16, 512)
        CAP = 0.125
        ROPE_BASE = 10000.0

        def rmsnorm(x, g):
            return x * jax.lax.rsqrt(jnp.mean(x * x, -1, keepdims=True) + 1e-06) * g

        def rope(t, pos):
            hd = t.shape[-1]
            inv = 1.0 / ROPE_BASE ** (jnp.arange(0, hd, 2, dtype=jnp.float32) / hd)
            f = pos[:, None, :, None].astype(jnp.float32) * inv
            emb = jnp.concatenate([f, f], axis=-1)
            cos, sin = (jnp.cos(emb), jnp.sin(emb))
            rot = jnp.concatenate([-t[..., hd // 2:], t[..., :hd // 2]], axis=-1)
            return t * cos + rot * sin
        b, s, d = x.shape
        hd = d // H
        weights = (x @ router_w)[..., 0] + router_b[0]
        k = int(CAP * s)
        topv, topi = jax.lax.top_k(weights, k)
        thr = topv[:, -1]
        sel_mask = (weights > thr[:, None]).astype(x.dtype)
        kc = k - 1
        sel_idx = jnp.sort(topi[:, :kc], axis=1)
        bidx = jnp.arange(b)[:, None]
        x_sel = x[bidx, sel_idx]
        pos_sel = position_ids[bidx, sel_idx]
        w_sel = weights[bidx, sel_idx]
        m = attention_mask[:, 0]
        m_sel = m[bidx[:, :, None], sel_idx[:, :, None], sel_idx[:, None, :]]
        hn = rmsnorm(x_sel, ln1)

        def heads(t):
            return t.reshape(b, kc, H, hd).transpose(0, 2, 1, 3)
        q = rope(heads(hn @ wq), pos_sel)
        kk = rope(heads(hn @ wk), pos_sel)
        v = heads(hn @ wv)
        sc = jnp.einsum('bhqd,bhkd->bhqk', q, kk) / np.sqrt(hd).astype(np.float32)
        sc = sc + m_sel[:, None]
        a = jax.nn.softmax(sc, axis=-1)
        o = jnp.einsum('bhqk,bhkd->bhqd', a, v).transpose(0, 2, 1, 3).reshape(b, kc, d) @ wo
        x1 = x_sel + o
        x2 = x1 + jax.nn.gelu(rmsnorm(x1, ln2) @ w1) @ w2
        proc = x2 * w_sel[..., None]
        out = jnp.zeros_like(x).at[bidx, sel_idx].set(proc)
        return out + x * (1.0 - sel_mask)[..., None]

    def _L1_attn_ref(x, Wq, bq, Wk, bk, Wv, bv, Wo, bo, P):
        import math
        import jax, jax.numpy as jnp
        import numpy as np
        D_MODEL = 128
        N_HEADS = 16
        D_K = D_MODEL // N_HEADS
        EPS = 1e-06

        def _kernel_feats(data, P):
            norm = 1.0 / math.sqrt(math.sqrt(D_K))
            proj = jnp.einsum('bhnd,fd->bhnf', data * norm, P)
            return jax.nn.relu(proj) + 1e-06
        B, N, _ = x.shape
        H, dk = (N_HEADS, D_K)

        def heads(W, b):
            y = x @ W.T + b
            return y.reshape(B, N, H, dk).transpose(0, 2, 1, 3)
        Q, K, V = (heads(Wq, bq), heads(Wk, bk), heads(Wv, bv))
        Qf = _kernel_feats(Q, P)
        Kf = _kernel_feats(K, P)
        KV = jnp.einsum('bhnf,bhnd->bhfd', Kf, V)
        Ksum = Kf.sum(axis=2)
        denom = jnp.einsum('bhnf,bhf->bhn', Qf, Ksum) + EPS
        out = jnp.einsum('bhnf,bhfd->bhnd', Qf, KV) / denom[..., None]
        out = out.transpose(0, 2, 1, 3).reshape(B, N, D_MODEL)
        return out @ Wo.T + bo

    def _L1_ffn_ref(x, Wqkv, q_scale, k_scale, Wo, ln_g, ln_b, W1, b1, W2, b2):
        import jax, jax.numpy as jnp
        import numpy as np
        DIM = 128
        DEPTH = 6
        HEADS = 16
        DIM_HEAD = 64
        WINDOW = 32
        INNER = HEADS * DIM_HEAD
        DIM_INNER = int(DIM * 4 * 2 / 3)
        QK_SCALE = 8.0

        def shift_tokens(t):
            a, s = jnp.split(t, 2, -1)
            s = jnp.pad(s, ((0, 0), (1, 0), (0, 0)))[:, :-1]
            return jnp.concatenate([a, s], -1)

        def l2norm(t):
            return t / jnp.maximum(jnp.linalg.norm(t, axis=-1, keepdims=True), 1e-12)

        def rotate_half(x):
            x1, x2 = jnp.split(x, 2, -1)
            return jnp.concatenate([-x2, x1], -1)

        def rotary_tables(n):
            half = jnp.arange(0, DIM_HEAD, 2, dtype=jnp.float32)
            inv_freq = 1.0 / 10000.0 ** (half / DIM_HEAD)
            t = jnp.arange(n, dtype=jnp.float32)
            freqs = t[:, None] * inv_freq[None, :]
            freqs = jnp.concatenate([freqs, freqs], -1)
            base_scale = (half + 0.4 * DIM_HEAD) / (1.4 * DIM_HEAD)
            power = (t - n // 2) / (WINDOW // 2)
            scale = base_scale[None, :] ** power[:, None]
            scale = jnp.concatenate([scale, scale], -1)
            return (freqs, scale)

        def local_attention(q, k, v):
            b, h, n, d = q.shape
            w = WINDOW
            nw = n // w
            bq = q.reshape(b, h, nw, w, d)
            bk = k.reshape(b, h, nw, w, d)
            bv = v.reshape(b, h, nw, w, d)

            def look(t):
                p = jnp.pad(t, ((0, 0), (0, 0), (1, 0), (0, 0), (0, 0)))
                return jnp.concatenate([p[:, :, :nw], p[:, :, 1:]], axis=3)
            bk2, bv2 = (look(bk), look(bv))
            seq = jnp.arange(n).reshape(nw, w)
            seq_p = jnp.pad(seq, ((1, 0), (0, 0)), constant_values=-1)
            jt = jnp.concatenate([seq_p[:nw], seq_p[1:]], axis=1)
            it = seq[:, :, None]
            jb = jt[:, None, :]
            mask = (it < jb) | (it > jb + w) | (jb == -1)
            sim = jnp.einsum('bhwie,bhwje->bhwij', bq, bk2) * QK_SCALE
            sim = jnp.where(mask, -jnp.finfo(sim.dtype).max, sim)
            attn = jax.nn.softmax(sim, -1)
            out = jnp.einsum('bhwij,bhwje->bhwie', attn, bv2)
            return out.reshape(b, h, n, d)

        def attn_layer(x, Wqkv, qs, ksc, Wo):
            b, n, _ = x.shape
            qkv = x @ Wqkv
            q, k, v = jnp.split(qkv, 3, -1)
            sh = lambda t: t.reshape(b, n, HEADS, DIM_HEAD).transpose(0, 2, 1, 3)
            q, k, v = (sh(q), sh(k), sh(v))
            q = l2norm(q) * qs
            k = l2norm(k) * ksc
            freqs, scale = rotary_tables(n)
            cos, sin = (jnp.cos(freqs), jnp.sin(freqs))
            q = q * cos * scale + rotate_half(q) * sin * scale
            inv = 1.0 / scale
            k = k * cos * inv + rotate_half(k) * sin * inv
            out = local_attention(q, k, v)
            out = out.transpose(0, 2, 1, 3).reshape(b, n, INNER)
            return out @ Wo

        def ffn_layer(x, g, bln, W1, b1, W2, b2):
            mu = x.mean(-1, keepdims=True)
            var = ((x - mu) ** 2).mean(-1, keepdims=True)
            xn = (x - mu) / jnp.sqrt(var + 1e-05) * g + bln
            hg = xn @ W1 + b1
            a, gate = jnp.split(hg, 2, -1)
            return a * jax.nn.gelu(gate, approximate=False) @ W2 + b2
        for i in range(DEPTH):
            x = attn_layer(shift_tokens(x), Wqkv[i], q_scale[i], k_scale[i], Wo[i]) + x
            x = ffn_layer(shift_tokens(x), ln_g[i], ln_b[i], W1[i], b1[i], W2[i], b2[i]) + x
        return x
    x = L0_attn_x
    x = x + _layernorm(_L0_attn_ref(_layernorm(x, axis=-1), L0_attn_w_kv_down, L0_attn_w_kv_up, L0_attn_w_q, L0_attn_w_out), axis=-1)
    x = x + _layernorm(_L0_ffn_ref(_layernorm(x, axis=-1), L0_ffn_attention_mask, L0_ffn_position_ids, L0_ffn_router_w, L0_ffn_router_b, L0_ffn_wq, L0_ffn_wk, L0_ffn_wv, L0_ffn_wo, L0_ffn_w1, L0_ffn_w2, L0_ffn_ln1, L0_ffn_ln2), axis=-1)
    x = x + _layernorm(_L1_attn_ref(_layernorm(x, axis=-1), L1_attn_Wq, L1_attn_bq, L1_attn_Wk, L1_attn_bk, L1_attn_Wv, L1_attn_bv, L1_attn_Wo, L1_attn_bo, L1_attn_P), axis=-1)
    x = x + _layernorm(_L1_ffn_ref(_layernorm(x, axis=-1), L1_ffn_Wqkv, L1_ffn_q_scale, L1_ffn_k_scale, L1_ffn_Wo, L1_ffn_ln_g, L1_ffn_ln_b, L1_ffn_W1, L1_ffn_b1, L1_ffn_W2, L1_ffn_b2), axis=-1)
    return x

_drawn_inputs = setup_inputs


def setup_inputs(seed=0):
    import zlib

    import numpy as np

    out = dict(_drawn_inputs(seed))
    spreads = {'L0_ffn_ln1': (1.0, 0.6),
     'L0_ffn_ln2': (1.0, 0.6),
     'L1_attn_bq': (0.0, 0.442),
     'L1_attn_bk': (0.0, 0.8),
     'L1_attn_bv': (0.0, 0.1),
     'L1_attn_bo': (0.0, 0.1),
     'L1_ffn_q_scale': (1.0, 0.6),
     'L1_ffn_k_scale': (1.0, 0.6),
     'L1_ffn_ln_g': (1.0, 0.6),
     'L1_ffn_ln_b': (0.0, 0.8),
     'L1_ffn_b1': (0.0, 0.8),
     'L1_ffn_b2': (0.0, 0.8)}
    factors = {'L0_ffn_router_w': 6.664,
     'L0_ffn_wq': 8.0,
     'L0_ffn_wk': 8.0,
     'L0_ffn_wv': 8.0,
     'L0_ffn_wo': 8.0,
     'L0_ffn_w1': 7.282,
     'L0_ffn_w2': 6.962,
     'L1_ffn_W1': 6.65,
     'L1_ffn_W2': 6.531}
    for name, (base, spread) in spreads.items():
        noise = np.random.default_rng([zlib.crc32(name.encode()), seed]).standard_normal(out[name].shape)
        drawn = base * np.exp(spread * noise) if base else spread * noise
        out[name] = jnp.asarray(drawn.astype(out[name].dtype))
    for name, factor in factors.items():
        out[name] = (out[name] * factor).astype(out[name].dtype)
    return out
```

```python
from contextlib import ExitStack

import concourse.bass as bass
from concourse import mybir

F32 = mybir.dt.float32
I32 = mybir.dt.int32
U32 = mybir.dt.uint32
ALU = mybir.AluOpType
ACT = mybir.ActivationFunctionType
AX = mybir.AxisListType

P = 128
B, T, C = 4, 1024, 128
NT = B * T // P
TPB = T // P
LN_EPS = 1e-5


class Item:

    def __init__(self, index, t=0, slot=0, turn=0, units=None):
        self.index, self.t, self.slot, self.turn, self.units = index, t, slot, turn, units

    def has(self, ahead):
        return self.units is None or self.t + ahead < self.units


SEED = 8


def reached(item, per, k, back=0, seed=SEED):
    return (item.index + (seed - back)) * per + k


def pipeline(eng, base, units, unroll, stages):
    lag_max = max(lag for lag, _ in stages)
    peeled = -(-lag_max // unroll) * unroll

    def step(s, static, u, turn):
        for lag, do in stages:
            if static and not 0 <= s - lag < units:
                continue
            do(Item(base + (s - lag), s - lag, (u - lag) % unroll, turn + (u - lag) // unroll,
                    units if static else None))

    for s in range(peeled):
        step(s, True, s % unroll, s // unroll)
    with eng.Fori(0, (units - peeled) // unroll, 1) as k:
        for u in range(unroll):
            step(k * unroll + (peeled + u), False, u, k + peeled // unroll)
    for s in range(units, units + lag_max):
        step(s, True, s % unroll, s // unroll)


class Normalizer:

    G = 4
    W = NT // G

    def __init__(self, nc, ctx):
        def sb(n, shape):
            return ctx.enter_context(nc.sbuf_tensor("n_" + n, shape, F32))

        def sem(n):
            return ctx.enter_context(nc.semaphore("n_" + n))

        self.nc, self.runs, self.residual_runs = nc, 0, 0
        self.squares = sb("squares", [P, NT, C])
        self.mean, self.var, self.rstd, self.power = (
            sb("mean", [P, NT]), sb("var", [P, NT]), sb("rstd", [P, NT]), sb("power", [P, NT]))
        self.power_set = sem("power_set")
        self.summed, self.centred, self.squared, self.var_done, self.rstd_done, self.scaled, self.ended = (
            sem("summed"), sem("centred"), sem("squared"), sem("var_done"), sem("rstd_done"), sem("scaled"), sem("ended"))

    def run(self, src, dst, eps, residual=None):
        nc, G, W, n, r = self.nc, self.G, self.W, self.runs, self.residual_runs
        squares, mean, var, rstd, power = self.squares, self.mean, self.var, self.rstd, self.power
        power_set, summed, centred, squared = self.power_set, self.summed, self.centred, self.squared
        var_done, rstd_done, scaled, ended = self.var_done, self.rstd_done, self.scaled, self.ended
        self.runs += 1
        self.residual_runs += residual is not None

        def tiles(g):
            return slice(W * g, W * g + W)

        with nc.Block() as block:
            @block.vector
            def _(dve):
                if n == 0:
                    dve.memset(power[:], -0.5).then_inc(power_set, 1)
                for g in range(G):
                    dve.tensor_reduce(mean[:, tiles(g)], src[:, tiles(g), :], AX.X, ALU.add).then_inc(summed, 1)
                dve.wait_ge(summed, n * (G + 1) + G)
                dve.tensor_scalar(mean[:], mean[:], 1.0 / C, None, ALU.mult).then_inc(summed, 1)
                dve.wait_ge(summed, (n + 1) * (G + 1))
                for g in range(G):
                    dve.tensor_tensor(dst[:, tiles(g), :], src[:, tiles(g), :],
                                      mean[:, tiles(g)].unsqueeze(2).to_broadcast([P, W, C]),
                                      ALU.subtract).then_inc(centred, 1)
                for g in range(G):
                    dve.wait_ge(squared, n * G + g + 1)
                    dve.tensor_reduce(var[:, tiles(g)], squares[:, tiles(g), :], AX.X, ALU.add).then_inc(var_done, 1)
                    dve.wait_ge(var_done, 2 * (n * G + g) + 1)
                    dve.tensor_scalar(var[:, tiles(g)], var[:, tiles(g)], 1.0 / C, eps, ALU.mult, ALU.add).then_inc(var_done, 1)
                for g in range(G):
                    dve.wait_ge(rstd_done, n * G + g + 1)
                    dve.tensor_tensor(dst[:, tiles(g), :], dst[:, tiles(g), :],
                                      rstd[:, tiles(g)].unsqueeze(2).to_broadcast([P, W, C]), ALU.mult).then_inc(scaled, 1)
                    if residual is not None:
                        dve.wait_ge(scaled, n * G + g + 1)
                        dve.tensor_tensor(residual[:, tiles(g), :], residual[:, tiles(g), :], dst[:, tiles(g), :],
                                          ALU.add).then_inc(ended, 1)
                dve.wait_ge(scaled, (n + 1) * G)
                if residual is not None:
                    dve.wait_ge(ended, (r + 1) * G)

            @block.scalar
            def _(act):
                for g in range(G):
                    act.wait_ge(centred, n * G + g + 1)
                    act.activation(squares[:, tiles(g), :], dst[:, tiles(g), :], ACT.Square).then_inc(squared, 1)

            @block.gpsimd
            def _(pool):
                pool.wait_ge(power_set, 1)
                for g in range(G):
                    pool.wait_ge(var_done, 2 * (n * G + g + 1))
                    pool.tensor_tensor(rstd[:, tiles(g)], var[:, tiles(g)], power[:, tiles(g)], ALU.pow).then_inc(rstd_done, 1)


def causal_attention(nc, A, xn, z, ident, psum):
    H, D = 16, 64
    PAIRS, QT = H // 2, TPB
    UNITS, U = PAIRS * QT, 2 * QT
    SEEDED = 24
    with ExitStack() as ctx:
        def sb(name, shape):
            return ctx.enter_context(nc.sbuf_tensor("a_" + name, shape, F32))

        def sem(name):
            return ctx.enter_context(nc.semaphore("a_" + name))

        w_down, w_up, w_q = sb("w_down", [P, P]), sb("w_up", [P, 2 * H * D]), sb("w_q", [P, H * D])
        w_out = sb("w_out", [P, PAIRS, C])
        causal = sb("causal", [P, P])
        w_pair = sb("w_pair", [P, 3, P])
        x_b = sb("x_b", [P, TPB, C])
        xT, latT = sb("xT", [P, T]), sb("latT", [P, T])
        qT, kT, V = sb("qT", [P, 2, T]), sb("kT", [P, 2, T]), sb("V", [P, 2, TPB, P])
        probs = sb("probs", [P, 2, 2, T])
        pT = sb("pT", [P, 2, 2, T])
        nmax, rsum, rinv = sb("nmax", [P, 2, 2]), sb("rsum", [P, 2, 2]), sb("rinv", [P, 2, 2])
        oT = sb("oT", [P, PAIRS, T])

        S = [psum[:, 2 * h:2 * h + 2, :].rearrange("p a n -> p (a n)") for h in range(2)]
        TR = [psum[:, 4, :], psum[:, 5, :]]
        OB, PB = psum[:, 6, :], psum[:, 7, :]

        loaded, held = sem("loaded"), sem("held")
        x_copied, x_turned, x_in, lat_done, lat_in, out_done, out_in = (
            sem("x_copied"), sem("x_turned"), sem("x_in"), sem("lat_done"), sem("lat_in"), sem("out_done"), sem("out_in"))
        w_staged, projected, proj_in = sem("w_staged"), sem("projected"), sem("proj_in")
        scored, masked, maxed, exped, inverted, scaled, turned, pT_in, attended, o_in = (
            sem("scored"), sem("masked"), sem("maxed"), sem("exped"), sem("inverted"), sem("scaled"), sem("turned"),
            sem("pT_in"), sem("attended"), sem("o_in"))
        PER = {scored: 2, masked: 2, maxed: 2, exped: 2, inverted: 2, scaled: 2, turned: 4, pT_in: 4, attended: 1, o_in: 1}

        def at(s, it, k, back=0):
            return s, reached(it, PER[s], k, back, SEEDED)

        def at_pair(s, it, b, per, k, back=0):
            return s, (b * PAIRS + it.turn * 2 + (it.slot // QT + 2 - back)) * per + k

        def seed(eng, sems):
            for s in sems:
                eng.sem_inc(s, PER[s] * SEEDED)

        block = ctx.enter_context(nc.Block())

        @block.sync
        def _(sp):
            sp.dma_start(w_down[:], A["w_kv_down"]).then_inc(loaded, 16)
            sp.dma_start(w_q[:], A["w_q"]).then_inc(loaded, 16)
            sp.dma_start(w_up[:], A["w_kv_up"]).then_inc(loaded, 16)
            sp.dma_start(causal[:], A["causal"]).then_inc(loaded, 16)
            sp.dma_start(w_out[:], A["w_out"].rearrange("(h p) c -> p h c", p=P)).then_inc(loaded, 16)

        @block.gpsimd
        def _(pool):
            pool.sem_inc(w_staged, 2)
            pool.wait_ge(loaded, 80)
            with pool.Fori(0, B, 1) as b:
                def stage(it):
                    if it.slot % QT:
                        return
                    pool.wait_ge(*at_pair(projected, it, b, 6, 0))
                    for n, (w, off) in enumerate([(w_q, 0), (w_up, 0), (w_up, H * D)]):
                        pair = it.turn * 2 + it.slot // QT
                        pool.sem_inc(held, 1)
                        src = w[:, off:off + H * D].rearrange("p (a n) -> p a n", n=P)
                        i = pool.tensor_copy(w_pair[:, n:n + 1, :], src[:, bass.ds(pair, 1), :])
                    i.then_inc(w_staged, 1)
                with pool.Fori(0, PAIRS // 2, 1) as k:
                    for u in (0, QT):
                        stage(Item(0, 0, u, k))

        @block.tensor
        def _(pe):
            seed(pe, [scored, turned, attended])
            pe.sem_inc(projected, 12)
            pe.wait_ge(loaded, 80)
            with pe.Fori(0, B, 1) as b:
                pe.wait_ge(x_copied, b + 1)
                for c in range(2):
                    for j in range(4):
                        m = pe.transpose(TR[c][:, j * P:(j + 1) * P], x_b[:, 4 * c + j, :], ident[:])
                    m.then_inc(x_turned, 1)
                for c in range(2):
                    pe.wait_ge(x_in, 2 * b + c + 1)
                    pe.matmul([OB, PB][c], w_down[:], xT[:, 512 * c:512 * c + 512], start=True, stop=True).then_inc(lat_done, 1)

                def score(h):
                    r = slice(64 * h, 64 * h + 64)

                    def do(it):
                        i, pb = it.slot % QT, it.slot // QT % 2
                        if i == 0 and h == 0:
                            pe.wait_ge(*at_pair(proj_in, it, b, 6, 4))
                        pe.wait_ge(*at(exped, it, h + 1, 1))
                        w = (i + 1) * P
                        for c in range(0, w, 512):
                            n = min(512, w - c)
                            m = pe.matmul(S[h][:, c:c + n], qT[r, pb, i * P:(i + 1) * P], kT[r, pb, c:c + n],
                                          start=True, stop=True)
                        m.then_inc(scored, 1)
                    return do

                def turn(h):
                    def do(it):
                        i, par = it.slot % QT, it.slot % 2
                        pe.wait_ge(*at(scaled, it, h + 1))
                        chunks = range(0, i + 1, 4)
                        for n, c in enumerate(chunks):
                            bank = TR[(n + h) % 2]
                            pe.wait_ge(*at(pT_in, it, 2 * h + n))
                            if len(chunks) == 1 or n == 0:
                                pe.wait_ge(*at(pT_in, it, 2 * h))
                            for k in range(c, min(c + 4, i + 1)):
                                m = pe.transpose(bank[:, (k - c) * P:(k - c + 1) * P],
                                                 probs[:, par, h, k * P:(k + 1) * P], ident[:])
                            m.then_inc(turned, 2 // len(chunks))
                    return do

                def attend(it):
                    i, pb, par = it.slot % QT, it.slot // QT % 2, it.slot % 2
                    if i == 0:
                        pe.wait_ge(*at_pair(proj_in, it, b, 6, 6))
                    pe.wait_ge(*at(pT_in, it, 4))
                    pe.wait_ge(*at(o_in, it, 1, 1))
                    for k in range(i + 1):
                        for h in range(2):
                            m = pe.matmul(OB[64 * h:64 * h + 64, 0:P], V[:, pb, k, 64 * h:64 * h + 64],
                                          pT[:, par, h, k * P:(k + 1) * P], start=(k == 0), stop=(k == i),
                                          tile_position=(0, 64 * h))
                    m.then_inc(attended, 1)

                def project(it):
                    n = it.slot % QT
                    if n == 0:
                        pe.wait_ge(*at_pair(w_staged, it, b, 1, 1))
                        pe.wait_ge(lat_in, 2 * b + 2)
                    if n >= 6:
                        return
                    pe.wait_ge(*at_pair(proj_in, it, b, 6, n))
                    c = n % 2
                    if n < 4:
                        m = pe.matmul(PB, w_pair[:, n // 2, :], [xT, latT][n // 2][:, 512 * c:512 * c + 512],
                                      start=True, stop=True)
                    else:
                        for j in range(4):
                            m = pe.matmul(PB[:, j * P:(j + 1) * P], latT[:, (4 * c + j) * P:(4 * c + j + 1) * P],
                                          w_pair[:, 2, :], start=True, stop=True)
                    m.then_inc(projected, 1)

                pipeline(pe, b * UNITS, UNITS, U, [
                    (8, score(0)), (9, turn(0)), (0, project), (8, score(1)), (9, turn(1)), (10, attend)])
                done = Item(b * UNITS + UNITS)
                pe.wait_ge(*at(o_in, done, 0))
                for i in range(TPB):
                    pe.wait_ge(out_in, b * TPB + i + 1)
                    for p in range(PAIRS):
                        m = pe.matmul([OB, PB][i % 2][:, 0:C], oT[:, p, i * P:(i + 1) * P], w_out[:, p, :],
                                      start=(p == 0), stop=(p == PAIRS - 1))
                    m.then_inc(out_done, 1)

        @block.scalar
        def _(act):
            seed(act, [exped, pT_in])
            act.sem_inc(proj_in, 12)
            with act.Fori(0, B, 1) as b:
                for c in range(2):
                    act.wait_ge(x_turned, 2 * b + c + 1)
                    act.activation(xT[:, 512 * c:512 * c + 512], TR[c], ACT.Copy).then_inc(x_in, 1)
                for c in range(2):
                    act.wait_ge(lat_done, 2 * b + c + 1)
                    act.activation(latT[:, 512 * c:512 * c + 512], [OB, PB][c], ACT.Copy).then_inc(lat_in, 1)

                def take_projection(it):
                    n, pb = it.slot % QT, it.slot // QT % 2
                    if n >= 6:
                        return
                    c = n % 2
                    act.wait_ge(*at_pair(projected, it, b, 6, n + 1))
                    if n < 4:
                        act.wait_ge(*at(scored, it, 2, 9 + n))
                    else:
                        act.wait_ge(*at(attended, it, 1, 9 + n))
                    if n < 2:
                        i = act.activation(qT[:, pb, 512 * c:512 * c + 512], PB, ACT.Copy, scale=float(D) ** -0.5)
                    elif n < 4:
                        i = act.activation(kT[:, pb, 512 * c:512 * c + 512], PB, ACT.Copy)
                    else:
                        i = act.activation(V[:, pb, 4 * c:4 * c + 4, :], PB.rearrange("p (a n) -> p a n", a=4), ACT.Copy)
                    i.then_inc(proj_in, 1)

                def exps(h):
                    def do(it):
                        par, w = it.slot % 2, (it.slot % QT + 1) * P
                        act.wait_ge(*at(maxed, it, h + 1))
                        act.wait_ge(*at(turned, it, 2 * h + 2, 2))
                        act.wait_ge(*at(inverted, it, h + 1, 2))
                        act.activation(probs[:, par, h, 0:w], S[h][:, 0:w], ACT.Exp, bias=nmax[:, par, h:h + 1],
                                       accum_out=rsum[:, par, h:h + 1]).then_inc(exped, 1)
                    return do

                def take_pT(h):
                    def do(it):
                        i, par = it.slot % QT, it.slot % 2
                        chunks = range(0, i + 1, 4)
                        act.wait_ge(*at(attended, it, 1, 2))
                        for n, c in enumerate(chunks):
                            w = (min(c + 4, i + 1) - c) * P
                            act.wait_ge(*at(turned, it, 2 * h + (n + 1) * (2 // len(chunks))))
                            act.activation(pT[:, par, h, c * P:c * P + w], TR[(n + h) % 2][:, 0:w],
                                           ACT.Copy).then_inc(pT_in, 2 // len(chunks))
                    return do

                pipeline(act, b * UNITS, UNITS, U, [
                    (9, take_pT(0)), (8, exps(0)), (0, take_projection), (9, take_pT(1)), (8, exps(1))])

        @block.vector
        def _(dve):
            seed(dve, [masked, maxed, inverted, scaled, o_in])
            dve.sem_inc(out_in, 1)
            with dve.Fori(0, B, 1) as b:
                dve.wait_ge(out_in, b * TPB + 1)
                dve.sem_inc(held, 1)
                dve.tensor_copy(x_b[:], xn[:, bass.ds(b * TPB, TPB), :]).then_inc(x_copied, 1)

                def mask_and_max(h):
                    def do(it):
                        i, par = it.slot % QT, it.slot % 2
                        w = (i + 1) * P
                        dve.wait_ge(*at(scored, it, h + 1))
                        dve.tensor_tensor(S[h][:, w - P:w], S[h][:, w - P:w], causal[:], ALU.add).then_inc(masked, 1)
                        dve.wait_ge(*at(masked, it, h + 1))
                        dve.wait_ge(*at(exped, it, h + 1, 2))
                        dve.tensor_reduce(nmax[:, par, h:h + 1], S[h][:, 0:w], AX.X, ALU.max, negate=True).then_inc(maxed, 1)
                    return do

                def scale(h):
                    def do(it):
                        par, w = it.slot % 2, (it.slot % QT + 1) * P
                        dve.wait_ge(*at(exped, it, h + 1))
                        dve.reciprocal(rinv[:, par, h:h + 1], rsum[:, par, h:h + 1]).then_inc(inverted, 1)
                        dve.wait_ge(*at(inverted, it, h + 1))
                        p = probs[:, par, h, 0:w]
                        dve.tensor_scalar(p, p, rinv[:, par, h:h + 1], None, ALU.mult).then_inc(scaled, 1)
                    return do

                def take_o(it):
                    i = it.slot % QT
                    dve.wait_ge(*at(attended, it, 1))
                    dve.sem_inc(held, 1)
                    pair = it.turn * 2 + it.slot // QT
                    dve.tensor_copy(oT[:, bass.ds(pair, 1), i * P:(i + 1) * P], OB[:, 0:P].unsqueeze(1)).then_inc(o_in, 1)

                pipeline(dve, b * UNITS, UNITS, U, [
                    (8, mask_and_max(0)), (10, take_o), (8, mask_and_max(1)), (8, scale(0)), (8, scale(1))])
                for i in range(TPB):
                    dve.wait_ge(out_done, b * TPB + i + 1)
                    dve.sem_inc(held, 1)
                    dve.tensor_copy(z[:, bass.ds(b * TPB + i, 1), :], [OB, PB][i % 2][:, 0:C].unsqueeze(1)).then_inc(out_in, 1)
            dve.wait_ge(out_in, B * TPB + 1)


def routed_block(nc, A, xn, z, ident, psum, scratch):
    H, D, F = 16, 8, 512
    S = 512
    KEPT = 127
    MAGIC = 12582912.0
    INV_2PI = 0.15915494309189535
    C1, C2, C3 = 6.28125, 1.93500518798828125e-3, 3.0199159819e-7
    PI = 3.14159250259399414
    HALF_PI = 1.57079632679489662
    with ExitStack() as ctx:
        def sb(name, shape, dt=F32):
            return ctx.enter_context(nc.sbuf_tensor("m_" + name, shape, dt))

        def sem(name):
            return ctx.enter_context(nc.semaphore("m_" + name))

        XC = P + 2
        router = sb("router", [P, C])
        router_b = sb("router_b", [P, 1])
        products = sb("products", [P, NT, C])
        weights = sb("weights", [P, NT])
        weights_t = sb("weights_t", [NT, P])
        w_row = sb("w_row", [P, 2, T])
        from_here = sb("from_here", [P, 2 * T - P])
        junk = sb("junk", [P, 2, T])
        slots_sign = sb("slots_sign", [P, 2])
        at_least, ties, rank = sb("at_least", [P, NT]), sb("ties", [P, NT]), sb("rank", [P, NT])
        unselected = sb("unselected", [P, NT])
        slots = sb("slots", [P, P])
        pos_i = sb("pos_i", [P, B, TPB], I32)
        x_b = sb("x_b", [P, TPB, XC])
        one_hot = sb("one_hot", [P, TPB, P])
        one_hot_T = sb("one_hot_T", [P, TPB, P])
        last_row = sb("last_row", [P, 2, P])
        clamped = sb("clamped", [P, P])
        mask = sb("mask", [P, S // P, S])
        mask_rows = sb("mask_rows", [P, S // P, P])
        spare = sb("spare", [P, P])
        mask_sel = sb("mask_sel", [P, P])
        w_qkv, w_o, w_1, w_2 = sb("w_qkv", [P, 3 * P]), sb("w_o", [P, P]), sb("w_1", [P, F]), sb("w_2", [P, 4, P])
        ln = sb("ln", [P, 2, C])
        head_cols = sb("head_cols", [P, H])
        inv_freq = sb("inv_freq", [P, 4])
        minus_half = sb("minus_half", [P, 1])
        x_sel = sb("x_sel", [P, XC])
        sq = sb("sq", [P, C])
        ssum = sb("ssum", [P, 1])
        rms = sb("rms", [P, 1])
        hn = sb("hn", [P, C])
        hT = sb("hT", [P, P])
        ang, turns = sb("ang", [P, 4]), sb("turns", [P, 4])
        sincos_in, over, sincos = sb("sincos_in", [P, 2, 4]), sb("over", [P, 2, 4]), sb("sincos", [P, 2, 4])
        sin2 = sb("sin2", [P, 2, 4])
        qk_a, qk_b = sb("qk_a", [P, 2 * P]), sb("qk_b", [P, 2 * P])
        v = sb("v", [P, P])
        qT = sb("qT", [P, P])
        k_heads = sb("k_heads", [P, H, P])
        s = sb("s", [P, H, P])
        mx, sm = sb("mx", [P, H]), sb("sm", [P, H])
        pT = sb("pT", [P, H, P])
        o = sb("o", [P, P])
        oT = sb("oT", [P, P])
        x1, x2 = sb("x1", [P, C]), sb("x2", [P, C])
        hid = sb("hid", [P, 4, P])

        def bank(n, m=1):
            return psum[:, n:n + m, :].rearrange("p a n -> p (a n)")

        loaded, held, mask_in, stored = sem("loaded"), sem("held"), sem("mask_in"), sem("stored")
        row_in = [sem("even_row_in"), sem("odd_row_in")]
        batch_kept = sem("batch_kept")
        prepared, turned_w, copied_w, rank_step, batch_done = (
            sem("prepared"), sem("turned_w"), sem("copied_w"), sem("rank_step"), sem("batch_done"))

        class Steps:

            def __init__(self, name, names):
                self.sem, self.names, self.given = sem(name), names.split(), 0

            def done(self, ins, name):
                assert self.names[self.given % len(self.names)] == name, name
                self.given += 1
                ins.then_inc(self.sem, 1)

            def reached(self, b, name):
                return self.sem, b * len(self.names) + self.names.index(name) + 1

        pe_steps = Steps("pe_steps", """gathered one_hot_turned clamped_row mask_rows mask_selected normed_turned qkv
            qk_turned scores probs_turned attended o_turned projected normed2_turned hidden mlp scattered""")
        act_steps = Steps("act_steps", """one_hot_T clamped mask_rows hT sin qT v exps pT oT hT2 gelu""")
        dve_steps = Steps("dve_steps", """one_hot x_in pos_in w_in x_sel sq ssum rms_in hn
            ang turns turns2 turns3 r1 r2 r3 r4 r5 over wrapped clamp sin2 mask_sel qk_b qk_a qk k_heads
            s mx shifted sm rsm o x1 sq2 ssum2 rms_in2 hn2 x2 x2w""")
        pool_steps = Steps("pool_steps", "rms rms2")

        block = ctx.enter_context(nc.Block())

        @block.sync
        def _(sp):
            sp.dma_start(router[:], A["router_w"].rearrange("c o -> (o c)").partition_broadcast(P)).then_inc(loaded, 16)
            sp.dma_start(router_b[:], A["router_b"].partition_broadcast(P)).then_inc(loaded, 16)
            sp.dma_start(from_here[:], A["from_here"]).then_inc(loaded, 16)
            sp.dma_start(slots[:], A["slots"]).then_inc(loaded, 16)
            sp.dma_start(last_row[:], A["last_row"]).then_inc(loaded, 16)
            sp.dma_start(spare[:], A["spare"]).then_inc(loaded, 16)
            sp.dma_start(slots_sign[:], A["halves_sign"]).then_inc(loaded, 16)
            sp.dma_start(head_cols[:], A["head_cols"]).then_inc(loaded, 16)
            sp.dma_start(inv_freq[:], A["inv_freq"]).then_inc(loaded, 16)
            for n in range(3):
                sp.dma_start(w_qkv[:, n * P:(n + 1) * P], A[["wq", "wk", "wv"][n]]).then_inc(loaded, 16)
            sp.dma_start(w_o[:], A["wo"]).then_inc(loaded, 16)
            sp.dma_start(w_1[:], A["w1"]).then_inc(loaded, 16)
            sp.dma_start(w_2[:], A["w2"].rearrange("(h p) c -> p h c", p=P)).then_inc(loaded, 16)
            sp.dma_start(ln[:, 0, :], A["ln1"].partition_broadcast(P)).then_inc(loaded, 16)
            sp.dma_start(ln[:, 1, :], A["ln2"].partition_broadcast(P)).then_inc(loaded, 16)
            sp.dma_start(pos_i[:], A["pos"]).then_inc(loaded, 16)
            sp.wait_ge(copied_w, 1)
            sp.dma_start(scratch, weights_t[:]).then_inc(stored, 16)
            sp.wait_ge(stored, 16)
            rows = scratch.rearrange("(b t) p -> b (t p)", b=B)
            for b in range(B):
                if b >= 2:
                    sp.wait_ge(rank_step, (b - 1) * 2 * TPB)
                sp.dma_start(w_row[:, b % 2, :], rows[b].partition_broadcast(P)).then_inc(row_in[b % 2], 16)
            with sp.Fori(0, B, 1) as b:
                sp.wait_ge(batch_done, b + 1)
                sp.dma_start(mask[:], A["attention_mask"][bass.ds(b, 1)].rearrange("b o (t p) k -> p (b o t) k", p=P)
                             ).then_inc(mask_in, 16)

        LOADED = 16 * 18

        @block.gpsimd
        def _(pool):
            pool.wait_ge(prepared, 2)
            with pool.Fori(0, B, 1) as b:
                pool.wait_ge(*dve_steps.reached(b, "rms_in"))
                pool_steps.done(pool.tensor_tensor(rms[:], ssum[:], minus_half[:], ALU.pow), "rms")
                pool.wait_ge(*dve_steps.reached(b, "rms_in2"))
                pool_steps.done(pool.tensor_tensor(rms[:], ssum[:], minus_half[:], ALU.pow), "rms2")

        @block.tensor
        def _(pe):
            pe.wait_ge(loaded, LOADED)
            pe.wait_ge(prepared, 5)
            pe.transpose(bank(0)[0:NT, 0:P], weights[:], ident[:]).then_inc(turned_w, 1)
            with pe.Fori(0, B, 1) as b:
                def after(steps, name):
                    pe.wait_ge(*steps.reached(b, name))

                after(dve_steps, "w_in")
                for t in range(TPB):
                    m = pe.matmul(bank(0)[:, 0:XC], one_hot[:, t, :], x_b[:, t, :], start=(t == 0), stop=(t == TPB - 1))
                pe_steps.done(m, "gathered")
                for t in range(TPB):
                    m = pe.transpose(bank(1 + t // 4)[:, (t % 4) * P:(t % 4 + 1) * P], one_hot[:, t, :], ident[:])
                pe_steps.done(m, "one_hot_turned")
                for t in range(3, TPB):
                    m = pe.matmul(bank(3)[:, 0:P], last_row[:, min(t - 3, 1), :], one_hot[:, t, :],
                                  start=(t == 3), stop=(t == TPB - 1))
                pe_steps.done(m, "clamped_row")
                pe.wait_ge(mask_in, b * 16 + 16)
                after(act_steps, "clamped")
                for k in range(4):
                    for t in range(4):
                        m = pe.matmul(bank(4)[:, k * P:(k + 1) * P], mask[:, t, k * P:(k + 1) * P],
                                      one_hot[:, t, :] if t < 3 else clamped[:], start=(t == 0), stop=(t == 3))
                pe_steps.done(m, "mask_rows")
                after(act_steps, "mask_rows")
                for k in range(4):
                    m = pe.matmul(bank(5)[:, 0:P], mask_rows[:, k, :], one_hot[:, k, :] if k < 3 else clamped[:],
                                  start=(k == 0), stop=(k == 3))
                pe_steps.done(m, "mask_selected")
                after(dve_steps, "hn")
                pe_steps.done(pe.transpose(bank(0)[:, 0:P], hn[:], ident[:]), "normed_turned")
                after(act_steps, "hT")
                pe_steps.done(pe.matmul(bank(1)[:, 0:3 * P], hT[:], w_qkv[:], start=True, stop=True), "qkv")
                after(dve_steps, "qk")
                pe.transpose(bank(2)[:, 0:P], qk_a[:, 0:P], ident[:])
                pe_steps.done(pe.transpose(bank(3)[:, 0:P], qk_a[:, P:2 * P], ident[:]), "qk_turned")
                after(dve_steps, "k_heads")
                after(act_steps, "qT")
                for g in range(4):
                    m = pe.matmul(bank(4 + g), qT[:], k_heads[:, 4 * g:4 * g + 4, :].rearrange("p h k -> p (h k)"),
                                  start=True, stop=True)
                pe_steps.done(m, "scores")
                after(act_steps, "exps")
                after(act_steps, "v")
                for h in range(H):
                    m = pe.transpose(bank(h // 4)[:, (h % 4) * P:(h % 4 + 1) * P], s[:, h, :], ident[:])
                pe_steps.done(m, "probs_turned")
                after(act_steps, "pT")
                for h in range(H):
                    m = pe.matmul(bank(4)[:, D * h:D * h + D], pT[:, h, :], v[:, D * h:D * h + D], start=True, stop=True)
                pe_steps.done(m, "attended")
                after(dve_steps, "o")
                pe_steps.done(pe.transpose(bank(5)[:, 0:P], o[:], ident[:]), "o_turned")
                after(act_steps, "oT")
                pe_steps.done(pe.matmul(bank(6)[:, 0:C], oT[:], w_o[:], start=True, stop=True), "projected")
                after(dve_steps, "hn2")
                pe_steps.done(pe.transpose(bank(0)[:, 0:P], hn[:], ident[:]), "normed2_turned")
                after(act_steps, "hT2")
                for f in range(4):
                    m = pe.matmul(bank(1)[:, f * P:(f + 1) * P], w_1[:, f * P:(f + 1) * P], hT[:], start=True, stop=True)
                pe_steps.done(m, "hidden")
                after(act_steps, "gelu")
                for f in range(4):
                    m = pe.matmul(bank(2)[:, 0:C], hid[:, f, :], w_2[:, f, :], start=(f == 0), stop=(f == 3))
                pe_steps.done(m, "mlp")
                after(dve_steps, "x2w")
                for t in range(TPB):
                    m = pe.matmul(bank(3 + t // 4)[:, (t % 4) * P:(t % 4 + 1) * P], one_hot_T[:, t, :], x2[:],
                                  start=True, stop=True)
                pe_steps.done(m, "scattered")

        @block.scalar
        def _(act):
            act.wait_ge(turned_w, 1)
            act.activation(weights_t[:], bank(0)[0:NT, 0:P], ACT.Copy).then_inc(copied_w, 1)
            act.wait_ge(loaded, LOADED)
            with act.Fori(0, B, 1) as b:
                def after(steps, name):
                    act.wait_ge(*steps.reached(b, name))

                act.wait_ge(batch_done, b + 1)
                after(pe_steps, "one_hot_turned")
                act_steps.done(act.activation(one_hot_T[:].rearrange("p t n -> p (t n)"), bank(1, 2), ACT.Copy), "one_hot_T")
                after(pe_steps, "clamped_row")
                act_steps.done(act.activation(clamped[:], bank(3)[:, 0:P], ACT.Copy), "clamped")
                after(pe_steps, "mask_rows")
                act_steps.done(act.activation(mask_rows[:].rearrange("p t n -> p (t n)"), bank(4), ACT.Copy), "mask_rows")
                after(pe_steps, "normed_turned")
                act_steps.done(act.activation(hT[:], bank(0)[:, 0:P], ACT.Copy), "hT")
                after(dve_steps, "clamp")
                act_steps.done(act.activation(sincos[:], sincos_in[:], ACT.Sin), "sin")
                after(pe_steps, "qk_turned")
                act_steps.done(act.activation(qT[:], bank(2)[:, 0:P], ACT.Copy, scale=float(D) ** -0.5), "qT")
                after(dve_steps, "qk")
                act_steps.done(act.activation(v[:], bank(1)[:, 2 * P:3 * P], ACT.Copy), "v")
                after(dve_steps, "shifted")
                act_steps.done(act.activation(s[:], s[:], ACT.Exp), "exps")
                after(pe_steps, "probs_turned")
                act_steps.done(act.activation(pT[:].rearrange("p h n -> p (h n)"), bank(0, 4), ACT.Copy), "pT")
                after(pe_steps, "o_turned")
                act_steps.done(act.activation(oT[:], bank(5)[:, 0:P], ACT.Copy), "oT")
                after(pe_steps, "normed2_turned")
                act_steps.done(act.activation(hT[:], bank(0)[:, 0:P], ACT.Copy), "hT2")
                after(pe_steps, "hidden")
                act_steps.done(act.activation(hid[:].rearrange("p f n -> p (f n)"), bank(1), ACT.Gelu_apprx_tanh), "gelu")

        @block.vector
        def _(dve):
            dve.memset(minus_half[:], -0.5).then_inc(prepared, 1)
            dve.sem_inc(prepared, 1)
            dve.sem_inc(batch_done, 1)
            dve.wait_ge(loaded, LOADED)
            dve.tensor_tensor(products[:], xn[:], router[:].unsqueeze(1).to_broadcast([P, NT, C]), ALU.mult).then_inc(prepared, 1)
            dve.wait_ge(prepared, 3)
            dve.tensor_reduce(weights[:], products[:], AX.X, ALU.add).then_inc(prepared, 1)
            dve.wait_ge(prepared, 4)
            dve.tensor_scalar(weights[:], weights[:], router_b[:], None, ALU.add).then_inc(prepared, 1)
            dve.wait_ge(prepared, 5)
            for b in range(B):
                dve.wait_ge(row_in[b % 2], 16 * (b // 2 + 1))
                for t in range(TPB):
                    n = b * TPB + t
                    if n:
                        dve.wait_ge(rank_step, 2 * n)
                    w = weights[:, n:n + 1]
                    dve.tensor_scalar(junk[:, 0, :], w_row[:, b % 2, :], w, None, ALU.is_ge, ALU.add,
                                      accum_out=at_least[:, n:n + 1]).then_inc(rank_step, 1)
                    off = T - P - t * P
                    dve.scalar_tensor_tensor(out=junk[:, 1, :], in0=w_row[:, b % 2, :], scalar=w,
                                             in1=from_here[:, off:off + T], op0=ALU.is_equal, op1=ALU.mult,
                                             accum_out=ties[:, n:n + 1]).then_inc(rank_step, 1)
            dve.wait_ge(rank_step, 2 * NT)
            dve.tensor_tensor(rank[:], at_least[:], ties[:], ALU.subtract).then_inc(prepared, 1)
            dve.tensor_scalar(unselected[:], at_least[:], float(KEPT) + 0.5, None, ALU.is_gt).then_inc(prepared, 1)
            dve.wait_ge(prepared, 7)
            with dve.Fori(0, B, 1) as b:
                tiles = bass.ds(b * TPB, TPB)

                def after(steps, name):
                    dve.wait_ge(*steps.reached(b, name))

                def step(name, ins):
                    dve_steps.done(ins, name)

                def then(name, ins):
                    dve_steps.done(ins, name)
                    after(dve_steps, name)

                dve.wait_ge(batch_done, b + 1)
                dve.sem_inc(held, 1)
                step("one_hot", dve.tensor_tensor(one_hot[:], slots[:].unsqueeze(1).to_broadcast([P, TPB, P]),
                                                  rank[:, tiles].unsqueeze(2).to_broadcast([P, TPB, P]), ALU.is_equal))
                step("x_in", dve.tensor_copy(x_b[:, :, 0:C], xn[:, tiles, :]))
                step("pos_in", dve.tensor_copy(x_b[:, :, C:C + 1], pos_i[:, bass.ds(b, 1), :].rearrange("p o (t a) -> p (o t) a", a=1)))
                step("w_in", dve.tensor_copy(x_b[:, :, C + 1:C + 2], weights[:, tiles].unsqueeze(2)))
                after(pe_steps, "gathered")
                then("x_sel", dve.tensor_copy(x_sel[:], bank(0)[:, 0:XC]))
                x = x_sel[:, 0:C]

                def rmsnorm(x, gain, n):
                    then("sq" + n, dve.tensor_tensor(sq[:], x, x, ALU.mult))
                    then("ssum" + n, dve.tensor_reduce(ssum[:], sq[:], AX.X, ALU.add))
                    step("rms_in" + n, dve.tensor_scalar(ssum[:], ssum[:], 1.0 / C, 1e-6, ALU.mult, ALU.add))
                    after(pool_steps, "rms" + n)
                    step("hn" + n, dve.scalar_tensor_tensor(out=hn[:], in0=x, scalar=rms[:], in1=gain, op0=ALU.mult, op1=ALU.mult))

                rmsnorm(x, ln[:, 0, :], "")
                r = sincos_in[:, 0, :]
                then("ang", dve.tensor_scalar(ang[:], inv_freq[:], x_sel[:, C:C + 1], None, ALU.mult))
                then("turns", dve.tensor_scalar(turns[:], ang[:], INV_2PI, None, ALU.mult))
                then("turns2", dve.tensor_scalar(turns[:], turns[:], MAGIC, None, ALU.add))
                then("turns3", dve.tensor_scalar(turns[:], turns[:], -MAGIC, None, ALU.add))
                then("r1", dve.scalar_tensor_tensor(out=r, in0=turns[:], scalar=-C1, in1=ang[:], op0=ALU.mult, op1=ALU.add))
                then("r2", dve.scalar_tensor_tensor(out=r, in0=turns[:], scalar=-C2, in1=r, op0=ALU.mult, op1=ALU.add))
                then("r3", dve.scalar_tensor_tensor(out=r, in0=turns[:], scalar=-C3, in1=r, op0=ALU.mult, op1=ALU.add))
                then("r4", dve.tensor_scalar(sincos_in[:, 1, :], r, HALF_PI, None, ALU.add))
                then("r5", dve.tensor_scalar(over[:], sincos_in[:], PI, None, ALU.is_gt))
                then("over", dve.scalar_tensor_tensor(out=sincos_in[:], in0=over[:], scalar=-C1, in1=sincos_in[:],
                                                      op0=ALU.mult, op1=ALU.add))
                then("wrapped", dve.scalar_tensor_tensor(out=sincos_in[:], in0=over[:], scalar=-(C2 + C3), in1=sincos_in[:],
                                                         op0=ALU.mult, op1=ALU.add))
                step("clamp", dve.tensor_scalar(sincos_in[:], sincos_in[:], -PI, PI, ALU.max, ALU.min))
                after(act_steps, "sin")
                then("sin2", dve.tensor_tensor(sin2[:], sincos[:, 0:1, :].to_broadcast([P, 2, 4]),
                                               slots_sign[:].unsqueeze(2).to_broadcast([P, 2, 4]), ALU.mult))
                after(pe_steps, "mask_selected")
                step("mask_sel", dve.tensor_tensor(mask_sel[:], bank(5)[:, 0:P], spare[:], ALU.add))
                after(pe_steps, "qkv")
                qkv = bank(1)[:, 0:2 * P].rearrange("p (h r d) -> p h r d", r=2, d=4)
                step("qk_b", dve.tensor_tensor(qk_b[:].rearrange("p (h r d) -> p h r d", r=2, d=4), qkv[:, :, ::-1, :],
                                               sin2[:].unsqueeze(1).to_broadcast([P, 2 * H, 2, 4]), ALU.mult))
                then("qk_a", dve.tensor_tensor(qk_a[:].rearrange("p (h r d) -> p h r d", r=2, d=4), qkv,
                                               sincos[:, 1:2, :].unsqueeze(1).to_broadcast([P, 2 * H, 2, 4]), ALU.mult))
                step("qk", dve.tensor_tensor(qk_a[:], qk_a[:], qk_b[:], ALU.add))
                after(pe_steps, "qk_turned")
                step("k_heads", dve.tensor_tensor(k_heads[:], bank(3)[:, 0:P].unsqueeze(1).to_broadcast([P, H, P]),
                                                  head_cols[:].unsqueeze(2).to_broadcast([P, H, P]), ALU.mult))
                after(pe_steps, "scores")
                then("s", dve.tensor_tensor(s[:], bank(4, 4).rearrange("p (h k) -> p h k", h=H),
                                            mask_sel[:].unsqueeze(1).to_broadcast([P, H, P]), ALU.add))
                then("mx", dve.tensor_reduce(mx[:], s[:], AX.X, ALU.max))
                step("shifted", dve.tensor_tensor(s[:], s[:], mx[:].unsqueeze(2).to_broadcast([P, H, P]), ALU.subtract))
                after(act_steps, "exps")
                then("sm", dve.tensor_reduce(sm[:], s[:], AX.X, ALU.add))
                then("rsm", dve.reciprocal(sm[:], sm[:]))
                after(pe_steps, "attended")
                step("o", dve.tensor_tensor(o[:].rearrange("p (h d) -> p h d", h=H),
                                            bank(4)[:, 0:P].rearrange("p (h d) -> p h d", h=H),
                                            sm[:].unsqueeze(2).to_broadcast([P, H, D]), ALU.mult))
                after(pe_steps, "projected")
                then("x1", dve.tensor_tensor(x1[:], bank(6)[:, 0:C], x, ALU.add))
                rmsnorm(x1[:], ln[:, 1, :], "2")
                after(pe_steps, "mlp")
                then("x2", dve.tensor_tensor(x2[:], bank(2)[:, 0:C], x1[:], ALU.add))
                step("x2w", dve.tensor_scalar(x2[:], x2[:], x_sel[:, C + 1:C + 2], None, ALU.mult))
                dve.wait_ge(*pe_steps.reached(b, "gathered"))
                dve.sem_inc(held, 1)
                dve.tensor_tensor(z[:, tiles, :], x_b[:, :, 0:C],
                                  unselected[:, tiles].unsqueeze(2).to_broadcast([P, TPB, C]), ALU.mult).then_inc(batch_kept, 1)
                dve.wait_ge(batch_kept, b + 1)
                after(pe_steps, "scattered")
                dve.tensor_tensor(z[:, tiles, :], z[:, tiles, :], bank(3, 2).rearrange("p (t c) -> p t c", c=C),
                                  ALU.add).then_inc(batch_done, 1)


def linear_attention(nc, A, xn, z, ident, psum):
    H, D, U = 16, 8, TPB
    NORM = float(D) ** -0.25
    FEAT_EPS, DEN_EPS = 1e-6, 1e-6
    with ExitStack() as ctx:
        def sb(name, shape):
            return ctx.enter_context(nc.sbuf_tensor("l_" + name, shape, F32))

        def sem(name):
            return ctx.enter_context(nc.semaphore("l_" + name))

        wT = sb("wT", [P, 4, P])
        feat = sb("feat", [P, P])
        head_cols = sb("head_cols", [P, H])
        block_mask = sb("block_mask", [P, P])
        bias_cols = sb("bias_cols", [P, 2])
        bias_rows = sb("bias_rows", [P, 2, P])
        bias_norm = sb("bias_norm", [P, 2])
        x_in = sb("x_in", [P, 2, C])
        xT = sb("xT", [P, 2, P])
        q_s, k_s = sb("q_s", [P, 2, P]), sb("k_s", [P, 2, P])
        v_s = sb("v_s", [P, 2, P + 1])
        q_feat = sb("q_feat", [P, U, P])
        k_feat = sb("k_feat", [P, 2, P])
        kv = sb("kv", [P, P + H])
        ksum = sb("ksum", [P, 1])
        den = sb("den", [P, H])
        rden = sb("rden", [P, H])
        o_s = sb("o_s", [P, 2, P])
        oT = sb("oT", [P, 2, P])

        XB, QB, KB, VB, FBK, KVB, NB, OB = [psum[:, n, :] for n in range(8)]

        loaded, held, ready = sem("loaded"), sem("held"), sem("ready")
        x_turned, qkv_done, feat_done, kv_done, num_done, out_done = (
            sem("x_turned"), sem("qkv_done"), sem("feat_done"), sem("kv_done"), sem("num_done"), sem("out_done"))
        act_a, act_b = sem("act_a"), sem("act_b")
        z_in = sem("z_in")
        v_in, feat_in, dve_kv, dve_b = sem("v_in"), sem("feat_in"), sem("dve_kv"), sem("dve_b")
        staged = sem("staged")
        PER = {x_turned: 1, qkv_done: 3, feat_done: 2, kv_done: 1, num_done: 1, out_done: 2, act_a: 3, act_b: 1, v_in: 1, feat_in: 2, dve_b: 3, z_in: 1, staged: 1}

        def at(s, it, k, back=0):
            return s, reached(it, PER[s], k, back, 2 * SEED)

        def seed(eng, sems):
            for s in sems:
                eng.sem_inc(s, PER[s] * 2 * SEED)

        block = ctx.enter_context(nc.Block())

        @block.sync
        def _(sp):
            sp.dma_start(wT[:], A["la_wT"]).then_inc(loaded, 16)
            sp.dma_start(bias_cols[:], A["la_bias_cols"]).then_inc(loaded, 16)
            sp.dma_start(bias_rows[:], A["la_bias_rows"].partition_broadcast(P)).then_inc(loaded, 16)
            sp.dma_start(head_cols[:], A["head_cols"]).then_inc(loaded, 16)
            sp.dma_start(block_mask[:], A["head_blocks"]).then_inc(loaded, 16)
            sp.wait_ge(ready, 1)
            for h in range(H):
                sp.dma_start(feat[D * h:D * h + D, D * h:D * h + D], A["la_PT"]).then_inc(loaded, 16)

        @block.gpsimd
        def _(pool):
            seed(pool, [staged])

            def stage(it):
                pool.wait_ge(*at(x_turned, it, 1, 2))
                pool.sem_inc(held, 1)
                pool.tensor_copy(x_in[:, it.slot % 2, :].unsqueeze(1), xn[:, bass.ds(it.t, 1), :]).then_inc(staged, 1)
            pipeline(pool, 0, NT, U, [(0, stage)])

        @block.tensor
        def _(pe):
            seed(pe, [x_turned, qkv_done, feat_done, kv_done, num_done, out_done])
            pe.wait_ge(loaded, 80 + 16 * H)
            pe.wait_ge(ready, 4)

            def turn_x(it):
                u = it.slot % 2
                pe.wait_ge(*at(staged, it, 1))
                pe.wait_ge(*at(act_a, it, 1, 1))
                pe.transpose(XB[:, 0:P], x_in[:, u, :], ident[:]).then_inc(x_turned, 1)

            def qkv(it):
                u = it.slot % 2
                pe.wait_ge(*at(act_a, it, 1))
                pe.wait_ge(*at(act_a, it, 3, 1))
                pe.wait_ge(*at(v_in, it, 1, 1))
                pe.matmul(QB[:, 0:P], wT[:, 0, :], xT[:, u, :], start=True, stop=True).then_inc(qkv_done, 1)
                pe.matmul(KB[:, 0:P], wT[:, 1, :], xT[:, u, :], start=True, stop=True).then_inc(qkv_done, 1)
                pe.matmul(VB[:, 0:P], xT[:, u, :], wT[:, 2, :], start=True, stop=True).then_inc(qkv_done, 1)

            def features(it):
                u = it.slot % 2
                pe.wait_ge(*at(feat_in, it, 2, 1))
                pe.wait_ge(*at(act_a, it, 3))
                pe.matmul(FBK[:, 0:P], feat[:], q_s[:, u, :], start=True, stop=True).then_inc(feat_done, 1)
                pe.matmul(FBK[:, P:2 * P], k_s[:, u, :], feat[:], start=True, stop=True).then_inc(feat_done, 1)

            def sum_kv(it):
                u = it.slot % 2
                pe.wait_ge(*at(feat_in, it, 2))
                if it.slot == 0:
                    pe.wait_ge(dve_kv, (it.turn + 1) * 3)
                pe.matmul(KVB[:, 0:P + 1], k_feat[:, u, :], v_s[:, u, :], start=(it.slot == 0),
                          stop=(it.slot == U - 1)).then_inc(kv_done, 1)

            def numerators(it):
                if it.slot == 0:
                    pe.wait_ge(dve_kv, (it.turn + 2) * 3)
                pe.wait_ge(*at(dve_b, it, 3, 1))
                pe.matmul(NB[:, 0:P + H], q_feat[:, it.slot, :], kv[:], start=True, stop=True).then_inc(num_done, 1)

            def turn_o(it):
                u = it.slot % 2
                pe.wait_ge(*at(dve_b, it, 3))
                pe.wait_ge(*at(z_in, it, 1, 1))
                pe.transpose(OB[:, 0:P], o_s[:, u, :], ident[:]).then_inc(out_done, 1)

            def project(it):
                pe.wait_ge(*at(act_b, it, 1))
                pe.matmul(OB[:, 0:P], oT[:, it.slot % 2, :], wT[:, 3, :], start=True, stop=True).then_inc(out_done, 1)

            pipeline(pe, 0, NT, U, [(9, numerators), (0, turn_x), (10, turn_o), (1, features), (0, qkv),
                                    (1, sum_kv), (10, project)])

        @block.scalar
        def _(act):
            seed(act, [act_a, act_b])
            act.wait_ge(loaded, 80 + 16 * H)
            act.activation(bias_norm[:], bias_cols[:], ACT.Copy, scale=NORM).then_inc(ready, 1)
            act.wait_ge(ready, 4)

            def take_x(it):
                act.wait_ge(*at(x_turned, it, 1))
                act.wait_ge(*at(qkv_done, it, 3, 2))
                act.activation(xT[:, it.slot % 2, :], XB[:, 0:P], ACT.Copy).then_inc(act_a, 1)

            def take_qk(it):
                u = it.slot % 2
                act.wait_ge(*at(feat_done, it, 2, 2))
                act.wait_ge(*at(qkv_done, it, 1))
                act.activation(q_s[:, u, :], QB[:, 0:P], ACT.Identity, scale=NORM, bias=bias_norm[:, 0:1]).then_inc(act_a, 1)
                act.wait_ge(*at(qkv_done, it, 2))
                act.activation(k_s[:, u, :], KB[:, 0:P], ACT.Identity, scale=NORM, bias=bias_norm[:, 1:2]).then_inc(act_a, 1)

            def take_o(it):
                act.wait_ge(*at(out_done, it, 1))
                act.wait_ge(*at(out_done, it, 2, 2))
                act.activation(oT[:, it.slot % 2, :], OB[:, 0:P], ACT.Copy).then_inc(act_b, 1)

            pipeline(act, 0, NT, U, [(0, take_x), (10, take_o), (0, take_qk)])

        @block.vector
        def _(dve):
            seed(dve, [v_in, feat_in, dve_b, z_in])
            dve.memset(feat[:], 0.0).then_inc(ready, 1)
            dve.memset(v_s[:], 1.0).then_inc(ready, 1)
            dve.sem_inc(dve_kv, 3)
            dve.wait_ge(loaded, 80 + 16 * H)
            dve.sem_inc(ready, 1)

            def take_v(it):
                u = it.slot % 2
                dve.wait_ge(*at(qkv_done, it, 3))
                dve.wait_ge(*at(kv_done, it, 1, 2))
                dve.tensor_tensor(v_s[:, u, 0:P], VB[:, 0:P], bias_rows[:, 0, :], ALU.add).then_inc(v_in, 1)

            def take_features(it):
                u = it.slot % 2
                dve.wait_ge(*at(feat_done, it, 2))
                dve.wait_ge(*at(num_done, it, 1, 8))
                dve.tensor_scalar(q_feat[:, it.slot, :], FBK[:, 0:P], 0.0, FEAT_EPS, ALU.max, ALU.add).then_inc(feat_in, 1)
                dve.wait_ge(*at(kv_done, it, 1, 2))
                dve.tensor_scalar(k_feat[:, u, :], FBK[:, P:2 * P], 0.0, FEAT_EPS, ALU.max, ALU.add).then_inc(feat_in, 1)
                if it.slot == U - 1:
                    dve.wait_ge(*at(kv_done, it, 1))
                    dve.wait_ge(*at(num_done, it, 1, 8))
                    dve.tensor_copy(ksum[:], KVB[:, P:P + 1]).then_inc(dve_kv, 1)
                    dve.tensor_tensor(kv[:, 0:P], KVB[:, 0:P], block_mask[:],
                                      ALU.mult).then_inc(dve_kv, 1)
                    dve.wait_ge(dve_kv, it.turn * 3 + 5)
                    dve.tensor_scalar(kv[:, P:P + H], head_cols[:], ksum[:], None, ALU.mult).then_inc(dve_kv, 1)

            def divide(it):
                u = it.slot % 2
                dve.wait_ge(*at(num_done, it, 1))
                dve.tensor_scalar(den[:], NB[:, P:P + H], DEN_EPS, None, ALU.add).then_inc(dve_b, 1)
                dve.wait_ge(*at(dve_b, it, 1))
                dve.reciprocal(rden[:], den[:]).then_inc(dve_b, 1)
                dve.wait_ge(*at(dve_b, it, 2))
                dve.wait_ge(*at(out_done, it, 1, 2))
                dve.tensor_tensor(o_s[:, u, :].rearrange("p (h d) -> p h d", h=H),
                                  NB[:, 0:P].rearrange("p (h d) -> p h d", h=H),
                                  rden[:].unsqueeze(2).to_broadcast([P, H, D]), ALU.mult).then_inc(dve_b, 1)

            def take_z(it):
                dve.wait_ge(*at(out_done, it, 2))
                dve.tensor_tensor(z[:, bass.ds(it.t, 1), :].rearrange("p o c -> p (o c)"), OB[:, 0:P],
                                  bias_rows[:, 1, :], ALU.add).then_inc(z_in, 1)

            pipeline(dve, 0, NT, U, [(9, divide), (1, take_features), (0, take_v), (10, take_z)])
            dve.wait_ge(*at(z_in, Item(NT), 0))


DEPTH, HEADS, HD, WIN = 6, 16, 64, 32
INNER = HEADS * HD
QKV = 3 * INNER
FF = 341
FCH = [(0, 128), (128, 128), (256, FF - 256)]
QK_SCALE = 8.0
RSQRT_SEED = float(0x5F3759DF - (1 << 22) - (1 << 31))


def local_transformer(nc, A, Y, ident, psum):
    U = 4
    with ExitStack() as ctx:
        def sb(name, shape, dt=F32):
            return ctx.enter_context(nc.sbuf_tensor(name, shape, dt))

        def sem(name):
            return ctx.enter_context(nc.semaphore(name))

        w_qkv = sb("w_qkv", [P, QKV])
        w_out = sb("w_out", [P, 8, C])
        w_up = sb("w_up", [P, 2 * FF])
        w_down = sb("w_down", [P, 3, C])
        cols = sb("cols", [P, 8])
        rows = sb("rows", [P, 3 * P])
        rope_base = sb("rope_base", [P, TPB, 4, HD])
        rope = sb("rope", [P, TPB, 4, HD])
        mask = sb("mask", [P, TPB, 2 * WIN])
        keep_carry = sb("keep_carry", [P, TPB])
        minus_half = sb("minus_half", [P, 1])
        y_in = sb("y_in", [P, U, C])
        shifted = sb("shifted", [P, U, P + 1])
        squares = sb("squares", [P, 2, 512])
        rotated = sb("rotated", [P, 2, 512])
        qk = sb("qk", [P, 2, 4, 512])
        ss = sb("ss", [P, 2, 32])
        rs_a = sb("rs_a", [P, 32])
        rs_b = sb("rs_b", [P, 32])
        rs_y = sb("rs_y", [P, 2, 32])
        qT = sb("qT", [P, 2, 8, P])
        kT = sb("kT", [P, 2, 8, WIN + P])
        V = sb("V", [P, U, INNER])
        sc = sb("sc", [P, 2, 2, 512])
        mx = sb("mx", [P, 2, HEADS])
        sm = sb("sm", [P, 2, HEADS])
        rsum = sb("rsum", [P, 2, HEADS])
        pT = sb("pT", [P, 2, HEADS, P])
        pT_prev = sb("pT_prev", [P, 2, HEADS, WIN])
        oT = sb("oT", [P, 2, 8, P])
        y1 = sb("y1", [P, U, C])
        y1b = sb("y1b", [P, 2, C])
        f_shift = sb("f_shift", [P, U, P + 1])
        stats = sb("stats", [P, 6])
        mv = sb("mv", [P, 2])
        rstd = sb("rstd", [P, 1])
        veps = sb("veps", [P, 1])
        xn = sb("xn", [P, C])
        xg = sb("xg", [P, P])
        gate = sb("gate", [P, 3, P])
        hid = sb("hid", [P, 3, P])

        ATT = [psum[:, 0, :], psum[:, 1, :]]
        TR = psum[:, 2:4, :]
        SC = [psum[:, 4, :], psum[:, 5, :]]
        OB = psum[:, 6, :]
        FB = psum[:, 7, :]

        consts = sem("consts")
        zeroed = sem("zeroed")
        held = sem("held")
        w_in = sem("w_in")
        small_in = sem("small_in")
        tables = sem("tables")
        x_turned, projected, qk_turned, scored = sem("x_turned"), sem("projected"), sem("qk_turned"), sem("scored")
        p_turned, attended, out_projected, ffn_pe = sem("p_turned"), sem("attended"), sem("out_projected"), sem("ffn_pe")
        shifted_in, squared, v_in, qk_in = sem("shifted_in"), sem("squared"), sem("v_in"), sem("qk_in")
        k_prev, exped, p_spread_a, o_in, ffn_act = sem("k_prev"), sem("exped"), sem("p_spread_a"), sem("o_in"), sem("ffn_act")
        roped, ss_done, rs_step, masked, maxed = sem("roped"), sem("ss_done"), sem("rs_step"), sem("masked"), sem("maxed")
        summed, inverted, p_spread_d, y1_done, ffn_dve, y_done = (
            sem("summed"), sem("inverted"), sem("p_spread_d"), sem("y1_done"), sem("ffn_dve"), sem("y_done"))
        staged, rope_added, qk_normed, shifted_max, p_scaled, ffn_pool = (
            sem("staged"), sem("rope_added"), sem("qk_normed"), sem("shifted_max"), sem("p_scaled"), sem("ffn_pool"))
        PER = {x_turned: 1, projected: 6, qk_turned: 4, scored: 2, p_turned: 1, attended: 2, out_projected: 1,
               ffn_pe: 6, shifted_in: 3, squared: 4, v_in: 2, qk_in: 4, k_prev: 1, exped: 2, p_spread_a: 6,
               o_in: 2, ffn_act: 7, roped: 8, ss_done: 4, rs_step: 12, masked: 2, maxed: 2, summed: 2,
               inverted: 2, p_spread_d: 6, y1_done: 1, ffn_dve: 7, y_done: 1, staged: 1, rope_added: 4,
               qk_normed: 4, shifted_max: 2, p_scaled: 2, ffn_pool: 2}

        def seed(eng, sems):
            for s in sems:
                eng.sem_inc(s, PER[s] * SEED)

        def at(s, it, k, back=0):
            return s, reached(it, PER[s], k, back)

        def spread(copy, it, sub, s):
            b = it.slot % 2
            src = TR.rearrange("p c (a q) -> p c a q", a=4)
            dst = pT[:, b].rearrange("p (a s c) q -> p s c a q", s=2, c=2)
            prv = pT_prev[:, b].rearrange("p (a s c) q -> p s c a q", s=2, c=2)
            o = 64 * sub
            for d0, d1, s0, s1, j in [(0, 64, 0, 64, 1), (64, 128, 0, 64, 3), (32, 64, 0, 32, 2), (64, 96, 32, 64, 2),
                                      (0, 32, 32, 64, 0)]:
                q = slice(32 * j, 32 * j + 32)
                args = [ACT.Copy] if s is p_spread_a else []
                copy(dst[d0:d1, sub, :, :, q], src[o + s0:o + s1, :, :, q], *args).then_inc(s, 1)
            copy(prv[96:128, sub, :, :, :], src[o:o + 32, :, :, 0:32], *args).then_inc(s, 1)

        block = ctx.enter_context(nc.Block())

        @block.sync
        def _(sp):
            sp.dma_start(rope_base[:], A["rope_base"]).then_inc(consts, 16)
            sp.dma_start(mask[:], A["win_mask"]).then_inc(consts, 16)
            sp.dma_start(keep_carry[:], A["keep_carry"]).then_inc(consts, 16)
            with sp.Fori(0, DEPTH, 1) as l:
                done = Item(l * NT)
                sp.wait_ge(*at(projected, done, 0))
                sp.dma_start(w_qkv[:], A["Wqkv"][l]).then_inc(w_in, 16)
                sp.wait_ge(*at(y_done, done, 0))
                sp.dma_start(cols[:], A["cols"][l]).then_inc(small_in, 16)
                sp.dma_start(rows[:], A["rows"][l].partition_broadcast(P)).then_inc(small_in, 16)
                sp.dma_start(w_out[:], A["Wo"][l].rearrange("(h p) c -> p h c", p=P)).then_inc(w_in, 16)
                sp.dma_start(w_up[:], A["W1"][l]).then_inc(w_in, 16)
                sp.dma_start(w_down[:, 0:2, :], A["W2"][l, 0:256].rearrange("(h p) c -> p h c", p=P)).then_inc(w_in, 16)
                sp.dma_start(w_down[0:FF - 256, 2, :], A["W2"][l, 256:FF]).then_inc(w_in, 16)

        @block.tensor
        def _(pe):
            seed(pe, [x_turned, projected, qk_turned, scored, p_turned, attended, out_projected, ffn_pe])

            def turn_x(it):
                pe.wait_ge(*at(staged, it, 1))
                pe.wait_ge(*at(shifted_in, it, 0))
                pe.wait_ge(*at(y1_done, it, 1, 3))
                pe.transpose(FB[:, 0:P], y_in[:, it.slot, :], ident[:]).then_inc(x_turned, 1)

            def project(chunks):
                order = [0, 2, 1, 3, 4, 5]

                def do(it):
                    for c in chunks:
                        if c == 0:
                            pe.wait_ge(*at(shifted_in, it, 3))
                        if c == 0 or c == 1:
                            pe.wait_ge(*at(v_in, it, c + 1, 1))
                        else:
                            pe.wait_ge(*at(roped, it, 2 * (c - 2) + 2))
                        w = order[c] * 512
                        pe.matmul(ATT[c % 2], shifted[:, it.slot, 0:P], w_qkv[:, w:w + 512],
                                  start=True, stop=True).then_inc(projected, 1)
                return do

            def turn_qk(it):
                for n, c in enumerate([0, 2, 1, 3]):
                    pe.wait_ge(*at(qk_normed, it, c + 1))
                    if n < 2:
                        pe.wait_ge(*at(p_spread_a, it, 6, 2))
                        pe.wait_ge(*at(p_spread_d, it, 6, 2))
                        pe.wait_ge(*at(qk_in, it, 3 + n, 1))
                    else:
                        pe.wait_ge(*at(qk_in, it, n - 1))
                    for j in range(4):
                        m = pe.transpose(TR[:, n % 2, j * P:(j + 1) * P],
                                         qk[:, it.slot % 2, c, j * P:(j + 1) * P], ident[:])
                    m.then_inc(qk_turned, 1)

            def score(s):
                def do(it):
                    b = it.slot % 2
                    if s == 0:
                        pe.wait_ge(*at(qk_in, it, 4))
                        pe.wait_ge(*at(k_prev, it, 1))
                    pe.wait_ge(*at(masked, it, s + 1, 1))
                    pe.sem_inc(held, 1)
                    par = s
                    r = slice(64 * par, 64 * par + 64)
                    for pr in range(8):
                        for j in range(4):
                            m = pe.matmul(SC[s][32 * j:32 * j + 32, pr * 64:pr * 64 + 64],
                                          qT[r, b, pr, 32 * j:32 * j + 32],
                                          kT[r, b, pr, 32 * j:32 * j + 64],
                                          start=True, stop=True, tile_position=(64 * par, 32 * j))
                    m.then_inc(scored, 1)
                return do

            def turn_p(it):
                b = it.slot % 2
                for c in range(2):
                    pe.wait_ge(*at(p_scaled, it, c + 1))
                    if c == 0 and it.has(1):
                        pe.wait_ge(*at(qk_in, it, 4, -1))
                    elif c == 0:
                        pe.wait_ge(*at(p_spread_a, it, 6, 1))
                        pe.wait_ge(*at(p_spread_d, it, 6, 1))
                    for j in range(4):
                        m = pe.transpose(TR[:, c, j * P:(j + 1) * P], sc[:, b, c, j * P:(j + 1) * P], ident[:])
                m.then_inc(p_turned, 1)

            def attend(it):
                b = it.slot % 2
                pe.wait_ge(*at(p_spread_a, it, 6))
                pe.wait_ge(*at(p_spread_d, it, 6))
                pe.wait_ge(*at(v_in, it, 2))
                for c in range(2):
                    pe.wait_ge(*at(o_in, it, c))
                    for j in range(4):
                        for par in range(2):
                            h = 8 * c + 2 * j + par
                            pe.matmul(OB[64 * par:64 * par + 64, j * P:(j + 1) * P],
                                      V[:, it.slot, h * HD:(h + 1) * HD], pT[:, b, h, :],
                                      start=True, stop=False, tile_position=(0, 64 * par))
                        for par in range(2):
                            h = 8 * c + 2 * j + par
                            m = pe.matmul(OB[64 * par:64 * par + 64, j * P:j * P + WIN],
                                          V[96:128, (it.slot - 1) % U, h * HD:(h + 1) * HD],
                                          pT_prev[96:128, b, h, :],
                                          start=False, stop=True, tile_position=(96, 64 * par))
                    m.then_inc(attended, 1)

            def project_out(it):
                pe.wait_ge(*at(o_in, it, 2))
                if it.has(2):
                    pe.wait_ge(*at(shifted_in, it, 3, -2))
                pe.wait_ge(*at(y_done, it, 1, 1))
                for j in range(8):
                    m = pe.matmul(FB[:, 0:C], oT[:, it.slot % 2, j, :], w_out[:, j, :], start=(j == 0), stop=(j == 7))
                m.then_inc(out_projected, 1)

            def ffn(n):
                def do(it):
                    if n == 0:
                        pe.wait_ge(*at(y1_done, it, 1))
                        if it.has(3):
                            pe.wait_ge(*at(shifted_in, it, 3, -3))
                        m = pe.transpose(FB[:, 0:P], y1[:, it.slot, :], ident[:])
                    if n == 1:
                        pe.wait_ge(*at(ffn_act, it, 3))
                        m = pe.transpose(FB[:, 0:P], f_shift[:, it.slot, 0:P], ident[:])
                    if n == 2:
                        pe.wait_ge(*at(ffn_dve, it, 4))
                        m = pe.transpose(FB[:, 0:P], xn[:], ident[:])
                    if n in (3, 4):
                        pe.wait_ge(*at(ffn_act, it, 4 if n == 3 else 7))
                        for c, (f, w) in enumerate(FCH):
                            off = f + (FF if n == 3 else 0)
                            m = pe.matmul(FB[0:w, c * P:(c + 1) * P], w_up[:, off:off + w], xg[:], start=True, stop=True)
                    if n == 5:
                        pe.wait_ge(*at(ffn_dve, it, 7))
                        for c, (f, w) in enumerate(FCH):
                            m = pe.matmul(FB[:, 0:C], hid[0:w, c, :], w_down[0:w, c, :], start=(c == 0), stop=(c == 2))
                    m.then_inc(ffn_pe, 1)
                return do

            pe.wait_ge(zeroed, 7)
            with pe.Fori(0, DEPTH, 1) as l:
                pe.wait_ge(w_in, l * 80 + 80)
                pipeline(pe, l * NT, NT, U, [
                    (1, turn_x), (2, turn_qk), (1, project([0, 1])), (4, ffn(0)), (1, project([2, 3])),
                    (4, ffn(1)), (2, score(0)), (4, ffn(2)), (1, project([4, 5])), (4, ffn(3)),
                    (2, score(1)), (4, ffn(4)), (3, turn_p), (4, ffn(5)), (3, attend), (3, project_out)])

        @block.scalar
        def _(act):
            seed(act, [shifted_in, squared, v_in, qk_in, k_prev, exped, p_spread_a, o_in, ffn_act])

            def shift_in(buf, ring_free, src_sem, k, out_sem, back):
                def do(it):
                    act.wait_ge(*at(src_sem, it, k))
                    for s, kk, bk in ring_free:
                        act.wait_ge(*at(s, it, kk, bk))
                    act.wait_ge(*at(out_sem, it, back[0], 1))
                    act.activation(buf[0:64, it.slot, 0:P], FB[0:64, 0:P], ACT.Copy).then_inc(out_sem, 1)
                    act.activation(buf[64:P, it.slot, 1:P + 1], FB[64:P, 0:P], ACT.Copy).then_inc(out_sem, 1)
                    act.activation(buf[64:P, it.slot, 0:1], buf[64:P, (it.slot - 1) % U, P:P + 1], ACT.Identity,
                                   scale=keep_carry[64:P, bass.ds(it.t % TPB, 1)]).then_inc(out_sem, 1)
                return do

            def square(chunks):
                def do(it):
                    for c in chunks:
                        act.wait_ge(*at(projected, it, c + 1))
                        act.wait_ge(*(at(ss_done, it, c - 1) if c >= 2 else at(ss_done, it, c + 3, 1)))
                        act.activation(squares[:, c % 2, :], ATT[c % 2], ACT.Square).then_inc(squared, 1)
                return do

            def take_v(it):
                act.wait_ge(*at(attended, it, 2, 3))
                for c in range(2):
                    act.wait_ge(*at(projected, it, 5 + c))
                    act.activation(V[:, it.slot, 512 * c:512 * c + 512], ATT[c], ACT.Copy).then_inc(v_in, 1)

            def take_qk(it):
                b = it.slot % 2
                act.wait_ge(*at(scored, it, 2, 2))
                act.wait_ge(*at(qk_in, it, 4, 1))
                act.wait_ge(*at(k_prev, it, 1, 1))
                act.sem_inc(held, 1)
                act.activation(kT[:, b, :, 0:WIN], kT[:, 1 - b, :, P:P + WIN], ACT.Identity,
                               scale=keep_carry[:, bass.ds(it.t % TPB, 1)]).then_inc(k_prev, 1)
                for n in range(4):
                    act.wait_ge(*at(qk_turned, it, n + 1))
                    dst = qT[:, b, 4 * n:4 * n + 4, :] if n < 2 else kT[:, b, 4 * n - 8:4 * n - 4, WIN:]
                    act.activation(dst, TR[:, n % 2, :].rearrange("p (a q) -> p a q", a=4), ACT.Copy).then_inc(qk_in, 1)

            def exps(it):
                b = it.slot % 2
                for c in range(2):
                    act.wait_ge(*at(shifted_max, it, c + 1))
                    act.activation(sc[:, b, c, :], sc[:, b, c, :], ACT.Exp).then_inc(exped, 1)

            def spread_a(it):
                act.wait_ge(*at(p_turned, it, 1))
                act.wait_ge(*at(attended, it, 2, 2))
                spread(act.activation, it, 0, p_spread_a)

            def take_o(it):
                act.wait_ge(*at(out_projected, it, 1, 2))
                for c in range(2):
                    act.wait_ge(*at(attended, it, c + 1))
                    act.activation(oT[:, it.slot % 2, 4 * c:4 * c + 4, :],
                                   OB.rearrange("p (a q) -> p a q", a=4), ACT.Copy).then_inc(o_in, 1)

            def ffn_gain(it):
                act.wait_ge(*at(ffn_pe, it, 3))
                act.wait_ge(*at(ffn_pe, it, 5, 1))
                act.activation(xg[:], FB[:, 0:P], ACT.Identity, scale=cols[:, 6:7], bias=cols[:, 7:8]).then_inc(ffn_act, 1)

            def ffn_gelu(it):
                act.wait_ge(*at(ffn_pe, it, 4))
                act.wait_ge(*at(ffn_dve, it, 7, 1))
                for c, (f, w) in enumerate(FCH):
                    act.activation(gate[0:w, c, :], FB[0:w, c * P:(c + 1) * P], ACT.Gelu,
                                   bias=cols[0:w, 3 + c:4 + c]).then_inc(ffn_act, 1)

            act.wait_ge(consts, 48)
            act.wait_ge(zeroed, 7)
            with act.Fori(0, DEPTH, 1) as l:
                act.wait_ge(small_in, l * 32 + 32)
                pipeline(act, l * NT, NT, U, [
                    (1, shift_in(shifted, [(projected, 6, 4), (shifted_in, 3, 3)], x_turned, 1, shifted_in, [3])),
                    (2, take_qk), (1, square([0, 1])),
                    (4, shift_in(f_shift, [(ffn_pe, 2, 4)], ffn_pe, 1, ffn_act, [7])),
                    (1, square([2, 3])), (4, ffn_gain), (1, take_v), (4, ffn_gelu),
                    (2, exps), (3, spread_a), (3, take_o)])

        @block.vector
        def _(dve):
            seed(dve, [roped, ss_done, rs_step, masked, maxed, summed, inverted, p_spread_d, y1_done, ffn_dve, y_done])
            dve.memset(V[:], 0.0).then_inc(zeroed, 1)
            dve.memset(kT[:], 0.0).then_inc(zeroed, 1)
            dve.memset(pT[:], 0.0).then_inc(zeroed, 1)
            dve.memset(shifted[:], 0.0).then_inc(zeroed, 1)
            dve.memset(f_shift[:], 0.0).then_inc(zeroed, 1)
            dve.memset(minus_half[:], -0.5).then_inc(zeroed, 1)
            dve.memset(y1[:], 0.0).then_inc(zeroed, 1)

            def rotate(chunks):
                def do(it):
                    for c in chunks:
                        side = c % 2
                        dve.wait_ge(*at(squared, it, c + 1))
                        if c == 0:
                            dve.wait_ge(*at(qk_turned, it, 4, 2))
                        x = ATT[c % 2].rearrange("p (h r d) -> p h r d", h=8, r=2)
                        table = rope[:, bass.ds(it.t % TPB, 1), 2 * side:2 * side + 2, :]
                        cos = table[:, :, 0, :].to_broadcast([P, 8, HD])
                        sin = table[:, :, 1, :].to_broadcast([P, 8, HD]).rearrange("p h (r d) -> p h r d", r=2)
                        dve.tensor_tensor(qk[:, it.slot % 2, c, :].rearrange("p (h d) -> p h d", h=8),
                                          ATT[c % 2].rearrange("p (h d) -> p h d", h=8), cos, ALU.mult).then_inc(roped, 1)
                        dve.wait_ge(*(at(rope_added, it, c - 1) if c >= 2 else at(rope_added, it, c + 3, 1)))
                        dve.tensor_tensor(rotated[:, c % 2, :].rearrange("p (h r d) -> p h r d", h=8, r=2),
                                          x[:, :, ::-1, :], sin, ALU.mult).then_inc(roped, 1)
                return do

            def sum_squares(chunks):
                def do(it):
                    for c in chunks:
                        dve.wait_ge(*at(squared, it, c + 1))
                        dve.tensor_reduce(ss[:, it.slot % 2, 8 * c:8 * c + 8],
                                          squares[:, c % 2, :].rearrange("p (h d) -> p h d", h=8),
                                          AX.X, ALU.add).then_inc(ss_done, 1)
                return do

            def inverse_norms(it):
                b = it.slot % 2
                half, t = ss[:, b, :], rs_a[:]
                n = [0]

                def link(ins):
                    n[0] += 1
                    ins.then_inc(rs_step, 1)
                    dve.wait_ge(*at(rs_step, it, n[0]))
                dve.wait_ge(*at(ss_done, it, 4))
                dve.wait_ge(*at(qk_normed, it, 4, 2))
                link(dve.tensor_scalar(half, half, 1e-24, 0.5, ALU.max, ALU.mult))
                link(dve.tensor_scalar(rs_b[:].bitcast(I32), half.bitcast(I32), 1, None, ALU.logical_shift_right))
                y = rs_y[:, b, :]
                link(dve.tensor_scalar(y.bitcast(I32), rs_b[:].bitcast(I32), -1.0, RSQRT_SEED, ALU.mult, ALU.add))
                for _ in range(3):
                    link(dve.tensor_tensor(t, y, y, ALU.mult))
                    link(dve.tensor_tensor(t, t, half, ALU.mult))
                    link(dve.scalar_tensor_tensor(out=y, in0=t, scalar=-1.5, in1=y, op0=ALU.add, op1=ALU.mult))

            def mask_and_max(c):
                def do(it):
                    b = it.slot % 2
                    dve.wait_ge(*at(scored, it, c + 1))
                    dve.wait_ge(*at(p_turned, it, 1, 2))
                    m = mask[:, bass.ds(it.t % TPB, 1), :].to_broadcast([P, 8, 2 * WIN])
                    s = sc[:, b, c, :].rearrange("p (h k) -> p h k", h=8)
                    dve.scalar_tensor_tensor(out=s, in0=SC[c].rearrange("p (h k) -> p h k", h=8), scalar=QK_SCALE,
                                             in1=m, op0=ALU.mult, op1=ALU.add).then_inc(masked, 1)
                    dve.wait_ge(*at(masked, it, c + 1))
                    dve.wait_ge(*at(shifted_max, it, c + 1, 2))
                    dve.tensor_reduce(mx[:, b, 8 * c:8 * c + 8], s, AX.X, ALU.max).then_inc(maxed, 1)
                return do

            def sum_p(it):
                b = it.slot % 2
                for c in range(2):
                    h = slice(8 * c, 8 * c + 8)
                    dve.wait_ge(*at(exped, it, c + 1))
                    dve.tensor_reduce(sm[:, b, h], sc[:, b, c, :].rearrange("p (h k) -> p h k", h=8),
                                      AX.X, ALU.add).then_inc(summed, 1)
                    dve.wait_ge(*at(summed, it, c + 1))
                    dve.wait_ge(*at(p_scaled, it, c + 1, 2))
                    dve.reciprocal(rsum[:, b, h], sm[:, b, h]).then_inc(inverted, 1)

            def spread_d(it):
                dve.wait_ge(*at(p_turned, it, 1))
                dve.wait_ge(*at(attended, it, 2, 2))
                spread(dve.tensor_copy, it, 1, p_spread_d)

            def residual(it):
                dve.wait_ge(*at(out_projected, it, 1))
                dve.wait_ge(*at(ffn_pool, it, 2, 4))
                dve.wait_ge(*at(ffn_pe, it, 1, 4))
                dve.tensor_tensor(y1[:, it.slot, :], FB[:, 0:C], Y[:, bass.ds(it.t, 1), :].rearrange("p o c -> p (o c)"),
                                  ALU.add).then_inc(y1_done, 1)

            def ffn_stats(it):
                dve.wait_ge(*at(ffn_pe, it, 2))
                dve.bn_stats(stats[:], FB[:, 0:C]).then_inc(ffn_dve, 1)
                dve.wait_ge(*at(ffn_dve, it, 1))
                dve.sem_inc(held, 1)
                dve.bn_aggr(mv[:], stats[:]).then_inc(ffn_dve, 1)
                dve.wait_ge(*at(ffn_dve, it, 2))
                dve.tensor_scalar(veps[:], mv[:, 1:2], 1e-5, None, ALU.add).then_inc(ffn_dve, 1)

            def ffn_norm(it):
                dve.wait_ge(*at(ffn_pool, it, 1))
                dve.wait_ge(*at(ffn_pe, it, 3, 1))
                dve.tensor_scalar(xn[:], FB[:, 0:C], mv[:, 0:1], rstd[:], ALU.subtract, ALU.mult).then_inc(ffn_dve, 1)

            def ffn_gated(it):
                dve.wait_ge(*at(ffn_pe, it, 5))
                dve.wait_ge(*at(ffn_pe, it, 6, 1))
                for c, (f, w) in enumerate(FCH):
                    dve.scalar_tensor_tensor(out=hid[0:w, c, :], in0=FB[0:w, c * P:(c + 1) * P],
                                             scalar=cols[0:w, c:c + 1], in1=gate[0:w, c, :],
                                             op0=ALU.add, op1=ALU.mult).then_inc(ffn_dve, 1)

            def ffn_sum(it):
                dve.wait_ge(*at(ffn_pe, it, 6))
                dve.wait_ge(*at(ffn_pool, it, 2))
                dve.tensor_tensor(Y[:, bass.ds(it.t, 1), :].rearrange("p o c -> p (o c)"), FB[:, 0:C],
                                  y1b[:, it.slot % 2, :], ALU.add).then_inc(y_done, 1)

            with dve.Fori(0, DEPTH, 1) as l:
                dve.wait_ge(tables, l + 1)
                pipeline(dve, l * NT, NT, U, [
                    (1, rotate([0, 1])), (1, sum_squares([0, 1])), (1, rotate([2, 3])), (4, ffn_stats),
                    (1, sum_squares([2, 3])), (2, mask_and_max(0)), (4, ffn_norm), (1, inverse_norms),
                    (2, mask_and_max(1)), (4, ffn_gated), (2, sum_p), (3, spread_d), (4, ffn_sum), (3, residual)])

        @block.gpsimd
        def _(pool):
            seed(pool, [staged, rope_added, qk_normed, shifted_max, p_scaled, ffn_pool])

            def stage(it):
                pool.wait_ge(*at(x_turned, it, 1, 4))
                pool.sem_inc(held, 1)
                pool.tensor_copy(y_in[:, it.slot, :], Y[:, bass.ds(it.t, 1), :].rearrange("p o c -> p (o c)")).then_inc(staged, 1)

            def add_rotated(it):
                for c in range(4):
                    pool.wait_ge(*at(roped, it, 2 * c + 2))
                    dst = qk[:, it.slot % 2, c, :]
                    pool.tensor_tensor(dst, dst, rotated[:, c % 2, :], ALU.add).then_inc(rope_added, 1)

            def norm(it):
                b = it.slot % 2
                pool.wait_ge(*at(rs_step, it, 12))
                pool.wait_ge(*at(rope_added, it, 4))
                for c in range(4):
                    dst = qk[:, b, c, :].rearrange("p (h d) -> p h d", h=8)
                    r = rs_y[:, b, 8 * c:8 * c + 8].unsqueeze(2).to_broadcast([P, 8, HD])
                    pool.tensor_tensor(dst, dst, r, ALU.mult).then_inc(qk_normed, 1)

            def subtract_max(it):
                b = it.slot % 2
                for c in range(2):
                    pool.wait_ge(*at(maxed, it, c + 1))
                    s = sc[:, b, c, :].rearrange("p (h k) -> p h k", h=8)
                    pool.tensor_tensor(s, s, mx[:, b, 8 * c:8 * c + 8].unsqueeze(2).to_broadcast([P, 8, 2 * WIN]),
                                       ALU.subtract).then_inc(shifted_max, 1)

            def scale_p(it):
                b = it.slot % 2
                for c in range(2):
                    pool.wait_ge(*at(inverted, it, c + 1))
                    s = sc[:, b, c, :].rearrange("p (h k) -> p h k", h=8)
                    pool.tensor_tensor(s, s, rsum[:, b, 8 * c:8 * c + 8].unsqueeze(2).to_broadcast([P, 8, 2 * WIN]),
                                       ALU.mult).then_inc(p_scaled, 1)

            def ffn_rstd(it):
                pool.wait_ge(*at(ffn_dve, it, 3))
                pool.tensor_tensor(rstd[:], veps[:], minus_half[:], ALU.pow).then_inc(ffn_pool, 1)

            def ffn_bias(it):
                pool.wait_ge(*at(y1_done, it, 1))
                pool.wait_ge(*at(y_done, it, 1, 2))
                pool.tensor_tensor(y1b[:, it.slot % 2, :], y1[:, it.slot, :], rows[:, 0:P], ALU.add).then_inc(ffn_pool, 1)

            pool.wait_ge(consts, 48)
            pool.wait_ge(zeroed, 7)
            with pool.Fori(0, DEPTH, 1) as l:
                done = Item(l * NT)
                pool.wait_ge(small_in, l * 32 + 32)
                pool.wait_ge(*at(y_done, done, 0))
                par = rows[:, P:].rearrange("p (o a d) -> p o a d", o=1, a=4).to_broadcast([P, TPB, 4, HD])
                pool.tensor_tensor(rope[:], rope_base[:], par, ALU.mult).then_inc(tables, 1)
                pipeline(pool, l * NT, NT, U, [
                    (0, stage), (1, add_rotated), (4, ffn_rstd), (4, ffn_bias), (2, subtract_max), (1, norm), (2, scale_p)])


def sandwich_kernel(nc, A, out):
    with ExitStack() as ctx:
        x = ctx.enter_context(nc.sbuf_tensor("x", [P, NT, C], F32))
        y = ctx.enter_context(nc.sbuf_tensor("y", [P, NT, C], F32))
        ident = ctx.enter_context(nc.sbuf_tensor("ident", [P, P], F32))
        psum = ctx.enter_context(nc.psum_tensor("psum", [P, 8, 512], F32))
        x_loaded = ctx.enter_context(nc.semaphore("x_loaded"))
        out_stored = ctx.enter_context(nc.semaphore("out_stored"))
        scratch = nc.dram_tensor("router_weights_dram", (NT, P), F32).ap()
        norms = Normalizer(nc, ctx)

        with nc.Block() as block:
            @block.sync
            def _(sp):
                sp.dma_start(x[:], A["x"].rearrange("b (t p) c -> p (b t) c", p=P)).then_inc(x_loaded, 16)
                sp.dma_start(ident[:], A["ident"]).then_inc(x_loaded, 16)
                sp.wait_ge(x_loaded, 32)

        norms.run(x, y, LN_EPS)
        causal_attention(nc, A, y, y, ident, psum)
        norms.run(y, y, LN_EPS, residual=x)
        norms.run(x, y, LN_EPS)
        routed_block(nc, A, y, y, ident, psum, scratch)
        norms.run(y, y, LN_EPS, residual=x)
        norms.run(x, y, LN_EPS)
        linear_attention(nc, A, y, y, ident, psum)
        norms.run(y, y, LN_EPS, residual=x)
        norms.run(x, y, LN_EPS)
        local_transformer(nc, A, y, ident, psum)
        norms.run(y, y, LN_EPS, residual=x)

        with nc.Block() as block:
            @block.sync
            def _(sp):
                sp.dma_start(out.rearrange("b (t p) c -> p (b t) c", p=P), x[:]).then_inc(out_stored, 16)
                sp.wait_ge(out_stored, 16)


def _lay_out(inputs):
    import numpy as np
    f = np.float32
    d = {k: np.asarray(v) for k, v in inputs.items()}
    masked = f(-3e38)
    a = {"x": d["L0_attn_x"], "ident": np.eye(P, dtype=f)}

    for k in ("w_kv_down", "w_kv_up", "w_q", "w_out"):
        a[k] = d["L0_attn_" + k]
    a["causal"] = np.where(np.tril(np.ones((P, P), bool)), f(0), masked).astype(f)

    for k in ("attention_mask", "position_ids", "router_w", "router_b", "wq", "wk", "wv", "wo", "w1", "w2", "ln1", "ln2"):
        a[k] = d["L0_ffn_" + k]
    positions = a.pop("position_ids")
    positions = np.concatenate([positions, np.repeat(positions[:, -1:], T - positions.shape[1], 1)], 1)
    a["pos"] = positions.reshape(B, TPB, P).transpose(2, 0, 1)
    token, column = np.arange(P)[:, None], np.arange(2 * T - P)[None]
    a["from_here"] = (column - (T - P) >= token).astype(f)
    slot = np.arange(P)
    a["slots"] = np.tile(np.where(slot < P - 1, slot, -1).astype(f), (P, 1))
    a["spare"] = np.tile(np.where(slot < P - 1, f(0), masked).astype(f), (P, 1))
    all_last = np.zeros((P, P), f)
    all_last[:, P - 1] = 1
    a["last_row"] = np.stack([np.eye(P, dtype=f), all_last], 1)
    a["halves_sign"] = np.tile(np.array([-1, 1], f), (P, 1))
    a["inv_freq"] = np.tile(f(1) / f(10000) ** (np.arange(0, 8, 2, dtype=f) / f(8)), (P, 1)).astype(f)
    a["head_cols"] = (np.arange(P)[:, None] // 8 == np.arange(16)[None]).astype(f)

    a["head_blocks"] = np.repeat(a["head_cols"], 8, 1)

    a["la_wT"] = np.stack([d["L1_attn_" + k].T for k in ("Wq", "Wk", "Wv", "Wo")], 1)
    a["la_bias_cols"] = np.stack([d["L1_attn_bq"], d["L1_attn_bk"]], 1)
    a["la_bias_rows"] = np.stack([d["L1_attn_bv"], d["L1_attn_bo"]], 0)
    a["la_PT"] = d["L1_attn_P"].T

    for k in ("Wqkv", "Wo", "W1", "W2"):
        a[k] = d["L1_ffn_" + k]
    b1 = d["L1_ffn_b1"]
    cols = np.zeros((DEPTH, P, 8), b1.dtype)
    for k, (lo, w) in enumerate(FCH):
        cols[:, :w, k] = b1[:, lo:lo + w]
        cols[:, :w, 3 + k] = b1[:, FF + lo:FF + lo + w]
    cols[:, :, 6], cols[:, :, 7] = d["L1_ffn_ln_g"], d["L1_ffn_ln_b"]
    a["cols"] = cols

    def rotated(v):
        return np.concatenate([v[:, HD // 2:], v[:, :HD // 2]], 1)
    q, k = d["L1_ffn_q_scale"], d["L1_ffn_k_scale"]
    a["rows"] = np.concatenate([d["L1_ffn_b2"], q, rotated(q), k, rotated(k)], 1)
    half = np.arange(0, HD, 2, dtype=f)
    inv_freq = f(1) / (f(10000) ** (half / f(HD))).astype(f)
    position = np.arange(T, dtype=f)
    freqs = (position[:, None] * inv_freq[None]).astype(f)
    base = ((half + f(0.4 * HD)) / f(1.4 * HD)).astype(f)
    scale = (base[None] ** ((position - T // 2) / f(WIN // 2)).astype(f)[:, None]).astype(f)
    freqs, scale = np.concatenate([freqs, freqs], 1), np.concatenate([scale, scale], 1)
    sign = np.concatenate([-np.ones(HD // 2, f), np.ones(HD // 2, f)])
    table = np.stack([np.cos(freqs) * scale, np.sin(freqs) * sign * scale,
                      np.cos(freqs) * (f(1) / scale), np.sin(freqs) * sign * (f(1) / scale)], 1)
    a["rope_base"] = table.reshape(TPB, P, 4, HD).transpose(1, 0, 2, 3).astype(f)
    row, column = np.arange(P)[:, None] % WIN, np.arange(2 * WIN)[None]
    window = np.where((column >= row) & (column <= row + WIN), f(0), masked).astype(f)
    window = np.repeat(window[:, None], TPB, 1)
    window[0:WIN, 0, 0:WIN] = masked
    a["win_mask"] = window
    keep = np.ones((P, TPB), f)
    keep[:, 0] = 0
    a["keep_carry"] = keep
    return {k: np.ascontiguousarray(v) for k, v in a.items()}


def kernel(**inputs):
    import concourse.bacc as bacc
    from concourse.bass_utils import run_bass_kernel_spmd

    nc = bacc.Bacc("TRN2", target_bir_lowering=False, num_devices=1)
    arrays, aps = {}, {}
    for name, a in _lay_out(inputs).items():
        arrays[f"in_{name}_dram"] = a
        aps[name] = nc.dram_tensor(f"in_{name}_dram", a.shape, mybir.dt.from_np(a.dtype), kind="ExternalInput").ap()
    out = nc.dram_tensor("out_dram", (B, T, C), F32, kind="ExternalOutput").ap()
    sandwich_kernel(nc, aps, out)
    result = run_bass_kernel_spmd(nc, [arrays], core_ids=[0])
    return result.results[0]["out_dram"]
```

```python
from contextlib import ExitStack

import concourse.bass as bass
from concourse import mybir

F32 = mybir.dt.float32
I32 = mybir.dt.int32
U32 = mybir.dt.uint32
ALU = mybir.AluOpType
ACT = mybir.ActivationFunctionType
AX = mybir.AxisListType

P = 128
B, T, C = 4, 1024, 128
NT = B * T // P
TPB = T // P
LN_EPS = 1e-5


class Item:

    def __init__(self, index, t=0, slot=0, turn=0, units=None):
        self.index, self.t, self.slot, self.turn, self.units = index, t, slot, turn, units

    def has(self, ahead):
        return self.units is None or self.t + ahead < self.units


SEED = 8


def reached(item, per, k, back=0, seed=SEED):
    return (item.index + (seed - back)) * per + k


def pipeline(eng, base, units, unroll, stages):
    lag_max = max(lag for lag, _ in stages)
    peeled = -(-lag_max // unroll) * unroll

    def step(s, static, u, turn):
        for lag, do in stages:
            if static and not 0 <= s - lag < units:
                continue
            do(Item(base + (s - lag), s - lag, (u - lag) % unroll, turn + (u - lag) // unroll,
                    units if static else None))

    for s in range(peeled):
        step(s, True, s % unroll, s // unroll)
    with eng.Fori(0, (units - peeled) // unroll, 1) as k:
        for u in range(unroll):
            step(k * unroll + (peeled + u), False, u, k + peeled // unroll)
    for s in range(units, units + lag_max):
        step(s, True, s % unroll, s // unroll)


class Normalizer:

    G = 4
    W = NT // G

    def __init__(self, nc, ctx):
        def sb(n, shape):
            return ctx.enter_context(nc.sbuf_tensor("n_" + n, shape, F32))

        def sem(n):
            return ctx.enter_context(nc.semaphore("n_" + n))

        self.nc, self.runs, self.residual_runs = nc, 0, 0
        self.mean, self.var, self.rstd, self.power = (
            sb("mean", [P, NT]), sb("var", [P, NT]), sb("rstd", [P, NT]), sb("power", [P, NT]))
        self.power_set = sem("power_set")
        self.summed, self.centred, self.squared, self.var_done, self.rstd_done, self.scaled, self.ended = (
            sem("summed"), sem("centred"), sem("squared"), sem("var_done"), sem("rstd_done"), sem("scaled"), sem("ended"))

    def run(self, src, dst, eps, residual=None):
        nc, G, W, n, r = self.nc, self.G, self.W, self.runs, self.residual_runs
        mean, var, rstd, power = self.mean, self.var, self.rstd, self.power
        power_set, summed, centred, squared = self.power_set, self.summed, self.centred, self.squared
        var_done, rstd_done, scaled, ended = self.var_done, self.rstd_done, self.scaled, self.ended
        self.runs += 1
        self.residual_runs += residual is not None

        def tiles(g):
            return slice(W * g, W * g + W)

        with nc.sbuf_tensor(f"n_squares_{n}", [P, NT, C], F32) as squares, nc.Block() as block:
            @block.vector
            def _(dve):
                if n == 0:
                    dve.memset(power[:], -0.5).then_inc(power_set, 1)
                for g in range(G):
                    dve.tensor_reduce(mean[:, tiles(g)], src[:, tiles(g), :], AX.X, ALU.add).then_inc(summed, 1)
                dve.wait_ge(summed, n * (G + 1) + G)
                dve.tensor_scalar(mean[:], mean[:], 1.0 / C, None, ALU.mult).then_inc(summed, 1)
                dve.wait_ge(summed, (n + 1) * (G + 1))
                for g in range(G):
                    dve.tensor_tensor(dst[:, tiles(g), :], src[:, tiles(g), :],
                                      mean[:, tiles(g)].unsqueeze(2).to_broadcast([P, W, C]),
                                      ALU.subtract).then_inc(centred, 1)
                for g in range(G):
                    dve.wait_ge(squared, n * G + g + 1)
                    dve.tensor_reduce(var[:, tiles(g)], squares[:, tiles(g), :], AX.X, ALU.add).then_inc(var_done, 1)
                    dve.wait_ge(var_done, 2 * (n * G + g) + 1)
                    dve.tensor_scalar(var[:, tiles(g)], var[:, tiles(g)], 1.0 / C, eps, ALU.mult, ALU.add).then_inc(var_done, 1)
                for g in range(G):
                    dve.wait_ge(rstd_done, n * G + g + 1)
                    dve.tensor_tensor(dst[:, tiles(g), :], dst[:, tiles(g), :],
                                      rstd[:, tiles(g)].unsqueeze(2).to_broadcast([P, W, C]), ALU.mult).then_inc(scaled, 1)
                    if residual is not None:
                        dve.wait_ge(scaled, n * G + g + 1)
                        dve.tensor_tensor(residual[:, tiles(g), :], residual[:, tiles(g), :], dst[:, tiles(g), :],
                                          ALU.add).then_inc(ended, 1)
                dve.wait_ge(scaled, (n + 1) * G)
                if residual is not None:
                    dve.wait_ge(ended, (r + 1) * G)

            @block.scalar
            def _(act):
                for g in range(G):
                    act.wait_ge(centred, n * G + g + 1)
                    act.activation(squares[:, tiles(g), :], dst[:, tiles(g), :], ACT.Square).then_inc(squared, 1)

            @block.gpsimd
            def _(pool):
                pool.wait_ge(power_set, 1)
                for g in range(G):
                    pool.wait_ge(var_done, 2 * (n * G + g + 1))
                    pool.tensor_tensor(rstd[:, tiles(g)], var[:, tiles(g)], power[:, tiles(g)], ALU.pow).then_inc(rstd_done, 1)


def causal_attention(nc, A, xn, z, ident, psum):
    H, D = 16, 64
    PAIRS, QT = H // 2, TPB
    UNITS, U = PAIRS * QT, 2 * QT
    SEEDED = 24
    with ExitStack() as ctx:
        def sb(name, shape):
            return ctx.enter_context(nc.sbuf_tensor("a_" + name, shape, F32))

        def sem(name):
            return ctx.enter_context(nc.semaphore("a_" + name))

        w_down, w_up, w_q = sb("w_down", [P, P]), sb("w_up", [P, 2 * H * D]), sb("w_q", [P, H * D])
        w_out = sb("w_out", [P, PAIRS, C])
        causal = sb("causal", [P, P])
        w_pair = sb("w_pair", [P, 3, P])
        x_b = sb("x_b", [P, TPB, C])
        xT, latT = sb("xT", [P, T]), sb("latT", [P, T])
        qT, kT, V = sb("qT", [P, 2, T]), sb("kT", [P, 2, T]), sb("V", [P, 2, TPB, P])
        probs = sb("probs", [P, 2, 2, T])
        pT = sb("pT", [P, 2, 2, T])
        nmax, rsum, rinv = sb("nmax", [P, 2, 2]), sb("rsum", [P, 2, 2]), sb("rinv", [P, 2, 2])
        oT = sb("oT", [P, PAIRS, T])

        S = [psum[:, 2 * h:2 * h + 2, :].rearrange("p a n -> p (a n)") for h in range(2)]
        TR = [psum[:, 4, :], psum[:, 5, :]]
        OB, PB = psum[:, 6, :], psum[:, 7, :]

        loaded, held = sem("loaded"), sem("held")
        x_copied, x_turned, x_in, lat_done, lat_in, out_done, out_in = (
            sem("x_copied"), sem("x_turned"), sem("x_in"), sem("lat_done"), sem("lat_in"), sem("out_done"), sem("out_in"))
        w_staged, projected, proj_in = sem("w_staged"), sem("projected"), sem("proj_in")
        scored, masked, maxed, exped, inverted, scaled, turned, pT_in, attended, o_in = (
            sem("scored"), sem("masked"), sem("maxed"), sem("exped"), sem("inverted"), sem("scaled"), sem("turned"),
            sem("pT_in"), sem("attended"), sem("o_in"))
        PER = {scored: 2, masked: 2, maxed: 2, exped: 2, inverted: 2, scaled: 2, turned: 4, pT_in: 4, attended: 1, o_in: 1}

        def at(s, it, k, back=0):
            return s, reached(it, PER[s], k, back, SEEDED)

        def at_pair(s, it, b, per, k, back=0):
            return s, (b * PAIRS + it.turn * 2 + (it.slot // QT + 2 - back)) * per + k

        def seed(eng, sems):
            for s in sems:
                eng.sem_inc(s, PER[s] * SEEDED)

        def turned_bank(h, chunk, chunks):
            return chunk if chunks == 2 else h

        block = ctx.enter_context(nc.Block())

        @block.sync
        def _(sp):
            sp.dma_start(w_down[:], A["w_kv_down"]).then_inc(loaded, 16)
            sp.dma_start(w_q[:], A["w_q"]).then_inc(loaded, 16)
            sp.dma_start(w_up[:], A["w_kv_up"]).then_inc(loaded, 16)
            sp.dma_start(causal[:], A["causal"]).then_inc(loaded, 16)
            sp.dma_start(w_out[:], A["w_out"].rearrange("(h p) c -> p h c", p=P)).then_inc(loaded, 16)

        @block.gpsimd
        def _(pool):
            pool.sem_inc(w_staged, 2)
            pool.wait_ge(loaded, 80)
            with pool.Fori(0, B, 1) as b:
                def stage(it):
                    if it.slot % QT:
                        return
                    pool.wait_ge(*at_pair(projected, it, b, 6, 0))
                    for n, (w, off) in enumerate([(w_q, 0), (w_up, 0), (w_up, H * D)]):
                        pair = it.turn * 2 + it.slot // QT
                        pool.sem_inc(held, 1)
                        src = w[:, off:off + H * D].rearrange("p (a n) -> p a n", n=P)
                        i = pool.tensor_copy(w_pair[:, n:n + 1, :], src[:, bass.ds(pair, 1), :])
                    i.then_inc(w_staged, 1)
                with pool.Fori(0, PAIRS // 2, 1) as k:
                    for u in (0, QT):
                        stage(Item(0, 0, u, k))

        @block.tensor
        def _(pe):
            seed(pe, [scored, turned, attended])
            pe.sem_inc(projected, 12)
            pe.wait_ge(loaded, 80)
            with pe.Fori(0, B, 1) as b:
                pe.wait_ge(x_copied, b + 1)
                for c in range(2):
                    for j in range(4):
                        m = pe.transpose(TR[c][:, j * P:(j + 1) * P], x_b[:, 4 * c + j, :], ident[:])
                    m.then_inc(x_turned, 1)
                for c in range(2):
                    pe.wait_ge(x_in, 2 * b + c + 1)
                    pe.matmul([OB, PB][c], w_down[:], xT[:, 512 * c:512 * c + 512], start=True, stop=True).then_inc(lat_done, 1)

                def score(h):
                    r = slice(64 * h, 64 * h + 64)

                    def do(it):
                        i, pb = it.slot % QT, it.slot // QT % 2
                        if i == 0 and h == 0:
                            pe.wait_ge(*at_pair(proj_in, it, b, 6, 4))
                        pe.wait_ge(*at(exped, it, h + 1, 1))
                        w = (i + 1) * P
                        for c in range(0, w, 512):
                            n = min(512, w - c)
                            m = pe.matmul(S[h][:, c:c + n], qT[r, pb, i * P:(i + 1) * P], kT[r, pb, c:c + n],
                                          start=True, stop=True)
                        m.then_inc(scored, 1)
                    return do

                def turn(h):
                    def do(it):
                        i, par = it.slot % QT, it.slot % 2
                        pe.wait_ge(*at(scaled, it, h + 1))
                        chunks = range(0, i + 1, 4)
                        for n, c in enumerate(chunks):
                            bank = TR[turned_bank(h, n, len(chunks))]
                            if len(chunks) == 2 and h == 1:
                                pe.wait_ge(*at(pT_in, it, n + 1))
                            elif 1 <= i <= 4:
                                pe.wait_ge(*at(pT_in, it, 2 * (h + n) + 2, 1))
                            else:
                                pe.wait_ge(*at(pT_in, it, 3 + h + n, 1))
                            for k in range(c, min(c + 4, i + 1)):
                                m = pe.transpose(bank[:, (k - c) * P:(k - c + 1) * P],
                                                 probs[:, par, h, k * P:(k + 1) * P], ident[:])
                            m.then_inc(turned, 2 // len(chunks))
                    return do

                def attend(it):
                    i, pb, par = it.slot % QT, it.slot // QT % 2, it.slot % 2
                    if i == 0:
                        pe.wait_ge(*at_pair(proj_in, it, b, 6, 6))
                    pe.wait_ge(*at(pT_in, it, 4))
                    pe.wait_ge(*at(o_in, it, 1, 1))
                    for k in range(i + 1):
                        for h in range(2):
                            m = pe.matmul(OB[64 * h:64 * h + 64, 0:P], V[:, pb, k, 64 * h:64 * h + 64],
                                          pT[:, par, h, k * P:(k + 1) * P], start=(k == 0), stop=(k == i),
                                          tile_position=(0, 64 * h))
                    m.then_inc(attended, 1)

                def project(it):
                    n = it.slot % QT
                    if n == 0:
                        pe.wait_ge(*at_pair(w_staged, it, b, 1, 1))
                        pe.wait_ge(lat_in, 2 * b + 2)
                    if n >= 6:
                        return
                    pe.wait_ge(*at_pair(proj_in, it, b, 6, n))
                    c = n % 2
                    if n < 4:
                        m = pe.matmul(PB, w_pair[:, n // 2, :], [xT, latT][n // 2][:, 512 * c:512 * c + 512],
                                      start=True, stop=True)
                    else:
                        for j in range(4):
                            m = pe.matmul(PB[:, j * P:(j + 1) * P], latT[:, (4 * c + j) * P:(4 * c + j + 1) * P],
                                          w_pair[:, 2, :], start=True, stop=True)
                    m.then_inc(projected, 1)

                pipeline(pe, b * UNITS, UNITS, U, [
                    (8, score(0)), (9, turn(0)), (0, project), (8, score(1)), (9, turn(1)), (10, attend)])
                done = Item(b * UNITS + UNITS)
                pe.wait_ge(*at(o_in, done, 0))
                for i in range(TPB):
                    pe.wait_ge(out_in, b * TPB + i + 1)
                    for p in range(PAIRS):
                        m = pe.matmul([OB, PB][i % 2][:, 0:C], oT[:, p, i * P:(i + 1) * P], w_out[:, p, :],
                                      start=(p == 0), stop=(p == PAIRS - 1))
                    m.then_inc(out_done, 1)

        @block.scalar
        def _(act):
            seed(act, [exped, pT_in])
            act.sem_inc(proj_in, 12)
            with act.Fori(0, B, 1) as b:
                for c in range(2):
                    act.wait_ge(x_turned, 2 * b + c + 1)
                    act.activation(xT[:, 512 * c:512 * c + 512], TR[c], ACT.Copy).then_inc(x_in, 1)
                for c in range(2):
                    act.wait_ge(lat_done, 2 * b + c + 1)
                    act.activation(latT[:, 512 * c:512 * c + 512], [OB, PB][c], ACT.Copy).then_inc(lat_in, 1)

                def take_projection(it):
                    n, pb = it.slot % QT, it.slot // QT % 2
                    if n >= 6:
                        return
                    c = n % 2
                    act.wait_ge(*at_pair(projected, it, b, 6, n + 1))
                    if n < 4:
                        act.wait_ge(*at(scored, it, 2, 9 + n))
                    else:
                        act.wait_ge(*at(attended, it, 1, 9 + n))
                    if n < 2:
                        i = act.activation(qT[:, pb, 512 * c:512 * c + 512], PB, ACT.Copy, scale=float(D) ** -0.5)
                    elif n < 4:
                        i = act.activation(kT[:, pb, 512 * c:512 * c + 512], PB, ACT.Copy)
                    else:
                        i = act.activation(V[:, pb, 4 * c:4 * c + 4, :], PB.rearrange("p (a n) -> p a n", a=4), ACT.Copy)
                    i.then_inc(proj_in, 1)

                def exps(h):
                    def do(it):
                        par, w = it.slot % 2, (it.slot % QT + 1) * P
                        act.wait_ge(*at(maxed, it, h + 1))
                        act.wait_ge(*at(turned, it, 2 * h + 2, 2))
                        act.wait_ge(*at(inverted, it, h + 1, 2))
                        act.activation(probs[:, par, h, 0:w], S[h][:, 0:w], ACT.Exp, bias=nmax[:, par, h:h + 1],
                                       accum_out=rsum[:, par, h:h + 1]).then_inc(exped, 1)
                    return do

                def take_pT(h):
                    def do(it):
                        i, par = it.slot % QT, it.slot % 2
                        chunks = range(0, i + 1, 4)
                        act.wait_ge(*at(attended, it, 1, 2))
                        for n, c in enumerate(chunks):
                            w = (min(c + 4, i + 1) - c) * P
                            act.wait_ge(*at(turned, it, 2 * h + (n + 1) * (2 // len(chunks))))
                            act.activation(pT[:, par, h, c * P:c * P + w], TR[turned_bank(h, n, len(chunks))][:, 0:w],
                                           ACT.Copy).then_inc(pT_in, 2 // len(chunks))
                    return do

                pipeline(act, b * UNITS, UNITS, U, [
                    (9, take_pT(0)), (8, exps(0)), (0, take_projection), (9, take_pT(1)), (8, exps(1))])

        @block.vector
        def _(dve):
            seed(dve, [masked, maxed, inverted, scaled, o_in])
            dve.sem_inc(out_in, 1)
            with dve.Fori(0, B, 1) as b:
                dve.wait_ge(out_in, b * TPB + 1)
                dve.sem_inc(held, 1)
                dve.tensor_copy(x_b[:], xn[:, bass.ds(b * TPB, TPB), :]).then_inc(x_copied, 1)

                def mask_and_max(h):
                    def do(it):
                        i, par = it.slot % QT, it.slot % 2
                        w = (i + 1) * P
                        dve.wait_ge(*at(scored, it, h + 1))
                        dve.tensor_tensor(S[h][:, w - P:w], S[h][:, w - P:w], causal[:], ALU.add).then_inc(masked, 1)
                        dve.wait_ge(*at(masked, it, h + 1))
                        dve.wait_ge(*at(exped, it, h + 1, 2))
                        dve.tensor_reduce(nmax[:, par, h:h + 1], S[h][:, 0:w], AX.X, ALU.max, negate=True).then_inc(maxed, 1)
                    return do

                def scale(h):
                    def do(it):
                        par, w = it.slot % 2, (it.slot % QT + 1) * P
                        dve.wait_ge(*at(exped, it, h + 1))
                        dve.reciprocal(rinv[:, par, h:h + 1], rsum[:, par, h:h + 1]).then_inc(inverted, 1)
                        dve.wait_ge(*at(inverted, it, h + 1))
                        p = probs[:, par, h, 0:w]
                        dve.tensor_scalar(p, p, rinv[:, par, h:h + 1], None, ALU.mult).then_inc(scaled, 1)
                    return do

                def take_o(it):
                    i = it.slot % QT
                    dve.wait_ge(*at(attended, it, 1))
                    dve.sem_inc(held, 1)
                    pair = it.turn * 2 + it.slot // QT
                    dve.tensor_copy(oT[:, bass.ds(pair, 1), i * P:(i + 1) * P], OB[:, 0:P].unsqueeze(1)).then_inc(o_in, 1)

                pipeline(dve, b * UNITS, UNITS, U, [
                    (8, mask_and_max(0)), (8, mask_and_max(1)), (8, scale(0)), (8, scale(1)), (10, take_o)])
                for i in range(TPB):
                    dve.wait_ge(out_done, b * TPB + i + 1)
                    dve.sem_inc(held, 1)
                    dve.tensor_copy(z[:, bass.ds(b * TPB + i, 1), :], [OB, PB][i % 2][:, 0:C].unsqueeze(1)).then_inc(out_in, 1)
            dve.wait_ge(out_in, B * TPB + 1)


def routed_block(nc, A, xn, z, ident, psum, scratch):
    H, D, F = 16, 8, 512
    S = 512
    KEPT = 127
    MAGIC = 12582912.0
    INV_2PI = 0.15915494309189535
    C1, C2, C3 = 6.28125, 1.93500518798828125e-3, 3.0199159819e-7
    PI = 3.14159250259399414
    HALF_PI = 1.57079632679489662
    with ExitStack() as ctx:
        def sb(name, shape, dt=F32):
            return ctx.enter_context(nc.sbuf_tensor("m_" + name, shape, dt))

        def sem(name):
            return ctx.enter_context(nc.semaphore("m_" + name))

        XC = P + 2
        router = sb("router", [P, C])
        router_b = sb("router_b", [P, 1])
        products = sb("products", [P, NT, C])
        weights = sb("weights", [P, NT])
        weights_t = sb("weights_t", [NT, P])
        w_row = sb("w_row", [P, 2, T])
        from_here = sb("from_here", [P, 2 * T - P])
        junk = sb("junk", [P, 2, T])
        slots_sign = sb("slots_sign", [P, 2])
        at_least, ties, rank = sb("at_least", [P, NT]), sb("ties", [P, NT]), sb("rank", [P, NT])
        unselected = sb("unselected", [P, NT])
        slots = sb("slots", [P, P])
        pos_i = sb("pos_i", [P, B, TPB], I32)
        x_b = sb("x_b", [P, TPB, XC])
        one_hot = sb("one_hot", [P, TPB, P])
        one_hot_T = sb("one_hot_T", [P, TPB, P])
        last_row = sb("last_row", [P, 2, P])
        clamped = sb("clamped", [P, P])
        mask = sb("mask", [P, S // P, S])
        mask_rows = sb("mask_rows", [P, S // P, P])
        spare = sb("spare", [P, P])
        mask_sel = sb("mask_sel", [P, P])
        w_qkv, w_o, w_1, w_2 = sb("w_qkv", [P, 3 * P]), sb("w_o", [P, P]), sb("w_1", [P, F]), sb("w_2", [P, 4, P])
        ln = sb("ln", [P, 2, C])
        head_cols = sb("head_cols", [P, H])
        inv_freq = sb("inv_freq", [P, 4])
        minus_half = sb("minus_half", [P, 1])
        x_sel = sb("x_sel", [P, XC])
        sq = sb("sq", [P, C])
        ssum = sb("ssum", [P, 1])
        rms = sb("rms", [P, 1])
        hn = sb("hn", [P, C])
        hT = sb("hT", [P, P])
        ang, turns = sb("ang", [P, 4]), sb("turns", [P, 4])
        sincos_in, over, sincos = sb("sincos_in", [P, 2, 4]), sb("over", [P, 2, 4]), sb("sincos", [P, 2, 4])
        sin2 = sb("sin2", [P, 2, 4])
        qk_a, qk_b = sb("qk_a", [P, 2 * P]), sb("qk_b", [P, 2 * P])
        v = sb("v", [P, P])
        qT = sb("qT", [P, P])
        k_heads = sb("k_heads", [P, H, P])
        s = sb("s", [P, H, P])
        mx, sm = sb("mx", [P, H]), sb("sm", [P, H])
        pT = sb("pT", [P, H, P])
        o = sb("o", [P, P])
        oT = sb("oT", [P, P])
        x1, x2 = sb("x1", [P, C]), sb("x2", [P, C])
        hid = sb("hid", [P, 4, P])

        def bank(n, m=1):
            return psum[:, n:n + m, :].rearrange("p a n -> p (a n)")

        loaded, held, mask_in, stored = sem("loaded"), sem("held"), sem("mask_in"), sem("stored")
        row_in = [sem("even_row_in"), sem("odd_row_in")]
        batch_kept = sem("batch_kept")
        prepared, turned_w, copied_w, rank_step, batch_done = (
            sem("prepared"), sem("turned_w"), sem("copied_w"), sem("rank_step"), sem("batch_done"))

        class Steps:

            def __init__(self, name, names):
                self.sem, self.names, self.given = sem(name), names.split(), 0

            def done(self, ins, name):
                assert self.names[self.given % len(self.names)] == name, name
                self.given += 1
                ins.then_inc(self.sem, 1)

            def reached(self, b, name):
                return self.sem, b * len(self.names) + self.names.index(name) + 1

        pe_steps = Steps("pe_steps", """gathered one_hot_turned clamped_row mask_rows mask_selected normed_turned qkv
            qk_turned scores probs_turned attended o_turned projected normed2_turned hidden mlp scattered""")
        act_steps = Steps("act_steps", """one_hot_T clamped mask_rows hT sin qT v exps pT oT hT2 gelu""")
        dve_steps = Steps("dve_steps", """one_hot x_in pos_in w_in x_sel sq ssum rms_in hn
            ang turns turns2 turns3 r1 r2 r3 r4 r5 over wrapped clamp sin2 mask_sel qk_b qk_a qk k_heads
            s mx shifted sm rsm o x1 sq2 ssum2 rms_in2 hn2 x2 x2w""")
        pool_steps = Steps("pool_steps", "rms rms2")

        block = ctx.enter_context(nc.Block())

        @block.sync
        def _(sp):
            sp.dma_start(router[:], A["router_w"].rearrange("c o -> (o c)").partition_broadcast(P)).then_inc(loaded, 16)
            sp.dma_start(router_b[:], A["router_b"].partition_broadcast(P)).then_inc(loaded, 16)
            sp.dma_start(from_here[:], A["from_here"]).then_inc(loaded, 16)
            sp.dma_start(slots[:], A["slots"]).then_inc(loaded, 16)
            sp.dma_start(last_row[:], A["last_row"]).then_inc(loaded, 16)
            sp.dma_start(spare[:], A["spare"]).then_inc(loaded, 16)
            sp.dma_start(slots_sign[:], A["halves_sign"]).then_inc(loaded, 16)
            sp.dma_start(head_cols[:], A["head_cols"]).then_inc(loaded, 16)
            sp.dma_start(inv_freq[:], A["inv_freq"]).then_inc(loaded, 16)
            for n in range(3):
                sp.dma_start(w_qkv[:, n * P:(n + 1) * P], A[["wq", "wk", "wv"][n]]).then_inc(loaded, 16)
            sp.dma_start(w_o[:], A["wo"]).then_inc(loaded, 16)
            sp.dma_start(w_1[:], A["w1"]).then_inc(loaded, 16)
            sp.dma_start(w_2[:], A["w2"].rearrange("(h p) c -> p h c", p=P)).then_inc(loaded, 16)
            sp.dma_start(ln[:, 0, :], A["ln1"].partition_broadcast(P)).then_inc(loaded, 16)
            sp.dma_start(ln[:, 1, :], A["ln2"].partition_broadcast(P)).then_inc(loaded, 16)
            sp.dma_start(pos_i[:], A["pos"]).then_inc(loaded, 16)
            sp.wait_ge(copied_w, 1)
            sp.dma_start(scratch, weights_t[:]).then_inc(stored, 16)
            sp.wait_ge(stored, 16)
            rows = scratch.rearrange("(b t) p -> b (t p)", b=B)
            for b in range(B):
                if b >= 2:
                    sp.wait_ge(rank_step, (b - 1) * 2 * TPB)
                sp.dma_start(w_row[:, b % 2, :], rows[b].partition_broadcast(P)).then_inc(row_in[b % 2], 16)
            with sp.Fori(0, B, 1) as b:
                sp.wait_ge(batch_done, b + 1)
                sp.dma_start(mask[:], A["attention_mask"][bass.ds(b, 1)].rearrange("b o (t p) k -> p (b o t) k", p=P)
                             ).then_inc(mask_in, 16)

        LOADED = 16 * 18

        @block.gpsimd
        def _(pool):
            pool.wait_ge(prepared, 2)
            with pool.Fori(0, B, 1) as b:
                pool.wait_ge(*dve_steps.reached(b, "rms_in"))
                pool_steps.done(pool.tensor_tensor(rms[:], ssum[:], minus_half[:], ALU.pow), "rms")
                pool.wait_ge(*dve_steps.reached(b, "rms_in2"))
                pool_steps.done(pool.tensor_tensor(rms[:], ssum[:], minus_half[:], ALU.pow), "rms2")

        @block.tensor
        def _(pe):
            pe.wait_ge(loaded, LOADED)
            pe.wait_ge(prepared, 5)
            pe.transpose(bank(0)[0:NT, 0:P], weights[:], ident[:]).then_inc(turned_w, 1)
            with pe.Fori(0, B, 1) as b:
                def after(steps, name):
                    pe.wait_ge(*steps.reached(b, name))

                after(dve_steps, "w_in")
                for t in range(TPB):
                    m = pe.matmul(bank(0)[:, 0:XC], one_hot[:, t, :], x_b[:, t, :], start=(t == 0), stop=(t == TPB - 1))
                pe_steps.done(m, "gathered")
                for t in range(TPB):
                    m = pe.transpose(bank(1 + t // 4)[:, (t % 4) * P:(t % 4 + 1) * P], one_hot[:, t, :], ident[:])
                pe_steps.done(m, "one_hot_turned")
                for t in range(3, TPB):
                    m = pe.matmul(bank(3)[:, 0:P], last_row[:, min(t - 3, 1), :], one_hot[:, t, :],
                                  start=(t == 3), stop=(t == TPB - 1))
                pe_steps.done(m, "clamped_row")
                pe.wait_ge(mask_in, b * 16 + 16)
                after(act_steps, "clamped")
                for k in range(4):
                    for t in range(4):
                        m = pe.matmul(bank(4)[:, k * P:(k + 1) * P], mask[:, t, k * P:(k + 1) * P],
                                      one_hot[:, t, :] if t < 3 else clamped[:], start=(t == 0), stop=(t == 3))
                pe_steps.done(m, "mask_rows")
                after(act_steps, "mask_rows")
                for k in range(4):
                    m = pe.matmul(bank(5)[:, 0:P], mask_rows[:, k, :], one_hot[:, k, :] if k < 3 else clamped[:],
                                  start=(k == 0), stop=(k == 3))
                pe_steps.done(m, "mask_selected")
                after(dve_steps, "hn")
                pe_steps.done(pe.transpose(bank(0)[:, 0:P], hn[:], ident[:]), "normed_turned")
                after(act_steps, "hT")
                pe_steps.done(pe.matmul(bank(1)[:, 0:3 * P], hT[:], w_qkv[:], start=True, stop=True), "qkv")
                after(dve_steps, "qk")
                pe.transpose(bank(2)[:, 0:P], qk_a[:, 0:P], ident[:])
                pe_steps.done(pe.transpose(bank(3)[:, 0:P], qk_a[:, P:2 * P], ident[:]), "qk_turned")
                after(dve_steps, "k_heads")
                after(act_steps, "qT")
                for g in range(4):
                    m = pe.matmul(bank(4 + g), qT[:], k_heads[:, 4 * g:4 * g + 4, :].rearrange("p h k -> p (h k)"),
                                  start=True, stop=True)
                pe_steps.done(m, "scores")
                after(act_steps, "exps")
                after(act_steps, "v")
                for h in range(H):
                    m = pe.transpose(bank(h // 4)[:, (h % 4) * P:(h % 4 + 1) * P], s[:, h, :], ident[:])
                pe_steps.done(m, "probs_turned")
                after(act_steps, "pT")
                for h in range(H):
                    m = pe.matmul(bank(4)[:, D * h:D * h + D], pT[:, h, :], v[:, D * h:D * h + D], start=True, stop=True)
                pe_steps.done(m, "attended")
                after(dve_steps, "o")
                pe_steps.done(pe.transpose(bank(5)[:, 0:P], o[:], ident[:]), "o_turned")
                after(act_steps, "oT")
                pe_steps.done(pe.matmul(bank(6)[:, 0:C], oT[:], w_o[:], start=True, stop=True), "projected")
                after(dve_steps, "hn2")
                pe_steps.done(pe.transpose(bank(0)[:, 0:P], hn[:], ident[:]), "normed2_turned")
                after(act_steps, "hT2")
                for f in range(4):
                    m = pe.matmul(bank(1)[:, f * P:(f + 1) * P], w_1[:, f * P:(f + 1) * P], hT[:], start=True, stop=True)
                pe_steps.done(m, "hidden")
                after(act_steps, "gelu")
                for f in range(4):
                    m = pe.matmul(bank(2)[:, 0:C], hid[:, f, :], w_2[:, f, :], start=(f == 0), stop=(f == 3))
                pe_steps.done(m, "mlp")
                after(dve_steps, "x2w")
                for t in range(TPB):
                    m = pe.matmul(bank(3 + t // 4)[:, (t % 4) * P:(t % 4 + 1) * P], one_hot_T[:, t, :], x2[:],
                                  start=True, stop=True)
                pe_steps.done(m, "scattered")

        @block.scalar
        def _(act):
            act.wait_ge(turned_w, 1)
            act.activation(weights_t[:], bank(0)[0:NT, 0:P], ACT.Copy).then_inc(copied_w, 1)
            act.wait_ge(loaded, LOADED)
            with act.Fori(0, B, 1) as b:
                def after(steps, name):
                    act.wait_ge(*steps.reached(b, name))

                act.wait_ge(batch_done, b + 1)
                after(pe_steps, "one_hot_turned")
                act_steps.done(act.activation(one_hot_T[:].rearrange("p t n -> p (t n)"), bank(1, 2), ACT.Copy), "one_hot_T")
                after(pe_steps, "clamped_row")
                act_steps.done(act.activation(clamped[:], bank(3)[:, 0:P], ACT.Copy), "clamped")
                after(pe_steps, "mask_rows")
                act_steps.done(act.activation(mask_rows[:].rearrange("p t n -> p (t n)"), bank(4), ACT.Copy), "mask_rows")
                after(pe_steps, "normed_turned")
                act_steps.done(act.activation(hT[:], bank(0)[:, 0:P], ACT.Copy), "hT")
                after(dve_steps, "clamp")
                act_steps.done(act.activation(sincos[:], sincos_in[:], ACT.Sin), "sin")
                after(pe_steps, "qk_turned")
                act_steps.done(act.activation(qT[:], bank(2)[:, 0:P], ACT.Copy, scale=float(D) ** -0.5), "qT")
                after(dve_steps, "qk")
                act_steps.done(act.activation(v[:], bank(1)[:, 2 * P:3 * P], ACT.Copy), "v")
                after(dve_steps, "shifted")
                act_steps.done(act.activation(s[:], s[:], ACT.Exp), "exps")
                after(pe_steps, "probs_turned")
                act_steps.done(act.activation(pT[:].rearrange("p h n -> p (h n)"), bank(0, 4), ACT.Copy), "pT")
                after(pe_steps, "o_turned")
                act_steps.done(act.activation(oT[:], bank(5)[:, 0:P], ACT.Copy), "oT")
                after(pe_steps, "normed2_turned")
                act_steps.done(act.activation(hT[:], bank(0)[:, 0:P], ACT.Copy), "hT2")
                after(pe_steps, "hidden")
                act_steps.done(act.activation(hid[:].rearrange("p f n -> p (f n)"), bank(1), ACT.Gelu_apprx_tanh), "gelu")

        @block.vector
        def _(dve):
            dve.memset(minus_half[:], -0.5).then_inc(prepared, 1)
            dve.sem_inc(prepared, 1)
            dve.sem_inc(batch_done, 1)
            dve.wait_ge(loaded, LOADED)
            dve.tensor_tensor(products[:], xn[:], router[:].unsqueeze(1).to_broadcast([P, NT, C]), ALU.mult).then_inc(prepared, 1)
            dve.wait_ge(prepared, 3)
            dve.tensor_reduce(weights[:], products[:], AX.X, ALU.add).then_inc(prepared, 1)
            dve.wait_ge(prepared, 4)
            dve.tensor_scalar(weights[:], weights[:], router_b[:], None, ALU.add).then_inc(prepared, 1)
            dve.wait_ge(prepared, 5)
            for b in range(B):
                dve.wait_ge(row_in[b % 2], 16 * (b // 2 + 1))
                for t in range(TPB):
                    n = b * TPB + t
                    if n:
                        dve.wait_ge(rank_step, 2 * n)
                    w = weights[:, n:n + 1]
                    dve.tensor_scalar(junk[:, 0, :], w_row[:, b % 2, :], w, None, ALU.is_ge, ALU.add,
                                      accum_out=at_least[:, n:n + 1]).then_inc(rank_step, 1)
                    off = T - P - t * P
                    dve.scalar_tensor_tensor(out=junk[:, 1, :], in0=w_row[:, b % 2, :], scalar=w,
                                             in1=from_here[:, off:off + T], op0=ALU.is_equal, op1=ALU.mult,
                                             accum_out=ties[:, n:n + 1]).then_inc(rank_step, 1)
            dve.wait_ge(rank_step, 2 * NT)
            dve.tensor_tensor(rank[:], at_least[:], ties[:], ALU.subtract).then_inc(prepared, 1)
            dve.tensor_scalar(unselected[:], at_least[:], float(KEPT) + 0.5, None, ALU.is_gt).then_inc(prepared, 1)
            dve.wait_ge(prepared, 7)
            with dve.Fori(0, B, 1) as b:
                tiles = bass.ds(b * TPB, TPB)

                def after(steps, name):
                    dve.wait_ge(*steps.reached(b, name))

                def step(name, ins):
                    dve_steps.done(ins, name)

                def then(name, ins):
                    dve_steps.done(ins, name)
                    after(dve_steps, name)

                dve.wait_ge(batch_done, b + 1)
                dve.sem_inc(held, 1)
                step("one_hot", dve.tensor_tensor(one_hot[:], slots[:].unsqueeze(1).to_broadcast([P, TPB, P]),
                                                  rank[:, tiles].unsqueeze(2).to_broadcast([P, TPB, P]), ALU.is_equal))
                step("x_in", dve.tensor_copy(x_b[:, :, 0:C], xn[:, tiles, :]))
                step("pos_in", dve.tensor_copy(x_b[:, :, C:C + 1], pos_i[:, bass.ds(b, 1), :].rearrange("p o (t a) -> p (o t) a", a=1)))
                step("w_in", dve.tensor_copy(x_b[:, :, C + 1:C + 2], weights[:, tiles].unsqueeze(2)))
                after(pe_steps, "gathered")
                then("x_sel", dve.tensor_copy(x_sel[:], bank(0)[:, 0:XC]))
                x = x_sel[:, 0:C]

                def rmsnorm(x, gain, n):
                    then("sq" + n, dve.tensor_tensor(sq[:], x, x, ALU.mult))
                    then("ssum" + n, dve.tensor_reduce(ssum[:], sq[:], AX.X, ALU.add))
                    step("rms_in" + n, dve.tensor_scalar(ssum[:], ssum[:], 1.0 / C, 1e-6, ALU.mult, ALU.add))
                    after(pool_steps, "rms" + n)
                    step("hn" + n, dve.scalar_tensor_tensor(out=hn[:], in0=x, scalar=rms[:], in1=gain, op0=ALU.mult, op1=ALU.mult))

                rmsnorm(x, ln[:, 0, :], "")
                r = sincos_in[:, 0, :]
                then("ang", dve.tensor_scalar(ang[:], inv_freq[:], x_sel[:, C:C + 1], None, ALU.mult))
                then("turns", dve.tensor_scalar(turns[:], ang[:], INV_2PI, None, ALU.mult))
                then("turns2", dve.tensor_scalar(turns[:], turns[:], MAGIC, None, ALU.add))
                then("turns3", dve.tensor_scalar(turns[:], turns[:], -MAGIC, None, ALU.add))
                then("r1", dve.scalar_tensor_tensor(out=r, in0=turns[:], scalar=-C1, in1=ang[:], op0=ALU.mult, op1=ALU.add))
                then("r2", dve.scalar_tensor_tensor(out=r, in0=turns[:], scalar=-C2, in1=r, op0=ALU.mult, op1=ALU.add))
                then("r3", dve.scalar_tensor_tensor(out=r, in0=turns[:], scalar=-C3, in1=r, op0=ALU.mult, op1=ALU.add))
                then("r4", dve.tensor_scalar(sincos_in[:, 1, :], r, HALF_PI, None, ALU.add))
                then("r5", dve.tensor_scalar(over[:], sincos_in[:], PI, None, ALU.is_gt))
                then("over", dve.scalar_tensor_tensor(out=sincos_in[:], in0=over[:], scalar=-C1, in1=sincos_in[:],
                                                      op0=ALU.mult, op1=ALU.add))
                then("wrapped", dve.scalar_tensor_tensor(out=sincos_in[:], in0=over[:], scalar=-(C2 + C3), in1=sincos_in[:],
                                                         op0=ALU.mult, op1=ALU.add))
                step("clamp", dve.tensor_scalar(sincos_in[:], sincos_in[:], -PI, PI, ALU.max, ALU.min))
                after(act_steps, "sin")
                then("sin2", dve.tensor_tensor(sin2[:], sincos[:, 0:1, :].to_broadcast([P, 2, 4]),
                                               slots_sign[:].unsqueeze(2).to_broadcast([P, 2, 4]), ALU.mult))
                after(pe_steps, "mask_selected")
                step("mask_sel", dve.tensor_tensor(mask_sel[:], bank(5)[:, 0:P], spare[:], ALU.add))
                after(pe_steps, "qkv")
                qkv = bank(1)[:, 0:2 * P].rearrange("p (h r d) -> p h r d", r=2, d=4)
                step("qk_b", dve.tensor_tensor(qk_b[:].rearrange("p (h r d) -> p h r d", r=2, d=4), qkv[:, :, ::-1, :],
                                               sin2[:].unsqueeze(1).to_broadcast([P, 2 * H, 2, 4]), ALU.mult))
                then("qk_a", dve.tensor_tensor(qk_a[:].rearrange("p (h r d) -> p h r d", r=2, d=4), qkv,
                                               sincos[:, 1:2, :].unsqueeze(1).to_broadcast([P, 2 * H, 2, 4]), ALU.mult))
                step("qk", dve.tensor_tensor(qk_a[:], qk_a[:], qk_b[:], ALU.add))
                after(pe_steps, "qk_turned")
                step("k_heads", dve.tensor_tensor(k_heads[:], bank(3)[:, 0:P].unsqueeze(1).to_broadcast([P, H, P]),
                                                  head_cols[:].unsqueeze(2).to_broadcast([P, H, P]), ALU.mult))
                after(pe_steps, "scores")
                then("s", dve.tensor_tensor(s[:], bank(4, 4).rearrange("p (h k) -> p h k", h=H),
                                            mask_sel[:].unsqueeze(1).to_broadcast([P, H, P]), ALU.add))
                then("mx", dve.tensor_reduce(mx[:], s[:], AX.X, ALU.max))
                step("shifted", dve.tensor_tensor(s[:], s[:], mx[:].unsqueeze(2).to_broadcast([P, H, P]), ALU.subtract))
                after(act_steps, "exps")
                then("sm", dve.tensor_reduce(sm[:], s[:], AX.X, ALU.add))
                then("rsm", dve.reciprocal(sm[:], sm[:]))
                after(pe_steps, "attended")
                step("o", dve.tensor_tensor(o[:].rearrange("p (h d) -> p h d", h=H),
                                            bank(4)[:, 0:P].rearrange("p (h d) -> p h d", h=H),
                                            sm[:].unsqueeze(2).to_broadcast([P, H, D]), ALU.mult))
                after(pe_steps, "projected")
                then("x1", dve.tensor_tensor(x1[:], bank(6)[:, 0:C], x, ALU.add))
                rmsnorm(x1[:], ln[:, 1, :], "2")
                after(pe_steps, "mlp")
                then("x2", dve.tensor_tensor(x2[:], bank(2)[:, 0:C], x1[:], ALU.add))
                step("x2w", dve.tensor_scalar(x2[:], x2[:], x_sel[:, C + 1:C + 2], None, ALU.mult))
                dve.wait_ge(*pe_steps.reached(b, "gathered"))
                dve.sem_inc(held, 1)
                dve.tensor_tensor(z[:, tiles, :], x_b[:, :, 0:C],
                                  unselected[:, tiles].unsqueeze(2).to_broadcast([P, TPB, C]), ALU.mult).then_inc(batch_kept, 1)
                dve.wait_ge(batch_kept, b + 1)
                after(pe_steps, "scattered")
                dve.tensor_tensor(z[:, tiles, :], z[:, tiles, :], bank(3, 2).rearrange("p (t c) -> p t c", c=C),
                                  ALU.add).then_inc(batch_done, 1)


def linear_attention(nc, A, xn, z, ident, psum):
    H, D, U = 16, 8, TPB
    NORM = float(D) ** -0.25
    FEAT_EPS, DEN_EPS = 1e-6, 1e-6
    with ExitStack() as ctx:
        def sb(name, shape):
            return ctx.enter_context(nc.sbuf_tensor("l_" + name, shape, F32))

        def sem(name):
            return ctx.enter_context(nc.semaphore("l_" + name))

        wT = sb("wT", [P, 4, P])
        feat = sb("feat", [P, P])
        head_cols = sb("head_cols", [P, H])
        block_mask = sb("block_mask", [P, P])
        bias_cols = sb("bias_cols", [P, 2])
        bias_rows = sb("bias_rows", [P, 2, P])
        bias_norm = sb("bias_norm", [P, 2])
        x_in = sb("x_in", [P, 2, C])
        xT = sb("xT", [P, 2, P])
        q_s, k_s = sb("q_s", [P, 2, P]), sb("k_s", [P, 2, P])
        v_s = sb("v_s", [P, 2, P + 1])
        q_feat = sb("q_feat", [P, U, P])
        k_feat = sb("k_feat", [P, 2, P])
        kv = sb("kv", [P, P + H])
        ksum = sb("ksum", [P, 1])
        den = sb("den", [P, H])
        rden = sb("rden", [P, H])
        o_s = sb("o_s", [P, 2, P])
        oT = sb("oT", [P, 2, P])

        XB, QB, KB, VB, FBK, KVB, NB, OB = [psum[:, n, :] for n in range(8)]

        loaded, held, ready = sem("loaded"), sem("held"), sem("ready")
        x_turned, qkv_done, feat_done, kv_done, num_done, out_done = (
            sem("x_turned"), sem("qkv_done"), sem("feat_done"), sem("kv_done"), sem("num_done"), sem("out_done"))
        act_a, act_b = sem("act_a"), sem("act_b")
        z_in = sem("z_in")
        v_in, feat_in, dve_kv, dve_b = sem("v_in"), sem("feat_in"), sem("dve_kv"), sem("dve_b")
        staged = sem("staged")
        PER = {x_turned: 1, qkv_done: 3, feat_done: 2, kv_done: 1, num_done: 1, out_done: 2, act_a: 3, act_b: 1, v_in: 1, feat_in: 2, dve_b: 3, z_in: 1, staged: 1}

        def at(s, it, k, back=0):
            return s, reached(it, PER[s], k, back, 2 * SEED)

        def seed(eng, sems):
            for s in sems:
                eng.sem_inc(s, PER[s] * 2 * SEED)

        block = ctx.enter_context(nc.Block())

        @block.sync
        def _(sp):
            sp.dma_start(wT[:], A["la_wT"]).then_inc(loaded, 16)
            sp.dma_start(bias_cols[:], A["la_bias_cols"]).then_inc(loaded, 16)
            sp.dma_start(bias_rows[:], A["la_bias_rows"].partition_broadcast(P)).then_inc(loaded, 16)
            sp.dma_start(head_cols[:], A["head_cols"]).then_inc(loaded, 16)
            sp.dma_start(block_mask[:], A["head_blocks"]).then_inc(loaded, 16)
            sp.wait_ge(ready, 1)
            for h in range(H):
                sp.dma_start(feat[D * h:D * h + D, D * h:D * h + D], A["la_PT"]).then_inc(loaded, 16)

        @block.gpsimd
        def _(pool):
            seed(pool, [staged])

            def stage(it):
                pool.wait_ge(*at(x_turned, it, 1, 2))
                pool.sem_inc(held, 1)
                pool.tensor_copy(x_in[:, it.slot % 2, :].unsqueeze(1), xn[:, bass.ds(it.t, 1), :]).then_inc(staged, 1)
            pipeline(pool, 0, NT, U, [(0, stage)])

        @block.tensor
        def _(pe):
            seed(pe, [x_turned, qkv_done, feat_done, kv_done, num_done, out_done])
            pe.wait_ge(loaded, 80 + 16 * H)
            pe.wait_ge(ready, 4)

            def turn_x(it):
                u = it.slot % 2
                pe.wait_ge(*at(staged, it, 1))
                pe.wait_ge(*at(act_a, it, 1, 1))
                pe.transpose(XB[:, 0:P], x_in[:, u, :], ident[:]).then_inc(x_turned, 1)

            def qkv(it):
                u = it.slot % 2
                pe.wait_ge(*at(act_a, it, 1))
                pe.wait_ge(*at(act_a, it, 3, 1))
                pe.wait_ge(*at(v_in, it, 1, 1))
                pe.matmul(QB[:, 0:P], wT[:, 0, :], xT[:, u, :], start=True, stop=True).then_inc(qkv_done, 1)
                pe.matmul(KB[:, 0:P], wT[:, 1, :], xT[:, u, :], start=True, stop=True).then_inc(qkv_done, 1)
                pe.matmul(VB[:, 0:P], xT[:, u, :], wT[:, 2, :], start=True, stop=True).then_inc(qkv_done, 1)

            def features(it):
                u = it.slot % 2
                pe.wait_ge(*at(feat_in, it, 2, 1))
                pe.wait_ge(*at(act_a, it, 3))
                pe.matmul(FBK[:, 0:P], feat[:], q_s[:, u, :], start=True, stop=True).then_inc(feat_done, 1)
                pe.matmul(FBK[:, P:2 * P], k_s[:, u, :], feat[:], start=True, stop=True).then_inc(feat_done, 1)

            def sum_kv(it):
                u = it.slot % 2
                pe.wait_ge(*at(feat_in, it, 2))
                if it.slot == 0:
                    pe.wait_ge(dve_kv, (it.turn + 1) * 3)
                pe.matmul(KVB[:, 0:P + 1], k_feat[:, u, :], v_s[:, u, :], start=(it.slot == 0),
                          stop=(it.slot == U - 1)).then_inc(kv_done, 1)

            def numerators(it):
                if it.slot == 0:
                    pe.wait_ge(dve_kv, (it.turn + 2) * 3)
                pe.wait_ge(*at(dve_b, it, 3, 1))
                pe.matmul(NB[:, 0:P + H], q_feat[:, it.slot, :], kv[:], start=True, stop=True).then_inc(num_done, 1)

            def turn_o(it):
                u = it.slot % 2
                pe.wait_ge(*at(dve_b, it, 3))
                pe.wait_ge(*at(z_in, it, 1, 1))
                pe.transpose(OB[:, 0:P], o_s[:, u, :], ident[:]).then_inc(out_done, 1)

            def project(it):
                pe.wait_ge(*at(act_b, it, 1))
                pe.matmul(OB[:, 0:P], oT[:, it.slot % 2, :], wT[:, 3, :], start=True, stop=True).then_inc(out_done, 1)

            pipeline(pe, 0, NT, U, [(9, numerators), (0, turn_x), (10, turn_o), (1, features), (0, qkv),
                                    (1, sum_kv), (10, project)])

        @block.scalar
        def _(act):
            seed(act, [act_a, act_b])
            act.wait_ge(loaded, 80 + 16 * H)
            act.activation(bias_norm[:], bias_cols[:], ACT.Copy, scale=NORM).then_inc(ready, 1)
            act.wait_ge(ready, 4)

            def take_x(it):
                act.wait_ge(*at(x_turned, it, 1))
                act.wait_ge(*at(qkv_done, it, 3, 2))
                act.activation(xT[:, it.slot % 2, :], XB[:, 0:P], ACT.Copy).then_inc(act_a, 1)

            def take_qk(it):
                u = it.slot % 2
                act.wait_ge(*at(feat_done, it, 2, 2))
                act.wait_ge(*at(qkv_done, it, 1))
                act.activation(q_s[:, u, :], QB[:, 0:P], ACT.Identity, scale=NORM, bias=bias_norm[:, 0:1]).then_inc(act_a, 1)
                act.wait_ge(*at(qkv_done, it, 2))
                act.activation(k_s[:, u, :], KB[:, 0:P], ACT.Identity, scale=NORM, bias=bias_norm[:, 1:2]).then_inc(act_a, 1)

            def take_o(it):
                act.wait_ge(*at(out_done, it, 1))
                act.wait_ge(*at(out_done, it, 2, 2))
                act.activation(oT[:, it.slot % 2, :], OB[:, 0:P], ACT.Copy).then_inc(act_b, 1)

            pipeline(act, 0, NT, U, [(0, take_x), (10, take_o), (0, take_qk)])

        @block.vector
        def _(dve):
            seed(dve, [v_in, feat_in, dve_b, z_in])
            dve.memset(feat[:], 0.0).then_inc(ready, 1)
            dve.memset(v_s[:], 1.0).then_inc(ready, 1)
            dve.sem_inc(dve_kv, 3)
            dve.wait_ge(loaded, 80 + 16 * H)
            dve.sem_inc(ready, 1)

            def take_v(it):
                u = it.slot % 2
                dve.wait_ge(*at(qkv_done, it, 3))
                dve.wait_ge(*at(kv_done, it, 1, 2))
                dve.tensor_tensor(v_s[:, u, 0:P], VB[:, 0:P], bias_rows[:, 0, :], ALU.add).then_inc(v_in, 1)

            def take_features(it):
                u = it.slot % 2
                dve.wait_ge(*at(feat_done, it, 2))
                dve.wait_ge(*at(num_done, it, 1, 8))
                dve.tensor_scalar(q_feat[:, it.slot, :], FBK[:, 0:P], 0.0, FEAT_EPS, ALU.max, ALU.add).then_inc(feat_in, 1)
                dve.wait_ge(*at(kv_done, it, 1, 2))
                dve.tensor_scalar(k_feat[:, u, :], FBK[:, P:2 * P], 0.0, FEAT_EPS, ALU.max, ALU.add).then_inc(feat_in, 1)
                if it.slot == U - 1:
                    dve.wait_ge(*at(kv_done, it, 1))
                    dve.wait_ge(*at(num_done, it, 1, 8))
                    dve.tensor_copy(ksum[:], KVB[:, P:P + 1]).then_inc(dve_kv, 1)
                    dve.tensor_tensor(kv[:, 0:P], KVB[:, 0:P], block_mask[:],
                                      ALU.mult).then_inc(dve_kv, 1)
                    dve.wait_ge(dve_kv, it.turn * 3 + 5)
                    dve.tensor_scalar(kv[:, P:P + H], head_cols[:], ksum[:], None, ALU.mult).then_inc(dve_kv, 1)

            def divide(it):
                u = it.slot % 2
                dve.wait_ge(*at(num_done, it, 1))
                dve.tensor_scalar(den[:], NB[:, P:P + H], DEN_EPS, None, ALU.add).then_inc(dve_b, 1)
                dve.wait_ge(*at(dve_b, it, 1))
                dve.reciprocal(rden[:], den[:]).then_inc(dve_b, 1)
                dve.wait_ge(*at(dve_b, it, 2))
                dve.wait_ge(*at(out_done, it, 1, 2))
                dve.tensor_tensor(o_s[:, u, :].rearrange("p (h d) -> p h d", h=H),
                                  NB[:, 0:P].rearrange("p (h d) -> p h d", h=H),
                                  rden[:].unsqueeze(2).to_broadcast([P, H, D]), ALU.mult).then_inc(dve_b, 1)

            def take_z(it):
                dve.wait_ge(*at(out_done, it, 2))
                dve.tensor_tensor(z[:, bass.ds(it.t, 1), :].rearrange("p o c -> p (o c)"), OB[:, 0:P],
                                  bias_rows[:, 1, :], ALU.add).then_inc(z_in, 1)

            pipeline(dve, 0, NT, U, [(9, divide), (1, take_features), (0, take_v), (10, take_z)])
            dve.wait_ge(*at(z_in, Item(NT), 0))


DEPTH, HEADS, HD, WIN = 6, 16, 64, 32
INNER = HEADS * HD
QKV = 3 * INNER
FF = 341
FCH = [(0, 128), (128, 128), (256, FF - 256)]
QK_SCALE = 8.0
QKV_ORDER = [0, 2, 1, 3, 4, 5]
TURN_ORDER = [0, 2, 1, 3]
RSQRT_SEED = float(0x5F3759DF - (1 << 22) - (1 << 31))


def local_transformer(nc, A, Y, ident, psum):
    U, GROUP = 8, 4
    UNITS = DEPTH * NT
    GROUPS_PER_LAYER = NT // GROUP
    with ExitStack() as ctx:
        def sb(name, shape, dt=F32):
            return ctx.enter_context(nc.sbuf_tensor(name, shape, dt))

        def sem(name):
            return ctx.enter_context(nc.semaphore(name))

        w_qkv = sb("w_qkv", [P, QKV])
        w_out = sb("w_out", [P, 8, C])
        w_up = sb("w_up", [P, 2 * FF])
        w_down = sb("w_down", [P, 3, C])
        cols = sb("cols", [P, 8])
        bias_row = sb("bias_row", [P, C])
        scales = sb("scales", [P, 4 * HD])
        rope_base = sb("rope_base", [P, TPB, 4, HD])
        rope = sb("rope", [P, 2, 4, HD])
        mask = sb("mask", [P, TPB, 2 * WIN])
        keep_carry = sb("keep_carry", [P, TPB])
        minus_half = sb("minus_half", [P, GROUP])
        y_in = sb("y_in", [P, GROUP, C])
        shifted = sb("shifted", [P, 2, GROUP * P + 1])
        squares = sb("squares", [P, 4, 512])
        rotated = sb("rotated", [P, 2, 512])
        qk = sb("qk", [P, 2, 4, 512])
        ss = sb("ss", [P, 2, 32])
        rs_a = sb("rs_a", [P, 32])
        rs_b = sb("rs_b", [P, 32])
        rs_y = sb("rs_y", [P, 2, 32])
        qT = sb("qT", [P, 8, P])
        kT = sb("kT", [P, 2, 8, WIN + P])
        V = sb("V", [P, 4, INNER])
        sc = sb("sc", [P, 2, 2, 512])
        mx = sb("mx", [P, 2, HEADS])
        sm = sb("sm", [P, 2, HEADS])
        rsum = sb("rsum", [P, 2, HEADS])
        pT = sb("pT", [P, HEADS, P])
        pT_prev = sb("pT_prev", [P, HEADS, WIN])
        oT = sb("oT", [P, 8, P])
        y1 = sb("y1", [P, 2, GROUP, C])
        f_shift = sb("f_shift", [P, 2, GROUP * P + 1])
        stats = sb("stats", [P, GROUP, 6])
        mv = sb("mv", [P, GROUP, 2])
        rstd = sb("rstd", [P, GROUP])
        veps = sb("veps", [P, GROUP])
        xn = sb("xn", [P, GROUP, C])
        xg = sb("xg", [P, GROUP * P])
        gate = sb("gate", [P, 3, GROUP * P])
        hid = sb("hid", [P, 3, GROUP * P])

        ATT = [psum[:, 0, :], psum[:, 1, :]]
        TR = psum[:, 2:4, :]
        SC = [psum[:, 4, :], psum[:, 5, :]]
        OB = psum[:, 6, :]
        FB = psum[:, 7, :]
        HID_BANKS = [SC[0], SC[1], OB]

        consts = sem("consts")
        zeroed = sem("zeroed")
        held = sem("held")
        scales_in, w_out_in, w_up_in, w_down_in, cols_in, bias_in = (
            sem("scales_in"), sem("w_out_in"), sem("w_up_in"), sem("w_down_in"), sem("cols_in"), sem("bias_in"))
        w_qkv_in = [sem(f"w_qkv_{c}_in") for c in range(6)]
        projected, qk_turned, scored = sem("projected"), sem("qk_turned"), sem("scored")
        p_turned, attended, out_projected = sem("p_turned"), sem("attended"), sem("out_projected")
        x_turned, y1_turned, shift_turned, xn_turned, gates_done, ups_done, down_done = (
            sem("x_turned"), sem("y1_turned"), sem("shift_turned"), sem("xn_turned"), sem("gates_done"),
            sem("ups_done"), sem("down_done"))
        squared, v_in, qk_in, k_prev, exped, p_spread_a, o_in = (
            sem("squared"), sem("v_in"), sem("qk_in"), sem("k_prev"), sem("exped"), sem("p_spread_a"), sem("o_in"))
        x_shifted, y1_shifted, gained, gelu_done = sem("x_shifted"), sem("y1_shifted"), sem("gained"), sem("gelu_done")
        roped, ss_done, rs_step, masked, maxed = sem("roped"), sem("ss_done"), sem("rs_step"), sem("masked"), sem("maxed")
        summed, inverted, p_spread_d, y1_done = sem("summed"), sem("inverted"), sem("p_spread_d"), sem("y1_done")
        stats_step, xn_done, gated, y_done = sem("stats_step"), sem("xn_done"), sem("gated"), sem("y_done")
        table_made, rope_added, qk_normed, shifted_max, p_scaled = (
            sem("table_made"), sem("rope_added"), sem("qk_normed"), sem("shifted_max"), sem("p_scaled"))
        staged, rstd_done, biased = sem("staged"), sem("rstd_done"), sem("biased")
        TILE_PER = {projected: 6, qk_turned: 4, scored: 2, p_turned: 1, attended: 2, out_projected: 1,
                    squared: 4, v_in: 2, qk_in: 4, k_prev: 1, exped: 2, p_spread_a: 6, o_in: 2,
                    roped: 8, ss_done: 4, rs_step: 12, masked: 2, maxed: 2, summed: 2, inverted: 2, p_spread_d: 6,
                    y1_done: 1, table_made: 1, rope_added: 4, qk_normed: 4, shifted_max: 2, p_scaled: 2}
        GROUP_PER = {x_turned: 1, y1_turned: 1, shift_turned: 1, xn_turned: 1, gates_done: 3, ups_done: 3,
                     down_done: 1, x_shifted: 3, y1_shifted: 3, gained: 1, gelu_done: 3, stats_step: 10, xn_done: 4,
                     gated: 3, y_done: 1, staged: 1, rstd_done: 1, biased: 1}
        GROUP_SEED = GROUPS_PER_LAYER + 1

        def seed(eng, sems):
            for s in sems:
                eng.sem_inc(s, TILE_PER[s] * SEED if s in TILE_PER else GROUP_PER[s] * GROUP_SEED)

        def at(s, it, k, back=0):
            return s, reached(it, TILE_PER[s], k, back)

        def at_group(s, it, k, back=0):
            return s, (it.turn * (U // GROUP) + (it.slot // GROUP + GROUP_SEED - back)) * GROUP_PER[s] + k

        def loads(s, it, per=1):
            return s, (it.t // NT + 1) * (16 * per)

        def by_group(do):
            return lambda it: do(it) if it.slot % GROUP == 0 else None

        def spread(copy, it, sub, s):
            src = TR.rearrange("p c (a q) -> p c a q", a=4)
            dst = pT[:].rearrange("p (a s c) q -> p s c a q", s=2, c=2)
            prv = pT_prev[:].rearrange("p (a s c) q -> p s c a q", s=2, c=2)
            o = 64 * sub
            args = [ACT.Copy] if s is p_spread_a else []
            for d0, d1, s0, s1, j in [(0, 64, 0, 64, 1), (64, 128, 0, 64, 3), (32, 64, 0, 32, 2), (64, 96, 32, 64, 2),
                                      (0, 32, 32, 64, 0)]:
                q = slice(32 * j, 32 * j + 32)
                copy(dst[d0:d1, sub, :, :, q], src[o + s0:o + s1, :, :, q], *args).then_inc(s, 1)
            copy(prv[96:128, sub, :, :, :], src[o:o + 32, :, :, 0:32], *args).then_inc(s, 1)

        block = ctx.enter_context(nc.Block())

        @block.sync
        def _(sp):
            def load_scales(l):
                sp.dma_start(scales[:], A["rows"][l, P:].partition_broadcast(P)).then_inc(scales_in, 16)

            def load_qkv(l, c):
                w = QKV_ORDER[c] * 512
                sp.dma_start(w_qkv[:, w:w + 512], A["Wqkv"][l, :, w:w + 512]).then_inc(w_qkv_in[c], 16)

            def load_out(l):
                sp.dma_start(w_out[:], A["Wo"][l].rearrange("(h p) c -> p h c", p=P)).then_inc(w_out_in, 16)

            def load_bias(l):
                sp.dma_start(bias_row[:], A["rows"][l, 0:P].partition_broadcast(P)).then_inc(bias_in, 16)

            def load_up(l):
                sp.dma_start(w_up[:], A["W1"][l]).then_inc(w_up_in, 16)

            def load_cols(l):
                sp.dma_start(cols[:], A["cols"][l]).then_inc(cols_in, 16)

            def load_down(l):
                sp.dma_start(w_down[:, 0:2, :], A["W2"][l, 0:256].rearrange("(h p) c -> p h c", p=P)).then_inc(w_down_in, 16)
                sp.dma_start(w_down[0:FF - 256, 2, :], A["W2"][l, 256:FF]).then_inc(w_down_in, 16)

            load_scales(0)
            sp.dma_start(rope_base[:], A["rope_base"]).then_inc(consts, 16)
            sp.dma_start(keep_carry[:], A["keep_carry"]).then_inc(consts, 16)
            sp.dma_start(mask[:], A["win_mask"]).then_inc(consts, 16)
            for c in range(6):
                load_qkv(0, c)
            load_out(0)
            load_bias(0)
            load_cols(0)
            load_up(0)
            load_down(0)
            if DEPTH == 1:
                return
            with sp.Fori(0, DEPTH - 1, 1) as l:
                nxt = Item(l * NT + NT, turn=(l + 1) * (NT // U))
                sp.wait_ge(*at(table_made, nxt, 0))
                sp.sem_inc(held, 1)
                load_scales(l + 1)
                for c in range(6):
                    sp.wait_ge(*at(projected, nxt, c + 1, 1))
                    sp.sem_inc(held, 1)
                    load_qkv(l + 1, c)
                sp.wait_ge(*at(out_projected, nxt, 0))
                sp.sem_inc(held, 1)
                load_out(l + 1)
                sp.wait_ge(*at_group(biased, nxt, 0))
                sp.sem_inc(held, 1)
                load_bias(l + 1)
                sp.wait_ge(*at_group(ups_done, nxt, 0))
                sp.sem_inc(held, 1)
                load_up(l + 1)
                sp.wait_ge(*at_group(gated, nxt, 0))
                sp.sem_inc(held, 1)
                load_cols(l + 1)
                sp.wait_ge(*at_group(down_done, nxt, 0))
                sp.sem_inc(held, 1)
                load_down(l + 1)

        @block.tensor
        def _(pe):
            seed(pe, [projected, qk_turned, scored, p_turned, attended, out_projected,
                      x_turned, y1_turned, shift_turned, xn_turned, gates_done, ups_done, down_done])

            def turn_x(it):
                pe.wait_ge(*at_group(staged, it, 1))
                pe.wait_ge(*at(y1_done, it, 1, 6))
                pe.wait_ge(*at_group(x_shifted, it, 3, 1))
                for j in range(GROUP):
                    m = pe.transpose(FB[:, j * P:(j + 1) * P], y_in[:, j, :], ident[:])
                m.then_inc(x_turned, 1)

            def project(c):
                def do(it):
                    pe.wait_ge(*loads(w_qkv_in[c], it))
                    if c == 0:
                        pe.wait_ge(*at_group(x_shifted, it, 3))
                    if c < 2:
                        pe.wait_ge(*at(v_in, it, c + 1, 1))
                    else:
                        pe.wait_ge(*at(roped, it, 2 * (c - 2) + 2))
                    w, x = QKV_ORDER[c] * 512, it.slot % GROUP * P
                    pe.matmul(ATT[c % 2], shifted[:, it.slot // GROUP, x:x + P], w_qkv[:, w:w + 512],
                              start=True, stop=True).then_inc(projected, 1)
                return do

            def turn_qk(n):
                def do(it):
                    pe.wait_ge(*at(qk_normed, it, n + 1))
                    if n < 2:
                        pe.wait_ge(*at(p_spread_a, it, 6, 2))
                        pe.wait_ge(*at(p_spread_d, it, 6, 2))
                        pe.wait_ge(*at(qk_in, it, 3 + n, 1))
                    else:
                        pe.wait_ge(*at(qk_in, it, n - 1))
                    for j in range(4):
                        m = pe.transpose(TR[:, n % 2, j * P:(j + 1) * P],
                                         qk[:, it.slot % 2, TURN_ORDER[n], j * P:(j + 1) * P], ident[:])
                    m.then_inc(qk_turned, 1)
                return do

            def score(s):
                def do(it):
                    if s == 0:
                        pe.wait_ge(*at(qk_in, it, 4))
                        pe.wait_ge(*at(k_prev, it, 1))
                    pe.wait_ge(*at(masked, it, s + 1, 1))
                    if it.slot % GROUP == 3:
                        pe.wait_ge(*at_group(gelu_done, it, s + 1, 1))
                    if it.slot % GROUP == 0:
                        pe.wait_ge(*at_group(gated, it, s + 1, 2))
                    pe.sem_inc(held, 1)
                    r = slice(64 * s, 64 * s + 64)
                    for pr in range(8):
                        for j in range(4):
                            m = pe.matmul(SC[s][32 * j:32 * j + 32, pr * 64:pr * 64 + 64],
                                          qT[r, pr, 32 * j:32 * j + 32],
                                          kT[r, it.slot % 2, pr, 32 * j:32 * j + 64],
                                          start=True, stop=True, tile_position=(64 * s, 32 * j))
                    m.then_inc(scored, 1)
                return do

            def turn_p(it):
                for c in range(2):
                    pe.wait_ge(*at(p_scaled, it, c + 1))
                    if c == 0 and it.has(1):
                        pe.wait_ge(*at(qk_in, it, 4, -1))
                    elif c == 0:
                        pe.wait_ge(*at(p_spread_a, it, 6, 1))
                        pe.wait_ge(*at(p_spread_d, it, 6, 1))
                    for j in range(4):
                        m = pe.transpose(TR[:, c, j * P:(j + 1) * P], sc[:, it.slot % 2, c, j * P:(j + 1) * P], ident[:])
                m.then_inc(p_turned, 1)

            def attend(c):
                def do(it):
                    if c == 0:
                        pe.wait_ge(*at(p_spread_a, it, 6))
                        pe.wait_ge(*at(p_spread_d, it, 6))
                        pe.wait_ge(*at(v_in, it, 2))
                        if it.slot % GROUP == 2:
                            pe.wait_ge(*at_group(gelu_done, it, 3, 1))
                        if it.slot % GROUP == 3:
                            pe.wait_ge(*at_group(gated, it, 3, 1))
                    pe.wait_ge(*at(o_in, it, c))
                    for j in range(4):
                        for par in range(2):
                            h = 8 * c + 2 * j + par
                            pe.matmul(OB[64 * par:64 * par + 64, j * P:(j + 1) * P],
                                      V[:, it.slot % 4, h * HD:(h + 1) * HD], pT[:, h, :],
                                      start=True, stop=False, tile_position=(0, 64 * par))
                        for par in range(2):
                            h = 8 * c + 2 * j + par
                            m = pe.matmul(OB[64 * par:64 * par + 64, j * P:j * P + WIN],
                                          V[96:128, (it.slot - 1) % 4, h * HD:(h + 1) * HD],
                                          pT_prev[96:128, h, :],
                                          start=False, stop=True, tile_position=(96, 64 * par))
                    m.then_inc(attended, 1)
                return do

            def project_out(it):
                pe.wait_ge(*loads(w_out_in, it))
                pe.wait_ge(*at(o_in, it, 2))
                pe.wait_ge(*at(y1_done, it, 1, 1))
                if it.slot % GROUP == 0:
                    pe.wait_ge(*at_group(y1_shifted, it, 3, 1))
                if it.slot % GROUP == 1:
                    pe.wait_ge(*at_group(gained, it, 1, 1))
                if it.slot % GROUP == 3 and it.has(5):
                    pe.wait_ge(*at_group(x_shifted, it, 3, -2))
                for j in range(8):
                    m = pe.matmul(FB[:, 0:C], oT[:, j, :], w_out[:, j, :], start=(j == 0), stop=(j == 7))
                m.then_inc(out_projected, 1)

            def turn_y1(it):
                pe.wait_ge(*at(y1_done, it, 1, -3))
                pe.wait_ge(*at_group(y_done, it, 1, 1))
                for j in range(GROUP):
                    m = pe.transpose(FB[:, j * P:(j + 1) * P], y1[:, it.slot // GROUP, j, :], ident[:])
                m.then_inc(y1_turned, 1)

            def turn_shifted(it):
                pe.wait_ge(*at_group(y1_shifted, it, 3))
                if it.has(4):
                    pe.wait_ge(*at(y1_done, it, 1, -4))
                for j in range(GROUP):
                    m = pe.transpose(FB[:, j * P:(j + 1) * P], f_shift[:, it.slot // GROUP, j * P:(j + 1) * P], ident[:])
                m.then_inc(shift_turned, 1)

            def turn_xn(it):
                pe.wait_ge(*at_group(xn_done, it, 4))
                for j in range(GROUP):
                    m = pe.transpose(FB[:, j * P:(j + 1) * P], xn[:, j, :], ident[:])
                m.then_inc(xn_turned, 1)

            def gates(it):
                pe.wait_ge(*loads(w_up_in, it))
                pe.wait_ge(*at_group(gained, it, 1))
                pe.wait_ge(*at_group(gated, it, 3, 1))
                if it.has(6):
                    pe.wait_ge(*at(masked, it, 2, -6))
                    pe.wait_ge(*at(o_in, it, 2, -5))
                for c, (f, w) in enumerate(FCH):
                    pe.matmul(HID_BANKS[c][0:w, :], w_up[:, FF + f:FF + f + w], xg[:], start=True,
                              stop=True).then_inc(gates_done, 1)

            def ups(it):
                if it.has(7):
                    pe.wait_ge(*at(masked, it, 2, -7))
                    pe.wait_ge(*at(o_in, it, 2, -6))
                for c, (f, w) in enumerate(FCH):
                    pe.wait_ge(*at_group(gelu_done, it, c + 1))
                    pe.matmul(HID_BANKS[c][0:w, :], w_up[:, f:f + w], xg[:], start=True, stop=True).then_inc(ups_done, 1)

            def down(it):
                pe.wait_ge(*loads(w_down_in, it, 2))
                if it.has(7):
                    pe.wait_ge(*at(y1_done, it, 1, -7))
                pe.wait_ge(*at_group(gated, it, 3))
                for j in range(GROUP):
                    for c, (f, w) in enumerate(FCH):
                        m = pe.matmul(FB[:, j * P:(j + 1) * P], hid[0:w, c, j * P:(j + 1) * P], w_down[0:w, c, :],
                                      start=(c == 0), stop=(c == 2))
                m.then_inc(down_done, 1)

            pe.wait_ge(zeroed, 7)
            pipeline(pe, 0, UNITS, U, [
                (6, turn_p), (5, score(0)), (5, score(1)),
                (10, by_group(turn_y1)), (3, project(2)), (3, project(3)),
                (6, attend(0)), (3, project(4)), (6, attend(1)), (11, by_group(turn_xn)), (3, project(5)), (6, project_out), (2, project(0)),
                (4, turn_qk(0)), (2, project(1)), (11, by_group(gates)), (12, by_group(ups)), (4, turn_qk(1)),
                (10, by_group(turn_shifted)), (13, by_group(down)),
                (4, turn_qk(2)), (4, turn_qk(3)), (0, by_group(turn_x))])

        @block.scalar
        def _(act):
            seed(act, [squared, v_in, qk_in, k_prev, exped, p_spread_a, o_in, x_shifted, y1_shifted, gained, gelu_done])

            def shift_in(buf, turned, read, out_sem):
                def do(it):
                    g = it.slot // GROUP
                    act.wait_ge(*at_group(turned, it, 1))
                    act.wait_ge(*read(it))
                    act.wait_ge(*at_group(out_sem, it, 3, 1))
                    act.activation(buf[0:64, g, 0:GROUP * P], FB[0:64, :], ACT.Copy).then_inc(out_sem, 1)
                    act.activation(buf[64:P, g, 1:GROUP * P + 1], FB[64:P, :], ACT.Copy).then_inc(out_sem, 1)
                    act.activation(buf[64:P, g, 0:1], buf[64:P, 1 - g, GROUP * P:GROUP * P + 1], ACT.Identity,
                                   scale=keep_carry[64:P, bass.ds(it.t % TPB, 1)]).then_inc(out_sem, 1)
                return do

            shift_x = shift_in(shifted, x_turned, lambda it: at(projected, it, 6, 5), x_shifted)
            shift_y1 = shift_in(f_shift, y1_turned, lambda it: at_group(shift_turned, it, 1, 2), y1_shifted)

            def square(c):
                def do(it):
                    act.wait_ge(*at(projected, it, c + 1))
                    act.wait_ge(*at(ss_done, it, c + 1, 1))
                    act.activation(squares[:, c, :], ATT[c % 2], ACT.Square).then_inc(squared, 1)
                return do

            def take_v(c):
                def do(it):
                    act.wait_ge(*at(projected, it, 5 + c))
                    act.wait_ge(*at(attended, it, 2, 3))
                    act.activation(V[:, it.slot % 4, 512 * c:512 * c + 512], ATT[c], ACT.Copy).then_inc(v_in, 1)
                return do

            def carry_k(it):
                b = it.slot % 2
                act.wait_ge(*at(scored, it, 2, 2))
                act.wait_ge(*at(qk_in, it, 4, 1))
                act.wait_ge(*at(k_prev, it, 1, 1))
                act.sem_inc(held, 1)
                act.activation(kT[:, b, :, 0:WIN], kT[:, 1 - b, :, P:P + WIN], ACT.Identity,
                               scale=keep_carry[:, bass.ds(it.t % TPB, 1)]).then_inc(k_prev, 1)

            def take_qk(n):
                def do(it):
                    if n == 0:
                        act.wait_ge(*at(scored, it, 2, 1))
                    act.wait_ge(*at(qk_turned, it, n + 1))
                    dst = qT[:, 4 * n:4 * n + 4, :] if n < 2 else kT[:, it.slot % 2, 4 * n - 8:4 * n - 4, WIN:]
                    act.activation(dst, TR[:, n % 2, :].rearrange("p (a q) -> p a q", a=4), ACT.Copy).then_inc(qk_in, 1)
                return do

            def exps(c):
                def do(it):
                    act.wait_ge(*at(shifted_max, it, c + 1))
                    s = sc[:, it.slot % 2, c, :]
                    act.activation(s, s, ACT.Exp).then_inc(exped, 1)
                return do

            def spread_a(it):
                act.wait_ge(*at(p_turned, it, 1))
                act.wait_ge(*at(attended, it, 2, 1))
                spread(act.activation, it, 0, p_spread_a)

            def take_o(c):
                def do(it):
                    act.wait_ge(*at(out_projected, it, 1, 1))
                    act.wait_ge(*at(attended, it, c + 1))
                    act.activation(oT[:, 4 * c:4 * c + 4, :],
                                   OB.rearrange("p (a q) -> p a q", a=4), ACT.Copy).then_inc(o_in, 1)
                return do

            def gain(it):
                act.wait_ge(*loads(cols_in, it))
                act.wait_ge(*at_group(xn_turned, it, 1))
                act.wait_ge(*at_group(ups_done, it, 3, 1))
                act.activation(xg[:], FB, ACT.Identity, scale=cols[:, 6:7], bias=cols[:, 7:8]).then_inc(gained, 1)

            def gelu(it):
                act.wait_ge(*at_group(gated, it, 3, 1))
                for c, (f, w) in enumerate(FCH):
                    act.wait_ge(*at_group(gates_done, it, c + 1))
                    act.activation(gate[0:w, c, :], HID_BANKS[c][0:w, :], ACT.Gelu,
                                   bias=cols[0:w, 3 + c:4 + c]).then_inc(gelu_done, 1)

            act.wait_ge(consts, 48)
            act.wait_ge(zeroed, 7)
            pipeline(act, 0, UNITS, U, [
                (6, spread_a), (10, by_group(shift_y1)),
                (3, square(2)), (3, square(3)), (5, exps(0)), (6, take_o(0)), (3, take_v(0)), (6, take_o(1)), (11, by_group(gain)),
                (5, exps(1)), (3, take_v(1)), (2, square(0)), (2, square(1)), (4, carry_k), (4, take_qk(0)), (4, take_qk(1)),
                (4, take_qk(2)), (4, take_qk(3)), (11, by_group(gelu)), (0, by_group(shift_x))])

        @block.vector
        def _(dve):
            seed(dve, [roped, ss_done, rs_step, masked, maxed, summed, inverted, p_spread_d, y1_done,
                       stats_step, xn_done, gated, y_done])
            for buf in (V, kT, pT, shifted, f_shift, y1):
                dve.memset(buf[:], 0.0).then_inc(zeroed, 1)
            dve.memset(minus_half[:], -0.5).then_inc(zeroed, 1)

            def rotate(c, half):
                def do(it):
                    table = rope[:, it.slot % 2, 2 * (c % 2):2 * (c % 2) + 2, :].unsqueeze(1)
                    if half == 0:
                        dve.wait_ge(*at(squared, it, c + 1))
                        if c == 0:
                            dve.wait_ge(*at(table_made, it, 1))
                            dve.wait_ge(*at(qk_turned, it, 4, 2))
                        dve.tensor_tensor(qk[:, it.slot % 2, c, :].rearrange("p (h d) -> p h d", h=8),
                                          ATT[c % 2].rearrange("p (h d) -> p h d", h=8),
                                          table[:, :, 0, :].to_broadcast([P, 8, HD]), ALU.mult).then_inc(roped, 1)
                    else:
                        dve.wait_ge(*(at(rope_added, it, c - 1) if c >= 2 else at(rope_added, it, c + 3, 1)))
                        sin = table[:, :, 1, :].to_broadcast([P, 8, HD]).rearrange("p h (r d) -> p h r d", r=2)
                        x = ATT[c % 2].rearrange("p (h r d) -> p h r d", h=8, r=2)
                        dve.tensor_tensor(rotated[:, c % 2, :].rearrange("p (h r d) -> p h r d", h=8, r=2),
                                          x[:, :, ::-1, :], sin, ALU.mult).then_inc(roped, 1)
                return do

            def sum_squares(c):
                def do(it):
                    if c == 0:
                        dve.wait_ge(*at(rs_step, it, 12, 2))
                    dve.wait_ge(*at(squared, it, c + 1))
                    dve.tensor_reduce(ss[:, it.slot % 2, 8 * c:8 * c + 8],
                                      squares[:, c, :].rearrange("p (h d) -> p h d", h=8),
                                      AX.X, ALU.add).then_inc(ss_done, 1)
                return do

            def inverse_norm(n):
                def do(it):
                    b = it.slot % 2
                    half, t, y = ss[:, b, :], rs_a[:], rs_y[:, b, :]
                    if n == 0:
                        dve.wait_ge(*at(ss_done, it, 4))
                        dve.wait_ge(*at(qk_normed, it, 4, 2))
                        i = dve.tensor_scalar(half, half, 1e-24, 0.5, ALU.max, ALU.mult)
                    else:
                        dve.wait_ge(*at(rs_step, it, n))
                        if n == 1:
                            i = dve.tensor_scalar(rs_b[:].bitcast(I32), half.bitcast(I32), 1, None, ALU.logical_shift_right)
                        elif n == 2:
                            i = dve.tensor_scalar(y.bitcast(I32), rs_b[:].bitcast(I32), -1.0, RSQRT_SEED, ALU.mult, ALU.add)
                        elif n % 3 == 0:
                            i = dve.tensor_tensor(t, y, y, ALU.mult)
                        elif n % 3 == 1:
                            i = dve.tensor_tensor(t, t, half, ALU.mult)
                        else:
                            i = dve.scalar_tensor_tensor(out=y, in0=t, scalar=-1.5, in1=y, op0=ALU.add, op1=ALU.mult)
                    i.then_inc(rs_step, 1)
                return do

            def mask_scores(c):
                def do(it):
                    dve.wait_ge(*at(scored, it, c + 1))
                    dve.wait_ge(*at(p_turned, it, 1, 2))
                    m = mask[:, bass.ds(it.t % TPB, 1), :].to_broadcast([P, 8, 2 * WIN])
                    dve.scalar_tensor_tensor(out=sc[:, it.slot % 2, c, :].rearrange("p (h k) -> p h k", h=8),
                                             in0=SC[c].rearrange("p (h k) -> p h k", h=8), scalar=QK_SCALE,
                                             in1=m, op0=ALU.mult, op1=ALU.add).then_inc(masked, 1)
                return do

            def find_max(c):
                def do(it):
                    b = it.slot % 2
                    dve.wait_ge(*at(masked, it, c + 1))
                    dve.wait_ge(*at(shifted_max, it, c + 1, 2))
                    dve.tensor_reduce(mx[:, b, 8 * c:8 * c + 8], sc[:, b, c, :].rearrange("p (h k) -> p h k", h=8),
                                      AX.X, ALU.max).then_inc(maxed, 1)
                return do

            def sum_p(c):
                def do(it):
                    b = it.slot % 2
                    dve.wait_ge(*at(exped, it, c + 1))
                    dve.tensor_reduce(sm[:, b, 8 * c:8 * c + 8], sc[:, b, c, :].rearrange("p (h k) -> p h k", h=8),
                                      AX.X, ALU.add).then_inc(summed, 1)
                return do

            def invert_sum(c):
                def do(it):
                    b, h = it.slot % 2, slice(8 * c, 8 * c + 8)
                    dve.wait_ge(*at(summed, it, c + 1))
                    dve.wait_ge(*at(p_scaled, it, c + 1, 2))
                    dve.reciprocal(rsum[:, b, h], sm[:, b, h]).then_inc(inverted, 1)
                return do

            def spread_d(it):
                dve.wait_ge(*at(p_turned, it, 1))
                dve.wait_ge(*at(attended, it, 2, 1))
                spread(dve.tensor_copy, it, 1, p_spread_d)

            def residual(it):
                dve.wait_ge(*at(out_projected, it, 1))
                dve.wait_ge(*at_group(y_done, it, 1, 2))
                dve.tensor_tensor(y1[:, it.slot // GROUP, it.slot % GROUP, :], FB[:, 0:C],
                                  Y[:, bass.ds(it.t % NT, 1), :].rearrange("p o c -> p (o c)"), ALU.add).then_inc(y1_done, 1)

            def ffn_stats(it):
                dve.wait_ge(*at_group(shift_turned, it, 1))
                dve.wait_ge(*at_group(xn_turned, it, 1, 1))
                dve.tensor_copy(xn[:].rearrange("p t c -> p (t c)"), FB).then_inc(stats_step, 1)
                dve.wait_ge(*at_group(stats_step, it, 1))
                dve.sem_inc(held, 1)
                for j in range(GROUP):
                    dve.bn_stats(stats[:, j, :], xn[:, j, :]).then_inc(stats_step, 1)
                dve.wait_ge(*at_group(stats_step, it, 5))
                dve.sem_inc(held, 1)
                for j in range(GROUP):
                    dve.bn_aggr(mv[:, j, :], stats[:, j, :]).then_inc(stats_step, 1)
                dve.wait_ge(*at_group(stats_step, it, 9))
                dve.tensor_scalar(veps[:], mv[:, :, 1:2].rearrange("p t o -> p (t o)"), 1e-5, None,
                                  ALU.add).then_inc(stats_step, 1)

            def ffn_norm(it):
                dve.wait_ge(*at_group(rstd_done, it, 1))
                for j in range(GROUP):
                    dve.tensor_scalar(xn[:, j, :], xn[:, j, :], mv[:, j, 0:1], rstd[:, j:j + 1],
                                      ALU.subtract, ALU.mult).then_inc(xn_done, 1)

            def ffn_gated(it):
                dve.wait_ge(*at_group(down_done, it, 1, 1))
                for c, (f, w) in enumerate(FCH):
                    dve.wait_ge(*at_group(ups_done, it, c + 1))
                    dve.scalar_tensor_tensor(out=hid[0:w, c, :], in0=HID_BANKS[c][0:w, :],
                                             scalar=cols[0:w, c:c + 1], in1=gate[0:w, c, :],
                                             op0=ALU.add, op1=ALU.mult).then_inc(gated, 1)

            def ffn_sum(it):
                dve.wait_ge(*at_group(down_done, it, 1))
                dve.wait_ge(*at_group(biased, it, 1))
                dve.tensor_tensor(Y[:, bass.ds(it.t % NT, GROUP), :], FB.rearrange("p (t c) -> p t c", t=GROUP),
                                  y1[:, it.slot // GROUP, :, :], ALU.add).then_inc(y_done, 1)

            dve.wait_ge(consts, 48)
            dve.wait_ge(zeroed, 7)
            newton = [(4, inverse_norm(n)) for n in range(12)]
            pipeline(dve, 0, UNITS, U, [
                newton[0], (3, rotate(0, 0)), newton[1], (3, rotate(0, 1)), newton[2], (3, rotate(1, 0)), newton[3],
                (3, rotate(1, 1)), newton[4], (6, spread_d), newton[5], (5, mask_scores(0)), newton[6],
                (5, find_max(0)), newton[7], (3, rotate(2, 0)), newton[8], (3, rotate(2, 1)), newton[9],
                (3, rotate(3, 0)), newton[10], (3, rotate(3, 1)), newton[11], (11, by_group(ffn_norm)),
                (5, mask_scores(1)), (5, find_max(1)),
                (3, sum_squares(0)), (3, sum_squares(1)), (5, sum_p(0)), (3, sum_squares(2)), (5, invert_sum(0)),
                (3, sum_squares(3)), (5, sum_p(1)), (6, residual), (5, invert_sum(1)), (12, by_group(ffn_gated)),
                (10, by_group(ffn_stats)), (13, by_group(ffn_sum))])

        @block.gpsimd
        def _(pool):
            seed(pool, [table_made, rope_added, qk_normed, shifted_max, p_scaled, staged, rstd_done, biased])

            def stage(it):
                pool.wait_ge(*at_group(y_done, it, 1, GROUPS_PER_LAYER))
                pool.wait_ge(*at_group(x_turned, it, 1, 1))
                pool.sem_inc(held, 1)
                pool.tensor_copy(y_in[:], Y[:, bass.ds(it.t % NT, GROUP), :]).then_inc(staged, 1)

            def make_table(it):
                pool.wait_ge(*loads(scales_in, it))
                pool.wait_ge(*at(roped, it, 8, 2))
                pool.sem_inc(held, 1)
                pool.tensor_tensor(rope[:, it.slot % 2, :, :].unsqueeze(1), rope_base[:, bass.ds(it.t % TPB, 1), :, :],
                                   scales[:].rearrange("p (o a d) -> p o a d", o=1, a=4), ALU.mult).then_inc(table_made, 1)

            def add_rotated(c):
                def do(it):
                    pool.wait_ge(*at(roped, it, 2 * c + 2))
                    dst = qk[:, it.slot % 2, c, :]
                    pool.tensor_tensor(dst, dst, rotated[:, c % 2, :], ALU.add).then_inc(rope_added, 1)
                return do

            def norm(n):
                def do(it):
                    b, c = it.slot % 2, TURN_ORDER[n]
                    if n == 0:
                        pool.wait_ge(*at(rs_step, it, 12))
                        pool.wait_ge(*at(rope_added, it, 4))
                    dst = qk[:, b, c, :].rearrange("p (h d) -> p h d", h=8)
                    r = rs_y[:, b, 8 * c:8 * c + 8].unsqueeze(2).to_broadcast([P, 8, HD])
                    pool.tensor_tensor(dst, dst, r, ALU.mult).then_inc(qk_normed, 1)
                return do

            def subtract_max(c):
                def do(it):
                    b = it.slot % 2
                    pool.wait_ge(*at(maxed, it, c + 1))
                    s = sc[:, b, c, :].rearrange("p (h k) -> p h k", h=8)
                    pool.tensor_tensor(s, s, mx[:, b, 8 * c:8 * c + 8].unsqueeze(2).to_broadcast([P, 8, 2 * WIN]),
                                       ALU.subtract).then_inc(shifted_max, 1)
                return do

            def scale_p(c):
                def do(it):
                    b = it.slot % 2
                    pool.wait_ge(*at(inverted, it, c + 1))
                    s = sc[:, b, c, :].rearrange("p (h k) -> p h k", h=8)
                    pool.tensor_tensor(s, s, rsum[:, b, 8 * c:8 * c + 8].unsqueeze(2).to_broadcast([P, 8, 2 * WIN]),
                                       ALU.mult).then_inc(p_scaled, 1)
                return do

            def ffn_rstd(it):
                pool.wait_ge(*at_group(stats_step, it, 10))
                pool.tensor_tensor(rstd[:], veps[:], minus_half[:], ALU.pow).then_inc(rstd_done, 1)

            def ffn_bias(it):
                pool.wait_ge(*loads(bias_in, it))
                pool.wait_ge(*at_group(y1_turned, it, 1))
                y = y1[:, it.slot // GROUP, :, :]
                pool.tensor_tensor(y, y, bias_row[:].unsqueeze(1).to_broadcast([P, GROUP, C]), ALU.add).then_inc(biased, 1)

            pool.wait_ge(consts, 48)
            pool.wait_ge(zeroed, 7)
            pipeline(pool, 0, UNITS, U, [
                (11, by_group(ffn_rstd)), (3, add_rotated(0)), (3, add_rotated(1)), (2, make_table),
                (5, subtract_max(0)), (3, add_rotated(2)), (3, add_rotated(3)), (0, by_group(stage)), (5, subtract_max(1)),
                (4, norm(0)), (4, norm(1)), (5, scale_p(0)), (4, norm(2)), (4, norm(3)), (5, scale_p(1)),
                (12, by_group(ffn_bias))])


def sandwich_kernel(nc, A, out):
    with ExitStack() as ctx:
        x = ctx.enter_context(nc.sbuf_tensor("x", [P, NT, C], F32))
        y = ctx.enter_context(nc.sbuf_tensor("y", [P, NT, C], F32))
        ident = ctx.enter_context(nc.sbuf_tensor("ident", [P, P], F32))
        psum = ctx.enter_context(nc.psum_tensor("psum", [P, 8, 512], F32))
        x_loaded = ctx.enter_context(nc.semaphore("x_loaded"))
        out_stored = ctx.enter_context(nc.semaphore("out_stored"))
        scratch = nc.dram_tensor("router_weights_dram", (NT, P), F32).ap()
        norms = Normalizer(nc, ctx)

        with nc.Block() as block:
            @block.sync
            def _(sp):
                sp.dma_start(x[:], A["x"].rearrange("b (t p) c -> p (b t) c", p=P)).then_inc(x_loaded, 16)
                sp.dma_start(ident[:], A["ident"]).then_inc(x_loaded, 16)
                sp.wait_ge(x_loaded, 32)

        norms.run(x, y, LN_EPS)
        causal_attention(nc, A, y, y, ident, psum)
        norms.run(y, y, LN_EPS, residual=x)
        norms.run(x, y, LN_EPS)
        routed_block(nc, A, y, y, ident, psum, scratch)
        norms.run(y, y, LN_EPS, residual=x)
        norms.run(x, y, LN_EPS)
        linear_attention(nc, A, y, y, ident, psum)
        norms.run(y, y, LN_EPS, residual=x)
        norms.run(x, y, LN_EPS)
        local_transformer(nc, A, y, ident, psum)
        norms.run(y, y, LN_EPS, residual=x)

        with nc.Block() as block:
            @block.sync
            def _(sp):
                sp.dma_start(out.rearrange("b (t p) c -> p (b t) c", p=P), x[:]).then_inc(out_stored, 16)
                sp.wait_ge(out_stored, 16)


def _lay_out(inputs):
    import numpy as np
    f = np.float32
    d = {k: np.asarray(v) for k, v in inputs.items()}
    masked = f(-3e38)
    a = {"x": d["L0_attn_x"], "ident": np.eye(P, dtype=f)}

    for k in ("w_kv_down", "w_kv_up", "w_q", "w_out"):
        a[k] = d["L0_attn_" + k]
    a["causal"] = np.where(np.tril(np.ones((P, P), bool)), f(0), masked).astype(f)

    for k in ("attention_mask", "position_ids", "router_w", "router_b", "wq", "wk", "wv", "wo", "w1", "w2", "ln1", "ln2"):
        a[k] = d["L0_ffn_" + k]
    positions = a.pop("position_ids")
    positions = np.concatenate([positions, np.repeat(positions[:, -1:], T - positions.shape[1], 1)], 1)
    a["pos"] = positions.reshape(B, TPB, P).transpose(2, 0, 1)
    token, column = np.arange(P)[:, None], np.arange(2 * T - P)[None]
    a["from_here"] = (column - (T - P) >= token).astype(f)
    slot = np.arange(P)
    a["slots"] = np.tile(np.where(slot < P - 1, slot, -1).astype(f), (P, 1))
    a["spare"] = np.tile(np.where(slot < P - 1, f(0), masked).astype(f), (P, 1))
    all_last = np.zeros((P, P), f)
    all_last[:, P - 1] = 1
    a["last_row"] = np.stack([np.eye(P, dtype=f), all_last], 1)
    a["halves_sign"] = np.tile(np.array([-1, 1], f), (P, 1))
    a["inv_freq"] = np.tile(f(1) / f(10000) ** (np.arange(0, 8, 2, dtype=f) / f(8)), (P, 1)).astype(f)
    a["head_cols"] = (np.arange(P)[:, None] // 8 == np.arange(16)[None]).astype(f)

    a["head_blocks"] = np.repeat(a["head_cols"], 8, 1)

    a["la_wT"] = np.stack([d["L1_attn_" + k].T for k in ("Wq", "Wk", "Wv", "Wo")], 1)
    a["la_bias_cols"] = np.stack([d["L1_attn_bq"], d["L1_attn_bk"]], 1)
    a["la_bias_rows"] = np.stack([d["L1_attn_bv"], d["L1_attn_bo"]], 0)
    a["la_PT"] = d["L1_attn_P"].T

    for k in ("Wqkv", "Wo", "W1", "W2"):
        a[k] = d["L1_ffn_" + k]
    b1 = d["L1_ffn_b1"]
    cols = np.zeros((DEPTH, P, 8), b1.dtype)
    for k, (lo, w) in enumerate(FCH):
        cols[:, :w, k] = b1[:, lo:lo + w]
        cols[:, :w, 3 + k] = b1[:, FF + lo:FF + lo + w]
    cols[:, :, 6], cols[:, :, 7] = d["L1_ffn_ln_g"], d["L1_ffn_ln_b"]
    a["cols"] = cols

    def rotated(v):
        return np.concatenate([v[:, HD // 2:], v[:, :HD // 2]], 1)
    q, k = d["L1_ffn_q_scale"], d["L1_ffn_k_scale"]
    a["rows"] = np.concatenate([d["L1_ffn_b2"], q, rotated(q), k, rotated(k)], 1)
    half = np.arange(0, HD, 2, dtype=f)
    inv_freq = f(1) / (f(10000) ** (half / f(HD))).astype(f)
    position = np.arange(T, dtype=f)
    freqs = (position[:, None] * inv_freq[None]).astype(f)
    base = ((half + f(0.4 * HD)) / f(1.4 * HD)).astype(f)
    scale = (base[None] ** ((position - T // 2) / f(WIN // 2)).astype(f)[:, None]).astype(f)
    freqs, scale = np.concatenate([freqs, freqs], 1), np.concatenate([scale, scale], 1)
    sign = np.concatenate([-np.ones(HD // 2, f), np.ones(HD // 2, f)])
    table = np.stack([np.cos(freqs) * scale, np.sin(freqs) * sign * scale,
                      np.cos(freqs) * (f(1) / scale), np.sin(freqs) * sign * (f(1) / scale)], 1)
    a["rope_base"] = table.reshape(TPB, P, 4, HD).transpose(1, 0, 2, 3).astype(f)
    row, column = np.arange(P)[:, None] % WIN, np.arange(2 * WIN)[None]
    window = np.where((column >= row) & (column <= row + WIN), f(0), masked).astype(f)
    window = np.repeat(window[:, None], TPB, 1)
    window[0:WIN, 0, 0:WIN] = masked
    a["win_mask"] = window
    keep = np.ones((P, TPB), f)
    keep[:, 0] = 0
    a["keep_carry"] = keep
    return {k: np.ascontiguousarray(v) for k, v in a.items()}


def kernel(**inputs):
    import concourse.bacc as bacc
    from concourse.bass_utils import run_bass_kernel_spmd

    nc = bacc.Bacc("TRN2", target_bir_lowering=False, num_devices=1)
    arrays, aps = {}, {}
    for name, a in _lay_out(inputs).items():
        arrays[f"in_{name}_dram"] = a
        aps[name] = nc.dram_tensor(f"in_{name}_dram", a.shape, mybir.dt.from_np(a.dtype), kind="ExternalInput").ap()
    out = nc.dram_tensor("out_dram", (B, T, C), F32, kind="ExternalOutput").ap()
    sandwich_kernel(nc, aps, out)
    result = run_bass_kernel_spmd(nc, [arrays], core_ids=[0])
    return result.results[0]["out_dram"]
```

```python
from contextlib import ExitStack

import concourse.bass as bass
from concourse import mybir

F32 = mybir.dt.float32
F32R = mybir.dt.float32r
I32 = mybir.dt.int32
U32 = mybir.dt.uint32
ALU = mybir.AluOpType
ACT = mybir.ActivationFunctionType
AX = mybir.AxisListType

P = 128
B, T, C = 4, 1024, 128
NT = B * T // P
TPB = T // P
LN_EPS = 1e-5
DEPTH, HEADS, HD, WIN = 6, 16, 64, 32
INNER = HEADS * HD
QKV = 3 * INNER


class Item:

    def __init__(self, index, t=0, slot=0, turn=0, units=None):
        self.index, self.t, self.slot, self.turn, self.units = index, t, slot, turn, units

    def has(self, ahead):
        return self.units is None or self.t + ahead < self.units


SEED = 8


def reached(item, per, k, back=0, seed=SEED):
    return (item.index + (seed - back)) * per + k


def pipeline(eng, base, units, unroll, stages):
    lag_max = max(lag for lag, _ in stages)
    peeled = -(-lag_max // unroll) * unroll

    def step(s, static, u, turn):
        for lag, do in stages:
            if static and not 0 <= s - lag < units:
                continue
            do(Item(base + (s - lag), s - lag, (u - lag) % unroll, turn + (u - lag) // unroll,
                    units if static else None))

    for s in range(peeled):
        step(s, True, s % unroll, s // unroll)
    with eng.Fori(0, (units - peeled) // unroll, 1) as k:
        for u in range(unroll):
            step(k * unroll + (peeled + u), False, u, k + peeled // unroll)
    for s in range(units, units + lag_max):
        step(s, True, s % unroll, s // unroll)


class Normalizer:

    G = 4
    W = NT // G

    def __init__(self, nc, ctx):
        def sb(n, shape):
            return ctx.enter_context(nc.sbuf_tensor("n_" + n, shape, F32))

        def sem(n):
            return ctx.enter_context(nc.semaphore("n_" + n))

        self.nc, self.runs, self.residual_runs = nc, 0, 0
        self.stats, self.mv = sb("stats", [P, NT, 6]), sb("mv", [P, NT, 2])
        self.var, self.rstd, self.power = sb("var", [P, NT]), sb("rstd", [P, NT]), sb("power", [P, NT])
        self.power_set = sem("power_set")
        self.counted, self.averaged, self.var_done, self.rstd_done, self.scaled, self.ended = (
            sem("counted"), sem("averaged"), sem("var_done"), sem("rstd_done"), sem("scaled"), sem("ended"))

    def run(self, src, dst, eps, residual=None):
        nc, G, W, n, r = self.nc, self.G, self.W, self.runs, self.residual_runs
        stats, mv, var, rstd, power = self.stats, self.mv, self.var, self.rstd, self.power
        power_set, counted, averaged, var_done = self.power_set, self.counted, self.averaged, self.var_done
        rstd_done, scaled, ended = self.rstd_done, self.scaled, self.ended
        self.runs += 1
        self.residual_runs += residual is not None

        def tiles(g):
            return slice(W * g, W * g + W)

        with nc.Block() as block:
            @block.vector
            def _(dve):
                if n == 0:
                    dve.memset(power[:], -0.5).then_inc(power_set, 1)

                def moments(g):
                    for t in range(W * g, W * g + W):
                        dve.bn_stats(stats[:, t, :], src[:, t, :]).then_inc(counted, 1)
                    dve.wait_ge(counted, n * NT + W * (g + 1))
                    for t in range(W * g, W * g + W):
                        dve.bn_aggr(mv[:, t, :], stats[:, t, :]).then_inc(averaged, 1)
                    dve.wait_ge(averaged, n * NT + W * (g + 1))
                    dve.tensor_scalar(var[:, tiles(g)].unsqueeze(2), mv[:, tiles(g), 1:2], eps, None,
                                      ALU.add).then_inc(var_done, 1)

                def scale(g):
                    dve.wait_ge(rstd_done, n * G + g + 1)
                    for t in range(W * g, W * g + W):
                        dve.tensor_scalar(dst[:, t, :], src[:, t, :], mv[:, t, 0:1], rstd[:, t:t + 1],
                                          ALU.subtract, ALU.mult).then_inc(scaled, 1)

                moments(0)
                for g in range(1, G):
                    moments(g)
                    scale(g - 1)
                scale(G - 1)
                dve.wait_ge(scaled, (n + 1) * NT)

            @block.gpsimd
            def _(pool):
                pool.wait_ge(power_set, 1)
                for g in range(G + 1):
                    if g < G:
                        pool.wait_ge(var_done, n * G + g + 1)
                        pool.tensor_tensor(rstd[:, tiles(g)], var[:, tiles(g)], power[:, tiles(g)],
                                           ALU.pow).then_inc(rstd_done, 1)
                    if g > 0 and residual is not None:
                        pool.wait_ge(scaled, n * NT + W * g)
                        pool.tensor_tensor(residual[:, tiles(g - 1), :], residual[:, tiles(g - 1), :],
                                           dst[:, tiles(g - 1), :], ALU.add).then_inc(ended, 1)
                if residual is not None:
                    pool.wait_ge(ended, (r + 1) * G)


def causal_attention(nc, A, xn, z, ident, psum, before):
    H, D = 16, 64
    PAIRS, QT = H // 2, TPB
    UNITS, U = PAIRS * QT, 2 * QT
    SEEDED = 24
    SCALE = float(D) ** -0.5
    with ExitStack() as ctx:
        def sb(name, shape, dt=F32):
            return ctx.enter_context(nc.sbuf_tensor("a_" + name, shape, dt))

        def sem(name):
            return ctx.enter_context(nc.semaphore("a_" + name))

        w_down, w_up, w_q = sb("w_down", [P, P]), sb("w_up", [P, 2 * H * D]), sb("w_q", [P, H * D])
        w_out = sb("w_out", [P, PAIRS, C])
        causal = sb("causal", [P, P])
        w_pair = sb("w_pair", [P, 3, P])
        HALF = QKV // 2
        whole, high = sb("whole", [P, HALF]), sb("high", [P, HALF], F32R)
        x_b = sb("x_b", [P, TPB, C])
        xT, latT = sb("xT", [P, T]), sb("latT", [P, T])
        q_hi, q_lo, k_hi, k_lo = (sb("q_hi", [P, 2, T], F32R), sb("q_lo", [P, 2, T], F32R),
                                  sb("k_hi", [P, 2, T], F32R), sb("k_lo", [P, 2, T], F32R))
        V = sb("V", [P, 2, TPB, P])
        probs = sb("probs", [P, 2, 2, T])
        pT = sb("pT", [P, 2, 2, T])
        nmax, rsum, rinv = sb("nmax", [P, 2, 2]), sb("rsum", [P, 2, 2]), sb("rinv", [P, 2, 2])
        oT = sb("oT", [P, PAIRS, T])

        S = [psum[:, 2 * h:2 * h + 2, :].rearrange("p a n -> p (a n)") for h in range(2)]
        TR = [psum[:, 4, :], psum[:, 5, :]]
        OB, PB = psum[:, 6, :], psum[:, 7, :]

        loaded, held = sem("loaded"), sem("held")
        x_copied, x_turned, x_in, lat_done, lat_in, out_done, out_in = (
            sem("x_copied"), sem("x_turned"), sem("x_in"), sem("lat_done"), sem("lat_in"), sem("out_done"), sem("out_in"))
        whole_in, parts_made, parts_out = sem("whole_in"), sem("parts_made"), sem("parts_out")
        w_staged, projected, proj_in, low_in = sem("w_staged"), sem("projected"), sem("proj_in"), sem("low_in")
        scored, masked, maxed, exped, inverted, scaled, turned, pT_in, attended, o_in = (
            sem("scored"), sem("masked"), sem("maxed"), sem("exped"), sem("inverted"), sem("scaled"), sem("turned"),
            sem("pT_in"), sem("attended"), sem("o_in"))
        PER = {scored: 2, masked: 2, maxed: 2, exped: 2, inverted: 2, scaled: 2, turned: 4, pT_in: 4, attended: 1, o_in: 1}

        def at(s, it, k, back=0):
            return s, reached(it, PER[s], k, back, SEEDED)

        def at_pair(s, it, b, per, k, back=0):
            return s, (b * PAIRS + it.turn * 2 + (it.slot // QT + 2 - back)) * per + k

        def seed(eng, sems):
            for s in sems:
                eng.sem_inc(s, PER[s] * SEEDED)

        def turned_bank(h, chunk, chunks):
            return chunk if chunks == 2 else h

        with nc.Block() as load_block:
            @load_block.sync
            def _(sp):
                sp.dma_start(w_down[:], A["w_kv_down"]).then_inc(loaded, 16)
                sp.dma_start(w_q[:], A["w_q"]).then_inc(loaded, 16)
                sp.dma_start(w_up[:], A["w_kv_up"]).then_inc(loaded, 16)
                sp.dma_start(causal[:], A["causal"]).then_inc(loaded, 16)
                sp.dma_start(w_out[:], A["w_out"].rearrange("(h p) c -> p h c", p=P)).then_inc(loaded, 16)

        before()
        block = ctx.enter_context(nc.Block())

        @block.sync
        def _(sp):
            sp.sem_inc(parts_out, 32)
            with sp.Fori(0, DEPTH, 1) as l:
                for half in range(2):
                    cols = slice(half * HALF, half * HALF + HALF)
                    sp.wait_ge(parts_out, (l * 2 + (half + 1)) * 32)
                    sp.sem_inc(held, 1)
                    sp.dma_start(whole[:].unsqueeze(1), A["Wqkv"][bass.ds(l, 1), :, cols].rearrange("l c n -> c l n")
                                 ).then_inc(whole_in, 16)
                    for part, buf in enumerate((high[:].bitcast(F32), whole[:])):
                        sp.wait_ge(parts_made, (l * 2 + half) * 2 + (part + 1))
                        sp.sem_inc(held, 1)
                        dram = A[("Wqkv_high", "Wqkv_low")[part]]
                        sp.dma_start(dram[bass.ds(l, 1), :, cols].rearrange("l c n -> c l n"), buf.unsqueeze(1)
                                     ).then_inc(parts_out, 16)
            sp.wait_ge(parts_out, 2 * DEPTH * 32 + 32)

        @block.gpsimd
        def _(pool):
            pool.sem_inc(w_staged, 2)
            pool.wait_ge(loaded, 80)

            def stage(it):
                pool.wait_ge(*at_pair(projected, it, 0, 6, 0))
                for n, (w, off) in enumerate([(w_q, 0), (w_up, 0), (w_up, H * D)]):
                    pair = (it.turn * 2 + it.slot // QT) % PAIRS
                    pool.sem_inc(held, 1)
                    src = w[:, off:off + H * D].rearrange("p (a n) -> p a n", n=P)
                    i = pool.tensor_copy(w_pair[:, n:n + 1, :], src[:, bass.ds(pair, 1), :])
                i.then_inc(w_staged, 1)

            def split(half):
                pool.wait_ge(whole_in, half * 16 + 16)
                pool.sem_inc(held, 1)
                pool.tensor_copy(high[:], whole[:]).then_inc(parts_made, 1)
                pool.wait_ge(parts_made, half * 2 + 1)
                pool.tensor_tensor(whole[:].bitcast(F32R), whole[:], high[:].bitcast(F32), ALU.subtract).then_inc(parts_made, 1)

            with pool.Fori(0, 2 * DEPTH, 1) as k:
                stage(Item(0, 0, 0, k))
                split(k)
                stage(Item(0, 0, QT, k))
            with pool.Fori(0, B * PAIRS // 2 - 2 * DEPTH, 1) as k:
                for u in (0, QT):
                    stage(Item(0, 0, u, k + 2 * DEPTH))

        @block.tensor
        def _(pe):
            seed(pe, [scored, turned, attended])
            pe.sem_inc(projected, 12)
            pe.wait_ge(loaded, 80)
            with pe.Fori(0, B, 1) as b:
                pe.wait_ge(x_copied, b + 1)
                for c in range(2):
                    for j in range(4):
                        m = pe.transpose(TR[c][:, j * P:(j + 1) * P], x_b[:, 4 * c + j, :], ident[:])
                    m.then_inc(x_turned, 1)
                for c in range(2):
                    pe.wait_ge(x_in, 2 * b + c + 1)
                    pe.matmul([OB, PB][c], w_down[:], xT[:, 512 * c:512 * c + 512], start=True, stop=True).then_inc(lat_done, 1)

                def score(h):
                    r = slice(64 * h, 64 * h + 64)

                    def do(it):
                        i, pb = it.slot % QT, it.slot // QT % 2
                        if i == 0 and h == 0:
                            pe.wait_ge(*at_pair(low_in, it, b, 4, 4))
                        pe.wait_ge(*at(exped, it, h + 1, 1))
                        w = (i + 1) * P
                        qs = slice(i * P, (i + 1) * P)
                        for c in range(0, w, 512):
                            n = max(min(512, w - c), 256)
                            for a, k in ((q_hi, k_lo), (q_lo, k_hi), (q_hi, k_hi)):
                                m = pe.matmul(S[h][:, c:c + n], a[r, pb, qs], k[r, pb, c:c + n],
                                              start=(k is k_lo), stop=(k is k_hi and a is q_hi))
                        m.then_inc(scored, 1)
                    return do

                def turn(h):
                    def do(it):
                        i, par = it.slot % QT, it.slot % 2
                        pe.wait_ge(*at(scaled, it, h + 1))
                        chunks = range(0, i + 1, 4)
                        for n, c in enumerate(chunks):
                            bank = TR[turned_bank(h, n, len(chunks))]
                            if len(chunks) == 2 and h == 1:
                                pe.wait_ge(*at(pT_in, it, n + 1))
                            elif 1 <= i <= 4:
                                pe.wait_ge(*at(pT_in, it, 2 * (h + n) + 2, 1))
                            else:
                                pe.wait_ge(*at(pT_in, it, 3 + h + n, 1))
                            for k in range(c, min(c + 4, i + 1)):
                                m = pe.transpose(bank[:, (k - c) * P:(k - c + 1) * P],
                                                 probs[:, par, h, k * P:(k + 1) * P], ident[:])
                            m.then_inc(turned, 2 // len(chunks))
                    return do

                def attend(it):
                    i, pb, par = it.slot % QT, it.slot // QT % 2, it.slot % 2
                    if i == 0:
                        pe.wait_ge(*at_pair(proj_in, it, b, 6, 6))
                    pe.wait_ge(*at(pT_in, it, 4))
                    pe.wait_ge(*at(o_in, it, 1, 1))
                    for k in range(i + 1):
                        for h in range(2):
                            m = pe.matmul(OB[64 * h:64 * h + 64, 0:P], V[:, pb, k, 64 * h:64 * h + 64],
                                          pT[:, par, h, k * P:(k + 1) * P], start=(k == 0), stop=(k == i),
                                          tile_position=(0, 64 * h))
                    m.then_inc(attended, 1)

                def project(it):
                    n = it.slot % QT
                    if n == 0:
                        pe.wait_ge(*at_pair(w_staged, it, b, 1, 1))
                        pe.wait_ge(lat_in, 2 * b + 2)
                    if n >= 6:
                        return
                    pe.wait_ge(*at_pair(proj_in, it, b, 6, n))
                    pe.wait_ge(*at_pair(low_in, it, b, 4, min(n, 4)))
                    c = n % 2
                    if n < 4:
                        m = pe.matmul(PB, w_pair[:, n // 2, :], [xT, latT][n // 2][:, 512 * c:512 * c + 512],
                                      start=True, stop=True)
                    else:
                        for j in range(4):
                            m = pe.matmul(PB[:, j * P:(j + 1) * P], latT[:, (4 * c + j) * P:(4 * c + j + 1) * P],
                                          w_pair[:, 2, :], start=True, stop=True)
                    m.then_inc(projected, 1)

                pipeline(pe, b * UNITS, UNITS, U, [
                (8, score(0)), (9, turn(0)), (8, score(1)), (0, project), (9, turn(1)), (10, attend)])
                done = Item(b * UNITS + UNITS)
                pe.wait_ge(*at(o_in, done, 0))
                for i in range(TPB):
                    pe.wait_ge(out_in, b * TPB + i + 1)
                    for p in range(PAIRS):
                        m = pe.matmul([OB, PB][i % 2][:, 0:C], oT[:, p, i * P:(i + 1) * P], w_out[:, p, :],
                                      start=(p == 0), stop=(p == PAIRS - 1))
                    m.then_inc(out_done, 1)

        @block.scalar
        def _(act):
            seed(act, [exped, pT_in])
            act.sem_inc(proj_in, 12)
            with act.Fori(0, B, 1) as b:
                for c in range(2):
                    act.wait_ge(x_turned, 2 * b + c + 1)
                    act.activation(xT[:, 512 * c:512 * c + 512], TR[c], ACT.Copy).then_inc(x_in, 1)
                for c in range(2):
                    act.wait_ge(lat_done, 2 * b + c + 1)
                    act.activation(latT[:, 512 * c:512 * c + 512], [OB, PB][c], ACT.Copy).then_inc(lat_in, 1)

                def take_projection(it):
                    n, pb = it.slot % QT, it.slot // QT % 2
                    if n >= 6:
                        return
                    c = n % 2
                    act.wait_ge(*at_pair(projected, it, b, 6, n + 1))
                    if n < 4:
                        act.wait_ge(*at(scored, it, 2, 9 + n))
                    else:
                        act.wait_ge(*at(attended, it, 1, 9 + n))
                    if n < 2:
                        i = act.activation(q_hi[:, pb, 512 * c:512 * c + 512], PB, ACT.Copy, scale=SCALE)
                    elif n < 4:
                        i = act.activation(k_hi[:, pb, 512 * c:512 * c + 512], PB, ACT.Copy)
                    else:
                        i = act.activation(V[:, pb, 4 * c:4 * c + 4, :], PB.rearrange("p (a n) -> p a n", a=4), ACT.Copy)
                    i.then_inc(proj_in, 1)

                def exps(h):
                    def do(it):
                        par, w = it.slot % 2, (it.slot % QT + 1) * P
                        act.wait_ge(*at(maxed, it, h + 1))
                        act.wait_ge(*at(turned, it, 2 * h + 2, 2))
                        act.wait_ge(*at(inverted, it, h + 1, 2))
                        act.activation(probs[:, par, h, 0:w], S[h][:, 0:w], ACT.Exp, bias=nmax[:, par, h:h + 1],
                                       accum_out=rsum[:, par, h:h + 1]).then_inc(exped, 1)
                    return do

                def take_pT(h):
                    def do(it):
                        i, par = it.slot % QT, it.slot % 2
                        chunks = range(0, i + 1, 4)
                        act.wait_ge(*at(attended, it, 1, 2))
                        for n, c in enumerate(chunks):
                            w = (min(c + 4, i + 1) - c) * P
                            act.wait_ge(*at(turned, it, 2 * h + (n + 1) * (2 // len(chunks))))
                            act.activation(pT[:, par, h, c * P:c * P + w], TR[turned_bank(h, n, len(chunks))][:, 0:w],
                                           ACT.Copy).then_inc(pT_in, 2 // len(chunks))
                    return do

                pipeline(act, b * UNITS, UNITS, U, [
                (9, take_pT(0)), (8, exps(0)), (0, take_projection), (9, take_pT(1)), (8, exps(1))])

        @block.vector
        def _(dve):
            seed(dve, [masked, maxed, inverted, scaled, o_in])
            dve.sem_inc(out_in, 1)
            dve.sem_inc(low_in, 8)
            with dve.Fori(0, B, 1) as b:
                dve.wait_ge(out_in, b * TPB + 1)
                dve.sem_inc(held, 1)
                dve.tensor_copy(x_b[:], xn[:, bass.ds(b * TPB, TPB), :]).then_inc(x_copied, 1)

                def mask_and_max(h):
                    def do(it):
                        i, par = it.slot % QT, it.slot % 2
                        w = (i + 1) * P
                        dve.wait_ge(*at(scored, it, h + 1))
                        dve.tensor_tensor(S[h][:, w - P:w], S[h][:, w - P:w], causal[:], ALU.add).then_inc(masked, 1)
                        dve.wait_ge(*at(masked, it, h + 1))
                        dve.wait_ge(*at(exped, it, h + 1, 2))
                        dve.tensor_reduce(nmax[:, par, h:h + 1], S[h][:, 0:w], AX.X, ALU.max, negate=True).then_inc(maxed, 1)
                    return do

                def take_low(it):
                    n, pb = it.slot % QT, it.slot // QT % 2
                    if n >= 4:
                        return
                    c = slice(n % 2 * 512, n % 2 * 512 + 512)
                    dve.wait_ge(*at_pair(proj_in, it, b, 6, n + 1))
                    hi, lo = ((q_hi, q_lo), (k_hi, k_lo))[n // 2]
                    dve.scalar_tensor_tensor(out=lo[:, pb, c], in0=PB, scalar=SCALE if n < 2 else 1.0, in1=hi[:, pb, c],
                                             op0=ALU.mult, op1=ALU.subtract).then_inc(low_in, 1)

                def scale(h):
                    def do(it):
                        par, w = it.slot % 2, (it.slot % QT + 1) * P
                        dve.wait_ge(*at(exped, it, h + 1))
                        dve.reciprocal(rinv[:, par, h:h + 1], rsum[:, par, h:h + 1]).then_inc(inverted, 1)
                        dve.wait_ge(*at(inverted, it, h + 1))
                        p = probs[:, par, h, 0:w]
                        dve.tensor_scalar(p, p, rinv[:, par, h:h + 1], None, ALU.mult).then_inc(scaled, 1)
                    return do

                def take_o(it):
                    i = it.slot % QT
                    dve.wait_ge(*at(attended, it, 1))
                    dve.sem_inc(held, 1)
                    pair = it.turn * 2 + it.slot // QT
                    dve.tensor_copy(oT[:, bass.ds(pair, 1), i * P:(i + 1) * P], OB[:, 0:P].unsqueeze(1)).then_inc(o_in, 1)

                pipeline(dve, b * UNITS, UNITS, U, [
                (8, mask_and_max(0)), (8, mask_and_max(1)), (8, scale(0)), (0, take_low), (10, take_o), (8, scale(1))])
                for i in range(TPB):
                    dve.wait_ge(out_done, b * TPB + i + 1)
                    dve.sem_inc(held, 1)
                    dve.tensor_copy(z[:, bass.ds(b * TPB + i, 1), :], [OB, PB][i % 2][:, 0:C].unsqueeze(1)).then_inc(out_in, 1)
            dve.wait_ge(out_in, B * TPB + 1)


def routed_block(nc, A, xn, z, ident, psum, scratch, before):
    H, D, F = 16, 8, 512
    S = 512
    KEPT = 127
    MAGIC = 12582912.0
    INV_2PI = 0.15915494309189535
    C1, C2, C3 = 6.28125, 1.93500518798828125e-3, 3.0199159819e-7
    PI = 3.14159250259399414
    HALF_PI = 1.57079632679489662
    with ExitStack() as ctx:
        def sb(name, shape, dt=F32):
            return ctx.enter_context(nc.sbuf_tensor("m_" + name, shape, dt))

        def sem(name):
            return ctx.enter_context(nc.semaphore("m_" + name))

        XC = P + 2
        router = sb("router", [P, C])
        router_b = sb("router_b", [P, 1])
        products = sb("products", [P, NT, C])
        weights = sb("weights", [P, NT])
        weights_t = sb("weights_t", [NT, P])
        w_row = sb("w_row", [P, 2, T])
        from_here = sb("from_here", [P, 2 * T - P])
        junk = sb("junk", [P, 2, T])
        slots_sign = sb("slots_sign", [P, 2])
        at_least, ties, rank = sb("at_least", [P, NT]), sb("ties", [P, NT]), sb("rank", [P, NT])
        unselected = sb("unselected", [P, NT])
        slots = sb("slots", [P, P])
        pos_i = sb("pos_i", [P, B, TPB], I32)
        x_b = sb("x_b", [P, TPB, XC])
        one_hot = sb("one_hot", [P, TPB, P])
        one_hot_T = sb("one_hot_T", [P, TPB, P])
        last_row = sb("last_row", [P, 2, P])
        clamped = sb("clamped", [P, P])
        mask = sb("mask", [P, S // P, S])
        mask_rows = sb("mask_rows", [P, S // P, P])
        spare = sb("spare", [P, P])
        mask_sel = sb("mask_sel", [P, P])
        w_qkv, w_o, w_1, w_2 = sb("w_qkv", [P, 3 * P]), sb("w_o", [P, P]), sb("w_1", [P, F]), sb("w_2", [P, 4, P])
        ln = sb("ln", [P, 2, C])
        head_cols = sb("head_cols", [P, H])
        inv_freq = sb("inv_freq", [P, 4])
        minus_half = sb("minus_half", [P, 1])
        x_sel = sb("x_sel", [P, XC])
        sq = sb("sq", [P, C])
        ssum = sb("ssum", [P, 1])
        rms = sb("rms", [P, 1])
        hn = sb("hn", [P, C])
        hT = sb("hT", [P, P])
        ang, turns = sb("ang", [P, 4]), sb("turns", [P, 4])
        sincos_in, over, sincos = sb("sincos_in", [P, 2, 4]), sb("over", [P, 2, 4]), sb("sincos", [P, 2, 4])
        sin2 = sb("sin2", [P, 2, 4])
        qk_a, qk_b = sb("qk_a", [P, 2 * P]), sb("qk_b", [P, 2 * P])
        v = sb("v", [P, P])
        qT = sb("qT", [P, P])
        k_heads = sb("k_heads", [P, H, P])
        s = sb("s", [P, H, P])
        mx, sm = sb("mx", [P, H]), sb("sm", [P, H])
        pT = sb("pT", [P, H, P])
        o = sb("o", [P, P])
        oT = sb("oT", [P, P])
        x1, x2 = sb("x1", [P, C]), sb("x2", [P, C])
        hid = sb("hid", [P, 4, P])

        def bank(n, m=1):
            return psum[:, n:n + m, :].rearrange("p a n -> p (a n)")

        loaded, held, mask_in, stored = sem("loaded"), sem("held"), sem("mask_in"), sem("stored")
        row_in = [sem("even_row_in"), sem("odd_row_in")]
        batch_kept = sem("batch_kept")
        prepared, turned_w, copied_w, rank_step, batch_done = (
            sem("prepared"), sem("turned_w"), sem("copied_w"), sem("rank_step"), sem("batch_done"))

        class Steps:

            def __init__(self, name, names):
                self.sem, self.names, self.given = sem(name), names.split(), 0

            def done(self, ins, name):
                assert self.names[self.given % len(self.names)] == name, name
                self.given += 1
                ins.then_inc(self.sem, 1)

            def reached(self, b, name):
                return self.sem, b * len(self.names) + self.names.index(name) + 1

        pe_steps = Steps("pe_steps", """gathered one_hot_turned clamped_row mask_rows mask_selected normed_turned qkv
            qk_turned scores probs_turned attended o_turned projected normed2_turned hidden mlp scattered""")
        act_steps = Steps("act_steps", """one_hot_T clamped mask_rows hT sin qT v exps pT oT hT2 gelu""")
        dve_steps = Steps("dve_steps", """one_hot x_in pos_in w_in x_sel sq ssum rms_in hn
            ang turns turns2 turns3 r1 r2 r3 r4 r5 over wrapped clamp sin2 mask_sel qk_b qk_a qk k_heads
            s mx shifted sm rsm o x1 sq2 ssum2 rms_in2 hn2 x2 x2w""")
        pool_steps = Steps("pool_steps", "rms rms2")

        with nc.Block() as load_block:
            @load_block.sync
            def _(sp):
                sp.dma_start(router[:], A["router_w"].rearrange("c o -> (o c)").partition_broadcast(P)).then_inc(loaded, 16)
                sp.dma_start(router_b[:], A["router_b"].partition_broadcast(P)).then_inc(loaded, 16)
                sp.dma_start(from_here[:], A["from_here"]).then_inc(loaded, 16)
                sp.dma_start(slots[:], A["slots"]).then_inc(loaded, 16)
                sp.dma_start(last_row[:], A["last_row"]).then_inc(loaded, 16)
                sp.dma_start(spare[:], A["spare"]).then_inc(loaded, 16)
                sp.dma_start(slots_sign[:], A["halves_sign"]).then_inc(loaded, 16)
                sp.dma_start(head_cols[:], A["head_cols"]).then_inc(loaded, 16)
                sp.dma_start(inv_freq[:], A["inv_freq"]).then_inc(loaded, 16)
                for n in range(3):
                    sp.dma_start(w_qkv[:, n * P:(n + 1) * P], A[["wq", "wk", "wv"][n]]).then_inc(loaded, 16)
                sp.dma_start(w_o[:], A["wo"]).then_inc(loaded, 16)
                sp.dma_start(w_1[:], A["w1"]).then_inc(loaded, 16)
                sp.dma_start(w_2[:], A["w2"].rearrange("(h p) c -> p h c", p=P)).then_inc(loaded, 16)
                sp.dma_start(ln[:, 0, :], A["ln1"].partition_broadcast(P)).then_inc(loaded, 16)
                sp.dma_start(ln[:, 1, :], A["ln2"].partition_broadcast(P)).then_inc(loaded, 16)
                sp.dma_start(pos_i[:], A["pos"]).then_inc(loaded, 16)

        before()
        block = ctx.enter_context(nc.Block())

        @block.sync
        def _(sp):
            sp.wait_ge(copied_w, 1)
            sp.dma_start(scratch, weights_t[:]).then_inc(stored, 16)
            sp.wait_ge(stored, 16)
            rows = scratch.rearrange("(b t) p -> b (t p)", b=B)
            for b in range(B):
                if b >= 2:
                    sp.wait_ge(rank_step, (b - 1) * 2 * TPB)
                sp.dma_start(w_row[:, b % 2, :], rows[b].partition_broadcast(P)).then_inc(row_in[b % 2], 16)
            with sp.Fori(0, B, 1) as b:
                sp.wait_ge(batch_done, b + 1)
                sp.dma_start(mask[:], A["attention_mask"][bass.ds(b, 1)].rearrange("b o (t p) k -> p (b o t) k", p=P)
                             ).then_inc(mask_in, 16)

        LOADED = 16 * 18

        @block.gpsimd
        def _(pool):
            pool.wait_ge(prepared, 2)
            with pool.Fori(0, B, 1) as b:
                pool.wait_ge(*dve_steps.reached(b, "rms_in"))
                pool_steps.done(pool.tensor_tensor(rms[:], ssum[:], minus_half[:], ALU.pow), "rms")
                pool.wait_ge(*dve_steps.reached(b, "rms_in2"))
                pool_steps.done(pool.tensor_tensor(rms[:], ssum[:], minus_half[:], ALU.pow), "rms2")

        @block.tensor
        def _(pe):
            pe.wait_ge(loaded, LOADED)
            pe.wait_ge(prepared, 5)
            pe.transpose(bank(0)[0:NT, 0:P], weights[:], ident[:]).then_inc(turned_w, 1)
            with pe.Fori(0, B, 1) as b:
                def after(steps, name):
                    pe.wait_ge(*steps.reached(b, name))

                after(dve_steps, "w_in")
                for t in range(TPB):
                    m = pe.matmul(bank(0)[:, 0:XC], one_hot[:, t, :], x_b[:, t, :], start=(t == 0), stop=(t == TPB - 1))
                pe_steps.done(m, "gathered")
                for t in range(TPB):
                    m = pe.transpose(bank(1 + t // 4)[:, (t % 4) * P:(t % 4 + 1) * P], one_hot[:, t, :], ident[:])
                pe_steps.done(m, "one_hot_turned")
                for t in range(3, TPB):
                    m = pe.matmul(bank(3)[:, 0:P], last_row[:, min(t - 3, 1), :], one_hot[:, t, :],
                                  start=(t == 3), stop=(t == TPB - 1))
                pe_steps.done(m, "clamped_row")
                pe.wait_ge(mask_in, b * 16 + 16)
                after(act_steps, "clamped")
                for k in range(4):
                    for t in range(4):
                        m = pe.matmul(bank(4)[:, k * P:(k + 1) * P], mask[:, t, k * P:(k + 1) * P],
                                      one_hot[:, t, :] if t < 3 else clamped[:], start=(t == 0), stop=(t == 3))
                pe_steps.done(m, "mask_rows")
                after(act_steps, "mask_rows")
                for k in range(4):
                    m = pe.matmul(bank(5)[:, 0:P], mask_rows[:, k, :], one_hot[:, k, :] if k < 3 else clamped[:],
                                  start=(k == 0), stop=(k == 3))
                pe_steps.done(m, "mask_selected")
                after(dve_steps, "hn")
                pe_steps.done(pe.transpose(bank(0)[:, 0:P], hn[:], ident[:]), "normed_turned")
                after(act_steps, "hT")
                pe_steps.done(pe.matmul(bank(1)[:, 0:3 * P], hT[:], w_qkv[:], start=True, stop=True), "qkv")
                after(dve_steps, "qk")
                pe.transpose(bank(2)[:, 0:P], qk_a[:, 0:P], ident[:])
                pe_steps.done(pe.transpose(bank(3)[:, 0:P], qk_a[:, P:2 * P], ident[:]), "qk_turned")
                after(dve_steps, "k_heads")
                after(act_steps, "qT")
                for g in range(4):
                    m = pe.matmul(bank(4 + g), qT[:], k_heads[:, 4 * g:4 * g + 4, :].rearrange("p h k -> p (h k)"),
                                  start=True, stop=True)
                pe_steps.done(m, "scores")
                after(act_steps, "exps")
                after(act_steps, "v")
                for h in range(H):
                    m = pe.transpose(bank(h // 4)[:, (h % 4) * P:(h % 4 + 1) * P], s[:, h, :], ident[:])
                pe_steps.done(m, "probs_turned")
                after(act_steps, "pT")
                for h in range(H):
                    m = pe.matmul(bank(4)[:, D * h:D * h + D], pT[:, h, :], v[:, D * h:D * h + D], start=True, stop=True)
                pe_steps.done(m, "attended")
                after(dve_steps, "o")
                pe_steps.done(pe.transpose(bank(5)[:, 0:P], o[:], ident[:]), "o_turned")
                after(act_steps, "oT")
                pe_steps.done(pe.matmul(bank(6)[:, 0:C], oT[:], w_o[:], start=True, stop=True), "projected")
                after(dve_steps, "hn2")
                pe_steps.done(pe.transpose(bank(0)[:, 0:P], hn[:], ident[:]), "normed2_turned")
                after(act_steps, "hT2")
                for f in range(4):
                    m = pe.matmul(bank(1)[:, f * P:(f + 1) * P], w_1[:, f * P:(f + 1) * P], hT[:], start=True, stop=True)
                pe_steps.done(m, "hidden")
                after(act_steps, "gelu")
                for f in range(4):
                    m = pe.matmul(bank(2)[:, 0:C], hid[:, f, :], w_2[:, f, :], start=(f == 0), stop=(f == 3))
                pe_steps.done(m, "mlp")
                after(dve_steps, "x2w")
                for t in range(TPB):
                    m = pe.matmul(bank(3 + t // 4)[:, (t % 4) * P:(t % 4 + 1) * P], one_hot_T[:, t, :], x2[:],
                                  start=True, stop=True)
                pe_steps.done(m, "scattered")

        @block.scalar
        def _(act):
            act.wait_ge(turned_w, 1)
            act.activation(weights_t[:], bank(0)[0:NT, 0:P], ACT.Copy).then_inc(copied_w, 1)
            act.wait_ge(loaded, LOADED)
            with act.Fori(0, B, 1) as b:
                def after(steps, name):
                    act.wait_ge(*steps.reached(b, name))

                act.wait_ge(batch_done, b + 1)
                after(pe_steps, "one_hot_turned")
                act_steps.done(act.activation(one_hot_T[:].rearrange("p t n -> p (t n)"), bank(1, 2), ACT.Copy), "one_hot_T")
                after(pe_steps, "clamped_row")
                act_steps.done(act.activation(clamped[:], bank(3)[:, 0:P], ACT.Copy), "clamped")
                after(pe_steps, "mask_rows")
                act_steps.done(act.activation(mask_rows[:].rearrange("p t n -> p (t n)"), bank(4), ACT.Copy), "mask_rows")
                after(pe_steps, "normed_turned")
                act_steps.done(act.activation(hT[:], bank(0)[:, 0:P], ACT.Copy), "hT")
                after(dve_steps, "clamp")
                act_steps.done(act.activation(sincos[:], sincos_in[:], ACT.Sin), "sin")
                after(pe_steps, "qk_turned")
                act_steps.done(act.activation(qT[:], bank(2)[:, 0:P], ACT.Copy, scale=float(D) ** -0.5), "qT")
                after(dve_steps, "qk")
                act_steps.done(act.activation(v[:], bank(1)[:, 2 * P:3 * P], ACT.Copy), "v")
                after(dve_steps, "shifted")
                act_steps.done(act.activation(s[:], s[:], ACT.Exp), "exps")
                after(pe_steps, "probs_turned")
                act_steps.done(act.activation(pT[:].rearrange("p h n -> p (h n)"), bank(0, 4), ACT.Copy), "pT")
                after(pe_steps, "o_turned")
                act_steps.done(act.activation(oT[:], bank(5)[:, 0:P], ACT.Copy), "oT")
                after(pe_steps, "normed2_turned")
                act_steps.done(act.activation(hT[:], bank(0)[:, 0:P], ACT.Copy), "hT2")
                after(pe_steps, "hidden")
                act_steps.done(act.activation(hid[:].rearrange("p f n -> p (f n)"), bank(1), ACT.Gelu_apprx_tanh), "gelu")

        @block.vector
        def _(dve):
            dve.memset(minus_half[:], -0.5).then_inc(prepared, 1)
            dve.sem_inc(prepared, 1)
            dve.sem_inc(batch_done, 1)
            dve.wait_ge(loaded, LOADED)
            dve.tensor_tensor(products[:], xn[:], router[:].unsqueeze(1).to_broadcast([P, NT, C]), ALU.mult).then_inc(prepared, 1)
            dve.wait_ge(prepared, 3)
            dve.tensor_reduce(weights[:], products[:], AX.X, ALU.add).then_inc(prepared, 1)
            dve.wait_ge(prepared, 4)
            dve.tensor_scalar(weights[:], weights[:], router_b[:], None, ALU.add).then_inc(prepared, 1)
            dve.wait_ge(prepared, 5)
            for b in range(B):
                dve.wait_ge(row_in[b % 2], 16 * (b // 2 + 1))
                for t in range(TPB):
                    n = b * TPB + t
                    if n:
                        dve.wait_ge(rank_step, 2 * n)
                    w = weights[:, n:n + 1]
                    dve.tensor_scalar(junk[:, 0, :], w_row[:, b % 2, :], w, None, ALU.is_ge, ALU.add,
                                      accum_out=at_least[:, n:n + 1]).then_inc(rank_step, 1)
                    off = T - P - t * P
                    dve.scalar_tensor_tensor(out=junk[:, 1, :], in0=w_row[:, b % 2, :], scalar=w,
                                             in1=from_here[:, off:off + T], op0=ALU.is_equal, op1=ALU.mult,
                                             accum_out=ties[:, n:n + 1]).then_inc(rank_step, 1)
            dve.wait_ge(rank_step, 2 * NT)
            dve.tensor_tensor(rank[:], at_least[:], ties[:], ALU.subtract).then_inc(prepared, 1)
            dve.tensor_scalar(unselected[:], at_least[:], float(KEPT) + 0.5, None, ALU.is_gt).then_inc(prepared, 1)
            dve.wait_ge(prepared, 7)
            with dve.Fori(0, B, 1) as b:
                tiles = bass.ds(b * TPB, TPB)

                def after(steps, name):
                    dve.wait_ge(*steps.reached(b, name))

                def step(name, ins):
                    dve_steps.done(ins, name)

                def then(name, ins):
                    dve_steps.done(ins, name)
                    after(dve_steps, name)

                dve.wait_ge(batch_done, b + 1)
                dve.sem_inc(held, 1)
                step("one_hot", dve.tensor_tensor(one_hot[:], slots[:].unsqueeze(1).to_broadcast([P, TPB, P]),
                                                  rank[:, tiles].unsqueeze(2).to_broadcast([P, TPB, P]), ALU.is_equal))
                step("x_in", dve.tensor_copy(x_b[:, :, 0:C], xn[:, tiles, :]))
                step("pos_in", dve.tensor_copy(x_b[:, :, C:C + 1], pos_i[:, bass.ds(b, 1), :].rearrange("p o (t a) -> p (o t) a", a=1)))
                step("w_in", dve.tensor_copy(x_b[:, :, C + 1:C + 2], weights[:, tiles].unsqueeze(2)))
                after(pe_steps, "gathered")
                then("x_sel", dve.tensor_copy(x_sel[:], bank(0)[:, 0:XC]))
                x = x_sel[:, 0:C]

                def rmsnorm(x, gain, n):
                    then("sq" + n, dve.tensor_tensor(sq[:], x, x, ALU.mult))
                    then("ssum" + n, dve.tensor_reduce(ssum[:], sq[:], AX.X, ALU.add))
                    step("rms_in" + n, dve.tensor_scalar(ssum[:], ssum[:], 1.0 / C, 1e-6, ALU.mult, ALU.add))
                    after(pool_steps, "rms" + n)
                    step("hn" + n, dve.scalar_tensor_tensor(out=hn[:], in0=x, scalar=rms[:], in1=gain, op0=ALU.mult, op1=ALU.mult))

                rmsnorm(x, ln[:, 0, :], "")
                r = sincos_in[:, 0, :]
                then("ang", dve.tensor_scalar(ang[:], inv_freq[:], x_sel[:, C:C + 1], None, ALU.mult))
                then("turns", dve.tensor_scalar(turns[:], ang[:], INV_2PI, None, ALU.mult))
                then("turns2", dve.tensor_scalar(turns[:], turns[:], MAGIC, None, ALU.add))
                then("turns3", dve.tensor_scalar(turns[:], turns[:], -MAGIC, None, ALU.add))
                then("r1", dve.scalar_tensor_tensor(out=r, in0=turns[:], scalar=-C1, in1=ang[:], op0=ALU.mult, op1=ALU.add))
                then("r2", dve.scalar_tensor_tensor(out=r, in0=turns[:], scalar=-C2, in1=r, op0=ALU.mult, op1=ALU.add))
                then("r3", dve.scalar_tensor_tensor(out=r, in0=turns[:], scalar=-C3, in1=r, op0=ALU.mult, op1=ALU.add))
                then("r4", dve.tensor_scalar(sincos_in[:, 1, :], r, HALF_PI, None, ALU.add))
                then("r5", dve.tensor_scalar(over[:], sincos_in[:], PI, None, ALU.is_gt))
                then("over", dve.scalar_tensor_tensor(out=sincos_in[:], in0=over[:], scalar=-C1, in1=sincos_in[:],
                                                      op0=ALU.mult, op1=ALU.add))
                then("wrapped", dve.scalar_tensor_tensor(out=sincos_in[:], in0=over[:], scalar=-(C2 + C3), in1=sincos_in[:],
                                                         op0=ALU.mult, op1=ALU.add))
                step("clamp", dve.tensor_scalar(sincos_in[:], sincos_in[:], -PI, PI, ALU.max, ALU.min))
                after(act_steps, "sin")
                then("sin2", dve.tensor_tensor(sin2[:], sincos[:, 0:1, :].to_broadcast([P, 2, 4]),
                                               slots_sign[:].unsqueeze(2).to_broadcast([P, 2, 4]), ALU.mult))
                after(pe_steps, "mask_selected")
                step("mask_sel", dve.tensor_tensor(mask_sel[:], bank(5)[:, 0:P], spare[:], ALU.add))
                after(pe_steps, "qkv")
                qkv = bank(1)[:, 0:2 * P].rearrange("p (h r d) -> p h r d", r=2, d=4)
                step("qk_b", dve.tensor_tensor(qk_b[:].rearrange("p (h r d) -> p h r d", r=2, d=4), qkv[:, :, ::-1, :],
                                               sin2[:].unsqueeze(1).to_broadcast([P, 2 * H, 2, 4]), ALU.mult))
                then("qk_a", dve.tensor_tensor(qk_a[:].rearrange("p (h r d) -> p h r d", r=2, d=4), qkv,
                                               sincos[:, 1:2, :].unsqueeze(1).to_broadcast([P, 2 * H, 2, 4]), ALU.mult))
                step("qk", dve.tensor_tensor(qk_a[:], qk_a[:], qk_b[:], ALU.add))
                after(pe_steps, "qk_turned")
                step("k_heads", dve.tensor_tensor(k_heads[:], bank(3)[:, 0:P].unsqueeze(1).to_broadcast([P, H, P]),
                                                  head_cols[:].unsqueeze(2).to_broadcast([P, H, P]), ALU.mult))
                after(pe_steps, "scores")
                then("s", dve.tensor_tensor(s[:], bank(4, 4).rearrange("p (h k) -> p h k", h=H),
                                            mask_sel[:].unsqueeze(1).to_broadcast([P, H, P]), ALU.add))
                then("mx", dve.tensor_reduce(mx[:], s[:], AX.X, ALU.max))
                step("shifted", dve.tensor_tensor(s[:], s[:], mx[:].unsqueeze(2).to_broadcast([P, H, P]), ALU.subtract))
                after(act_steps, "exps")
                then("sm", dve.tensor_reduce(sm[:], s[:], AX.X, ALU.add))
                then("rsm", dve.reciprocal(sm[:], sm[:]))
                after(pe_steps, "attended")
                step("o", dve.tensor_tensor(o[:].rearrange("p (h d) -> p h d", h=H),
                                            bank(4)[:, 0:P].rearrange("p (h d) -> p h d", h=H),
                                            sm[:].unsqueeze(2).to_broadcast([P, H, D]), ALU.mult))
                after(pe_steps, "projected")
                then("x1", dve.tensor_tensor(x1[:], bank(6)[:, 0:C], x, ALU.add))
                rmsnorm(x1[:], ln[:, 1, :], "2")
                after(pe_steps, "mlp")
                then("x2", dve.tensor_tensor(x2[:], bank(2)[:, 0:C], x1[:], ALU.add))
                step("x2w", dve.tensor_scalar(x2[:], x2[:], x_sel[:, C + 1:C + 2], None, ALU.mult))
                dve.wait_ge(*pe_steps.reached(b, "gathered"))
                dve.sem_inc(held, 1)
                dve.tensor_tensor(z[:, tiles, :], x_b[:, :, 0:C],
                                  unselected[:, tiles].unsqueeze(2).to_broadcast([P, TPB, C]), ALU.mult).then_inc(batch_kept, 1)
                dve.wait_ge(batch_kept, b + 1)
                after(pe_steps, "scattered")
                dve.tensor_tensor(z[:, tiles, :], z[:, tiles, :], bank(3, 2).rearrange("p (t c) -> p t c", c=C),
                                  ALU.add).then_inc(batch_done, 1)


def linear_attention(nc, A, xn, z, ident, psum, before):
    H, D, U = 16, 8, TPB
    NORM = float(D) ** -0.25
    FEAT_EPS, DEN_EPS = 1e-6, 1e-6
    with ExitStack() as ctx:
        def sb(name, shape):
            return ctx.enter_context(nc.sbuf_tensor("l_" + name, shape, F32))

        def sem(name):
            return ctx.enter_context(nc.semaphore("l_" + name))

        wT = sb("wT", [P, 4, P])
        feat = sb("feat", [P, P])
        head_cols = sb("head_cols", [P, H])
        block_mask = sb("block_mask", [P, P])
        bias_cols = sb("bias_cols", [P, 2])
        bias_rows = sb("bias_rows", [P, 2, P])
        bias_norm = sb("bias_norm", [P, 2])
        x_in = sb("x_in", [P, 2, C])
        xT = sb("xT", [P, 2, P])
        q_s, k_s = sb("q_s", [P, 2, P]), sb("k_s", [P, 2, P])
        v_s = sb("v_s", [P, 2, P + 1])
        q_feat = sb("q_feat", [P, U, P])
        k_feat = sb("k_feat", [P, 2, P])
        kv = sb("kv", [P, P + H])
        ksum = sb("ksum", [P, 1])
        den = sb("den", [P, H])
        rden = sb("rden", [P, H])
        o_s = sb("o_s", [P, 2, P])
        oT = sb("oT", [P, 2, P])

        XB, QB, KB, VB, FBK, KVB, NB, OB = [psum[:, n, :] for n in range(8)]

        loaded, held, ready = sem("loaded"), sem("held"), sem("ready")
        x_turned, qkv_done, feat_done, kv_done, num_done, out_done = (
            sem("x_turned"), sem("qkv_done"), sem("feat_done"), sem("kv_done"), sem("num_done"), sem("out_done"))
        act_a, act_b = sem("act_a"), sem("act_b")
        z_in = sem("z_in")
        v_in, feat_in, dve_kv, dve_b = sem("v_in"), sem("feat_in"), sem("dve_kv"), sem("dve_b")
        staged = sem("staged")
        PER = {x_turned: 1, qkv_done: 3, feat_done: 2, kv_done: 1, num_done: 1, out_done: 2, act_a: 3, act_b: 1, v_in: 1, feat_in: 2, dve_b: 3, z_in: 1, staged: 1}

        def at(s, it, k, back=0):
            return s, reached(it, PER[s], k, back, 2 * SEED)

        def seed(eng, sems):
            for s in sems:
                eng.sem_inc(s, PER[s] * 2 * SEED)

        with nc.Block() as load_block:
            @load_block.gpsimd
            def _(pool):
                pool.memset(feat[:], 0.0).then_inc(ready, 1)
                pool.memset(v_s[:], 1.0).then_inc(ready, 1)

            @load_block.sync
            def _(sp):
                sp.dma_start(wT[:], A["la_wT"]).then_inc(loaded, 16)
                sp.dma_start(bias_cols[:], A["la_bias_cols"]).then_inc(loaded, 16)
                sp.dma_start(bias_rows[:], A["la_bias_rows"].partition_broadcast(P)).then_inc(loaded, 16)
                sp.dma_start(head_cols[:], A["head_cols"]).then_inc(loaded, 16)
                sp.dma_start(block_mask[:], A["head_blocks"]).then_inc(loaded, 16)
                sp.wait_ge(ready, 2)
                for h in range(H):
                    sp.dma_start(feat[D * h:D * h + D, D * h:D * h + D], A["la_PT"]).then_inc(loaded, 16)

        before()
        block = ctx.enter_context(nc.Block())

        @block.gpsimd
        def _(pool):
            seed(pool, [staged])

            def stage(it):
                pool.wait_ge(*at(x_turned, it, 1, 2))
                pool.sem_inc(held, 1)
                pool.tensor_copy(x_in[:, it.slot % 2, :].unsqueeze(1), xn[:, bass.ds(it.t, 1), :]).then_inc(staged, 1)
            pipeline(pool, 0, NT, U, [(0, stage)])

        @block.tensor
        def _(pe):
            seed(pe, [x_turned, qkv_done, feat_done, kv_done, num_done, out_done])
            pe.wait_ge(loaded, 80 + 16 * H)
            pe.wait_ge(ready, 4)

            def turn_x(it):
                u = it.slot % 2
                pe.wait_ge(*at(staged, it, 1))
                pe.wait_ge(*at(act_a, it, 1, 1))
                pe.transpose(XB[:, 0:P], x_in[:, u, :], ident[:]).then_inc(x_turned, 1)

            def qkv(it):
                u = it.slot % 2
                pe.wait_ge(*at(act_a, it, 1))
                pe.wait_ge(*at(act_a, it, 3, 1))
                pe.wait_ge(*at(v_in, it, 1, 1))
                pe.matmul(QB[:, 0:P], wT[:, 0, :], xT[:, u, :], start=True, stop=True).then_inc(qkv_done, 1)
                pe.matmul(KB[:, 0:P], wT[:, 1, :], xT[:, u, :], start=True, stop=True).then_inc(qkv_done, 1)
                pe.matmul(VB[:, 0:P], xT[:, u, :], wT[:, 2, :], start=True, stop=True).then_inc(qkv_done, 1)

            def features(it):
                u = it.slot % 2
                pe.wait_ge(*at(feat_in, it, 2, 1))
                pe.wait_ge(*at(act_a, it, 3))
                pe.matmul(FBK[:, 0:P], feat[:], q_s[:, u, :], start=True, stop=True).then_inc(feat_done, 1)
                pe.matmul(FBK[:, P:2 * P], k_s[:, u, :], feat[:], start=True, stop=True).then_inc(feat_done, 1)

            def sum_kv(it):
                u = it.slot % 2
                pe.wait_ge(*at(feat_in, it, 2))
                if it.slot == 0:
                    pe.wait_ge(dve_kv, (it.turn + 1) * 3)
                pe.matmul(KVB[:, 0:P + 1], k_feat[:, u, :], v_s[:, u, :], start=(it.slot == 0),
                          stop=(it.slot == U - 1)).then_inc(kv_done, 1)

            def numerators(it):
                if it.slot == 0:
                    pe.wait_ge(dve_kv, (it.turn + 2) * 3)
                pe.wait_ge(*at(dve_b, it, 3, 1))
                pe.matmul(NB[:, 0:P + H], q_feat[:, it.slot, :], kv[:], start=True, stop=True).then_inc(num_done, 1)

            def turn_o(it):
                u = it.slot % 2
                pe.wait_ge(*at(dve_b, it, 3))
                pe.wait_ge(*at(z_in, it, 1, 1))
                pe.transpose(OB[:, 0:P], o_s[:, u, :], ident[:]).then_inc(out_done, 1)

            def project(it):
                pe.wait_ge(*at(act_b, it, 1))
                pe.matmul(OB[:, 0:P], oT[:, it.slot % 2, :], wT[:, 3, :], start=True, stop=True).then_inc(out_done, 1)

            pipeline(pe, 0, NT, U, [(9, numerators), (0, turn_x), (10, turn_o), (1, features), (0, qkv),
                                    (1, sum_kv), (10, project)])

        @block.scalar
        def _(act):
            seed(act, [act_a, act_b])
            act.wait_ge(loaded, 80 + 16 * H)
            act.activation(bias_norm[:], bias_cols[:], ACT.Copy, scale=NORM).then_inc(ready, 1)
            act.wait_ge(ready, 4)

            def take_x(it):
                act.wait_ge(*at(x_turned, it, 1))
                act.wait_ge(*at(qkv_done, it, 3, 2))
                act.activation(xT[:, it.slot % 2, :], XB[:, 0:P], ACT.Copy).then_inc(act_a, 1)

            def take_qk(it):
                u = it.slot % 2
                act.wait_ge(*at(feat_done, it, 2, 2))
                act.wait_ge(*at(qkv_done, it, 1))
                act.activation(q_s[:, u, :], QB[:, 0:P], ACT.Identity, scale=NORM, bias=bias_norm[:, 0:1]).then_inc(act_a, 1)
                act.wait_ge(*at(qkv_done, it, 2))
                act.activation(k_s[:, u, :], KB[:, 0:P], ACT.Identity, scale=NORM, bias=bias_norm[:, 1:2]).then_inc(act_a, 1)

            def take_o(it):
                act.wait_ge(*at(out_done, it, 1))
                act.wait_ge(*at(out_done, it, 2, 2))
                act.activation(oT[:, it.slot % 2, :], OB[:, 0:P], ACT.Copy).then_inc(act_b, 1)

            pipeline(act, 0, NT, U, [(0, take_x), (10, take_o), (0, take_qk)])

        @block.vector
        def _(dve):
            seed(dve, [v_in, feat_in, dve_b, z_in])
            dve.sem_inc(dve_kv, 3)
            dve.wait_ge(loaded, 80 + 16 * H)
            dve.sem_inc(ready, 1)

            def take_v(it):
                u = it.slot % 2
                dve.wait_ge(*at(qkv_done, it, 3))
                dve.wait_ge(*at(kv_done, it, 1, 2))
                dve.tensor_tensor(v_s[:, u, 0:P], VB[:, 0:P], bias_rows[:, 0, :], ALU.add).then_inc(v_in, 1)

            def take_features(it):
                u = it.slot % 2
                dve.wait_ge(*at(feat_done, it, 2))
                dve.wait_ge(*at(num_done, it, 1, 8))
                dve.tensor_scalar(q_feat[:, it.slot, :], FBK[:, 0:P], 0.0, FEAT_EPS, ALU.max, ALU.add).then_inc(feat_in, 1)
                dve.wait_ge(*at(kv_done, it, 1, 2))
                dve.tensor_scalar(k_feat[:, u, :], FBK[:, P:2 * P], 0.0, FEAT_EPS, ALU.max, ALU.add).then_inc(feat_in, 1)
                if it.slot == U - 1:
                    dve.wait_ge(*at(kv_done, it, 1))
                    dve.wait_ge(*at(num_done, it, 1, 8))
                    dve.tensor_copy(ksum[:], KVB[:, P:P + 1]).then_inc(dve_kv, 1)
                    dve.tensor_tensor(kv[:, 0:P], KVB[:, 0:P], block_mask[:],
                                      ALU.mult).then_inc(dve_kv, 1)
                    dve.wait_ge(dve_kv, it.turn * 3 + 5)
                    dve.tensor_scalar(kv[:, P:P + H], head_cols[:], ksum[:], None, ALU.mult).then_inc(dve_kv, 1)

            def divide(it):
                u = it.slot % 2
                dve.wait_ge(*at(num_done, it, 1))
                dve.tensor_scalar(den[:], NB[:, P:P + H], DEN_EPS, None, ALU.add).then_inc(dve_b, 1)
                dve.wait_ge(*at(dve_b, it, 1))
                dve.reciprocal(rden[:], den[:]).then_inc(dve_b, 1)
                dve.wait_ge(*at(dve_b, it, 2))
                dve.wait_ge(*at(out_done, it, 1, 2))
                dve.tensor_tensor(o_s[:, u, :].rearrange("p (h d) -> p h d", h=H),
                                  NB[:, 0:P].rearrange("p (h d) -> p h d", h=H),
                                  rden[:].unsqueeze(2).to_broadcast([P, H, D]), ALU.mult).then_inc(dve_b, 1)

            def take_z(it):
                dve.wait_ge(*at(out_done, it, 2))
                dve.tensor_tensor(z[:, bass.ds(it.t, 1), :].rearrange("p o c -> p (o c)"), OB[:, 0:P],
                                  bias_rows[:, 1, :], ALU.add).then_inc(z_in, 1)

            pipeline(dve, 0, NT, U, [(9, divide), (1, take_features), (0, take_v), (10, take_z)])
            dve.wait_ge(*at(z_in, Item(NT), 0))


FF = 341
FCH = [(0, 128), (128, 128), (256, FF - 256)]
QK_SCALE = 8.0
QKV_ORDER = [0, 2, 1, 3, 4, 5]
TURN_ORDER = [0, 2, 1, 3]
RSQRT_SEED = float(0x5F3759DF - (1 << 22) - (1 << 31))


def local_transformer(nc, A, Y, ident, psum, before):
    U, GROUP = 8, 4
    UNITS = DEPTH * NT
    GROUPS_PER_LAYER = NT // GROUP
    with ExitStack() as ctx:
        def sb(name, shape, dt=F32):
            return ctx.enter_context(nc.sbuf_tensor(name, shape, dt))

        def sem(name):
            return ctx.enter_context(nc.semaphore(name))

        w_high, w_low = sb("w_high", [P, QKV]), sb("w_low", [P, QKV])
        w_out = sb("w_out", [P, 8, C])
        w_up = sb("w_up", [P, 2 * FF])
        w_down = sb("w_down", [P, 3, C])
        cols = sb("cols", [P, 8])
        bias_row = sb("bias_row", [P, C])
        scales = sb("scales", [P, 4 * HD])
        rope_base = sb("rope_base", [P, TPB, 4, HD])
        rope = sb("rope", [P, 2, 4, HD])
        mask = sb("mask", [P, TPB, 2 * WIN])
        keep_carry = sb("keep_carry", [P, TPB])
        minus_half = sb("minus_half", [P, GROUP])
        y_in = sb("y_in", [P, GROUP, C])
        shifted = sb("shifted", [P, 1, GROUP * P + 1])
        x_high, x_low = sb("x_high", [P, 2, GROUP * P], F32R), sb("x_low", [P, 2, GROUP * P], F32R)
        squares = sb("squares", [P, 4, 512])
        rotated = sb("rotated", [P, 2, 512])
        qk = sb("qk", [P, 4, 4, 512])
        ss = sb("ss", [P, 2, 32])
        rs_a = sb("rs_a", [P, 32])
        rs_b = sb("rs_b", [P, 32])
        rs_y = sb("rs_y", [P, 2, 32])
        qT = sb("qT", [P, 8, P])
        kT = sb("kT", [P, 2, 8, WIN + P])
        V = sb("V", [P, 4, INNER])
        sc = sb("sc", [P, 2, 2, 512])
        mx = sb("mx", [P, 2, HEADS])
        sm = sb("sm", [P, 2, HEADS])
        rsum = sb("rsum", [P, 2, HEADS])
        pT = sb("pT", [P, HEADS, P])
        pT_prev = sb("pT_prev", [P, HEADS, WIN])
        oT = sb("oT", [P, 8, P])
        y1 = sb("y1", [P, 2, GROUP, C])
        f_shift = sb("f_shift", [P, 2, GROUP * P + 1])
        stats = sb("stats", [P, GROUP, 6])
        mv = sb("mv", [P, GROUP, 2])
        rstd = sb("rstd", [P, GROUP])
        veps = sb("veps", [P, GROUP])
        xn = sb("xn", [P, GROUP, C])
        xg = sb("xg", [P, GROUP * P])
        gate = sb("gate", [P, 3, GROUP * P])

        ATT = [psum[:, 0, :], psum[:, 1, :]]
        TR = psum[:, 2:4, :]
        SC = [psum[:, 4, :], psum[:, 5, :]]
        OB = psum[:, 6, :]
        FB = psum[:, 7, :]
        HID_BANKS = [SC[0], SC[1], OB]

        consts = sem("consts")
        zeroed = sem("zeroed")
        held = sem("held")
        scales_in, w_out_in, w_up_in, w_down_in, cols_in, bias_in = (
            sem("scales_in"), sem("w_out_in"), sem("w_up_in"), sem("w_down_in"), sem("cols_in"), sem("bias_in"))
        w_qkv_in = [sem(f"w_qkv_{c}_in") for c in range(6)]
        projected, qk_turned, scored = sem("projected"), sem("qk_turned"), sem("scored")
        p_turned, attended, out_projected = sem("p_turned"), sem("attended"), sem("out_projected")
        x_turned, y1_turned, shift_turned, xn_turned, gates_done, ups_done, down_done = (
            sem("x_turned"), sem("y1_turned"), sem("shift_turned"), sem("xn_turned"), sem("gates_done"),
            sem("ups_done"), sem("down_done"))
        squared, v_in, qk_in, k_prev, exped, p_spread_a, o_in = (
            sem("squared"), sem("v_in"), sem("qk_in"), sem("k_prev"), sem("exped"), sem("p_spread_a"), sem("o_in"))
        x_shifted, y1_shifted, gained, gelu_done = sem("x_shifted"), sem("y1_shifted"), sem("gained"), sem("gelu_done")
        high_taken, low_taken = sem("high_taken"), sem("low_taken")
        roped, ss_done, rs_step, masked, maxed = sem("roped"), sem("ss_done"), sem("rs_step"), sem("masked"), sem("maxed")
        summed, inverted, p_spread_d, y1_done = sem("summed"), sem("inverted"), sem("p_spread_d"), sem("y1_done")
        stats_step, xn_done, gated, y_done = sem("stats_step"), sem("xn_done"), sem("gated"), sem("y_done")
        table_made, rope_added, qk_normed, shifted_max, p_scaled = (
            sem("table_made"), sem("rope_added"), sem("qk_normed"), sem("shifted_max"), sem("p_scaled"))
        staged, rstd_done, biased = sem("staged"), sem("rstd_done"), sem("biased")
        TILE_PER = {projected: 6, qk_turned: 4, scored: 2, p_turned: 1, attended: 2, out_projected: 1,
                    squared: 4, v_in: 2, qk_in: 4, k_prev: 1, exped: 2, p_spread_a: 6, o_in: 2,
                    roped: 8, ss_done: 4, rs_step: 12, masked: 2, maxed: 2, summed: 2, inverted: 2, p_spread_d: 6,
                    y1_done: 1, table_made: 1, rope_added: 4, qk_normed: 4, shifted_max: 2, p_scaled: 2}
        GROUP_PER = {x_turned: 1, y1_turned: 1, shift_turned: 1, xn_turned: 1, gates_done: 3, ups_done: 3,
                     down_done: 1, x_shifted: 3, y1_shifted: 3, gained: 1, gelu_done: 3, high_taken: 1, low_taken: 1, stats_step: 10, xn_done: 4,
                     gated: 3, y_done: 1, staged: 1, rstd_done: 1, biased: 1}
        GROUP_SEED = GROUPS_PER_LAYER + 1

        def seed(eng, sems):
            for s in sems:
                eng.sem_inc(s, TILE_PER[s] * SEED if s in TILE_PER else GROUP_PER[s] * GROUP_SEED)

        def at(s, it, k, back=0):
            return s, reached(it, TILE_PER[s], k, back)

        def at_group(s, it, k, back=0):
            return s, (it.turn * (U // GROUP) + (it.slot // GROUP + GROUP_SEED - back)) * GROUP_PER[s] + k

        def loads(s, it, per=1):
            return s, (it.t // NT + 1) * (16 * per)

        def by_group(do):
            return lambda it: do(it) if it.slot % GROUP == 0 else None

        def spread(copy, it, sub, s):
            src = TR.rearrange("p c (a q) -> p c a q", a=4)
            dst = pT[:].rearrange("p (a s c) q -> p s c a q", s=2, c=2)
            prv = pT_prev[:].rearrange("p (a s c) q -> p s c a q", s=2, c=2)
            o = 64 * sub
            args = [ACT.Copy] if s is p_spread_a else []
            for d0, d1, s0, s1, j in [(0, 64, 0, 64, 1), (64, 128, 0, 64, 3), (32, 64, 0, 32, 2), (64, 96, 32, 64, 2),
                                      (0, 32, 32, 64, 0)]:
                q = slice(32 * j, 32 * j + 32)
                copy(dst[d0:d1, sub, :, :, q], src[o + s0:o + s1, :, :, q], *args).then_inc(s, 1)
            copy(prv[96:128, sub, :, :, :], src[o:o + 32, :, :, 0:32], *args).then_inc(s, 1)

        def load_scales(sp, l):
            sp.dma_start(scales[:], A["rows"][l, P:].partition_broadcast(P)).then_inc(scales_in, 16)

        def load_qkv(sp, l, c):
            w = QKV_ORDER[c] * 512
            sp.dma_start(w_high[:, w:w + 512], A["Wqkv_high"][l, :, w:w + 512]).then_inc(w_qkv_in[c], 16)
            sp.dma_start(w_low[:, w:w + 512], A["Wqkv_low"][l, :, w:w + 512]).then_inc(w_qkv_in[c], 16)

        def load_out(sp, l):
            sp.dma_start(w_out[:], A["Wo"][l].rearrange("(h p) c -> p h c", p=P)).then_inc(w_out_in, 16)

        def load_bias(sp, l):
            sp.dma_start(bias_row[:], A["rows"][l, 0:P].partition_broadcast(P)).then_inc(bias_in, 16)

        def load_up(sp, l):
            sp.dma_start(w_up[:], A["W1"][l]).then_inc(w_up_in, 16)

        def load_cols(sp, l):
            sp.dma_start(cols[:], A["cols"][l]).then_inc(cols_in, 16)

        def load_down(sp, l):
            sp.dma_start(w_down[:, 0:2, :], A["W2"][l, 0:256].rearrange("(h p) c -> p h c", p=P)).then_inc(w_down_in, 16)
            sp.dma_start(w_down[0:FF - 256, 2, :], A["W2"][l, 256:FF]).then_inc(w_down_in, 16)

        with nc.Block() as load_block:
            @load_block.sync
            def _(sp):
                load_scales(sp, 0)
                sp.dma_start(rope_base[:], A["rope_base"]).then_inc(consts, 16)
                sp.dma_start(keep_carry[:], A["keep_carry"]).then_inc(consts, 16)
                sp.dma_start(mask[:], A["win_mask"]).then_inc(consts, 16)
                for c in range(6):
                    load_qkv(sp, 0, c)
                load_out(sp, 0)
                load_bias(sp, 0)
                load_cols(sp, 0)
                load_up(sp, 0)
                load_down(sp, 0)

            @load_block.vector
            def _(dve):
                for buf in (pT, shifted, f_shift, y1):
                    dve.memset(buf[:], 0.0).then_inc(zeroed, 1)
                dve.memset(minus_half[:], -0.5).then_inc(zeroed, 1)

            @load_block.gpsimd
            def _(pool):
                for buf in (V, kT):
                    pool.memset(buf[:], 0.0).then_inc(zeroed, 1)

        before()
        block = ctx.enter_context(nc.Block())

        @block.sync
        def _(sp):
            with sp.Fori(0, DEPTH - 1, 1) as l:
                nxt = Item(l * NT + NT, turn=(l + 1) * (NT // U))
                sp.wait_ge(*at(table_made, nxt, 0))
                sp.sem_inc(held, 1)
                load_scales(sp, l + 1)
                for c in range(6):
                    sp.wait_ge(*at(projected, nxt, c + 1, 1))
                    sp.sem_inc(held, 1)
                    load_qkv(sp, l + 1, c)
                sp.wait_ge(*at(out_projected, nxt, 0))
                sp.sem_inc(held, 1)
                load_out(sp, l + 1)
                sp.wait_ge(*at_group(biased, nxt, 0))
                sp.sem_inc(held, 1)
                load_bias(sp, l + 1)
                sp.wait_ge(*at_group(ups_done, nxt, 0))
                sp.sem_inc(held, 1)
                load_up(sp, l + 1)
                sp.wait_ge(*at_group(gated, nxt, 0))
                sp.sem_inc(held, 1)
                load_cols(sp, l + 1)
                sp.wait_ge(*at_group(down_done, nxt, 0))
                sp.sem_inc(held, 1)
                load_down(sp, l + 1)

        @block.tensor
        def _(pe):
            seed(pe, [projected, qk_turned, scored, p_turned, attended, out_projected,
                      x_turned, y1_turned, shift_turned, xn_turned, gates_done, ups_done, down_done])

            def turn_x(it):
                pe.wait_ge(*at_group(staged, it, 1))
                pe.wait_ge(*at(y1_done, it, 1, 6))
                pe.wait_ge(*at_group(x_shifted, it, 3, 1))
                for j in range(GROUP):
                    m = pe.transpose(FB[:, j * P:(j + 1) * P], y_in[:, j, :], ident[:])
                m.then_inc(x_turned, 1)

            def project(c):
                def do(it):
                    pe.wait_ge(*loads(w_qkv_in[c], it, 2))
                    if c == 0:
                        pe.wait_ge(*at_group(low_taken, it, 1))
                    if c < 2:
                        pe.wait_ge(*at(v_in, it, c + 1, 1))
                    else:
                        pe.wait_ge(*at(roped, it, 2 * (c - 2) + 2))
                    w, x = QKV_ORDER[c] * 512, it.slot % GROUP * P
                    g = it.slot // GROUP
                    xh, xl = x_high[:, g, x:x + P], x_low[:, g, x:x + P]
                    wh, wl = w_high[:, w:w + 512].bitcast(F32R), w_low[:, w:w + 512].bitcast(F32R)
                    pe.matmul(ATT[c % 2], xh, wl, start=True, stop=False)
                    pe.matmul(ATT[c % 2], xl, wh, start=False, stop=False)
                    pe.matmul(ATT[c % 2], xh, wh, start=False, stop=True).then_inc(projected, 1)
                return do

            def turn_qk(n):
                def do(it):
                    pe.wait_ge(*at(qk_normed, it, n + 1))
                    if n < 2:
                        pe.wait_ge(*at(p_spread_a, it, 6, 2))
                        pe.wait_ge(*at(p_spread_d, it, 6, 2))
                        pe.wait_ge(*at(qk_in, it, 3 + n, 1))
                    else:
                        pe.wait_ge(*at(qk_in, it, n - 1))
                    for j in range(4):
                        m = pe.transpose(TR[:, n % 2, j * P:(j + 1) * P],
                                         qk[:, it.slot % 4, TURN_ORDER[n], j * P:(j + 1) * P], ident[:])
                    m.then_inc(qk_turned, 1)
                return do

            def score(s):
                def do(it):
                    if s == 0:
                        pe.wait_ge(*at(qk_in, it, 4))
                        pe.wait_ge(*at(k_prev, it, 1))
                    pe.wait_ge(*at(masked, it, s + 1, 1))
                    if it.slot % GROUP == 3:
                        pe.wait_ge(*at_group(gelu_done, it, s + 1, 1))
                    if it.slot % GROUP == 0:
                        pe.wait_ge(*at_group(gated, it, s + 1, 2))
                    pe.sem_inc(held, 1)
                    r = slice(64 * s, 64 * s + 64)
                    for pr in range(8):
                        for j in range(4):
                            m = pe.matmul(SC[s][32 * j:32 * j + 32, pr * 64:pr * 64 + 64],
                                          qT[r, pr, 32 * j:32 * j + 32],
                                          kT[r, it.slot % 2, pr, 32 * j:32 * j + 64],
                                          start=True, stop=True, tile_position=(64 * s, 32 * j))
                    m.then_inc(scored, 1)
                return do

            def turn_p(it):
                for c in range(2):
                    pe.wait_ge(*at(p_scaled, it, c + 1))
                    if c == 0 and it.has(1):
                        pe.wait_ge(*at(qk_in, it, 4, -1))
                    elif c == 0:
                        pe.wait_ge(*at(p_spread_a, it, 6, 1))
                        pe.wait_ge(*at(p_spread_d, it, 6, 1))
                    for j in range(4):
                        m = pe.transpose(TR[:, c, j * P:(j + 1) * P], sc[:, it.slot % 2, c, j * P:(j + 1) * P], ident[:])
                m.then_inc(p_turned, 1)

            def attend(c):
                def do(it):
                    if c == 0:
                        pe.wait_ge(*at(p_spread_a, it, 6))
                        pe.wait_ge(*at(p_spread_d, it, 6))
                        pe.wait_ge(*at(v_in, it, 2))
                        if it.slot % GROUP == 2:
                            pe.wait_ge(*at_group(gelu_done, it, 3, 1))
                        if it.slot % GROUP == 3:
                            pe.wait_ge(*at_group(gated, it, 3, 1))
                    pe.wait_ge(*at(o_in, it, c))
                    for j in range(4):
                        for par in range(2):
                            h = 8 * c + 2 * j + par
                            pe.matmul(OB[64 * par:64 * par + 64, j * P:(j + 1) * P],
                                      V[:, it.slot % 4, h * HD:(h + 1) * HD], pT[:, h, :],
                                      start=True, stop=False, tile_position=(0, 64 * par))
                        for par in range(2):
                            h = 8 * c + 2 * j + par
                            m = pe.matmul(OB[64 * par:64 * par + 64, j * P:j * P + WIN],
                                          V[96:128, (it.slot - 1) % 4, h * HD:(h + 1) * HD],
                                          pT_prev[96:128, h, :],
                                          start=False, stop=True, tile_position=(96, 64 * par))
                    m.then_inc(attended, 1)
                return do

            def project_out(it):
                pe.wait_ge(*loads(w_out_in, it))
                pe.wait_ge(*at(o_in, it, 2))
                pe.wait_ge(*at(y1_done, it, 1, 1))
                if it.slot % GROUP == 0:
                    pe.wait_ge(*at_group(y1_shifted, it, 3, 1))
                if it.slot % GROUP == 1:
                    pe.wait_ge(*at_group(gained, it, 1, 1))
                if it.slot % GROUP == 3 and it.has(5):
                    pe.wait_ge(*at_group(x_shifted, it, 3, -2))
                for j in range(8):
                    m = pe.matmul(FB[:, 0:C], oT[:, j, :], w_out[:, j, :], start=(j == 0), stop=(j == 7))
                m.then_inc(out_projected, 1)

            def turn_y1(it):
                pe.wait_ge(*at(y1_done, it, 1, -3))
                pe.wait_ge(*at_group(y_done, it, 1, 1))
                for j in range(GROUP):
                    m = pe.transpose(FB[:, j * P:(j + 1) * P], y1[:, it.slot // GROUP, j, :], ident[:])
                m.then_inc(y1_turned, 1)

            def turn_shifted(it):
                pe.wait_ge(*at_group(y1_shifted, it, 3))
                if it.has(4):
                    pe.wait_ge(*at(y1_done, it, 1, -4))
                for j in range(GROUP):
                    m = pe.transpose(FB[:, j * P:(j + 1) * P], f_shift[:, it.slot // GROUP, j * P:(j + 1) * P], ident[:])
                m.then_inc(shift_turned, 1)

            def turn_xn(it):
                pe.wait_ge(*at_group(xn_done, it, 4))
                for j in range(GROUP):
                    m = pe.transpose(FB[:, j * P:(j + 1) * P], xn[:, j, :], ident[:])
                m.then_inc(xn_turned, 1)

            def gates(it):
                pe.wait_ge(*loads(w_up_in, it))
                pe.wait_ge(*at_group(gained, it, 1))
                pe.wait_ge(*at_group(gated, it, 3, 1))
                if it.has(6):
                    pe.wait_ge(*at(masked, it, 2, -6))
                    pe.wait_ge(*at(o_in, it, 2, -5))
                for c, (f, w) in enumerate(FCH):
                    pe.matmul(HID_BANKS[c][0:w, :], w_up[:, FF + f:FF + f + w], xg[:], start=True,
                              stop=True).then_inc(gates_done, 1)

            def ups(it):
                if it.has(7):
                    pe.wait_ge(*at(masked, it, 2, -7))
                    pe.wait_ge(*at(o_in, it, 2, -6))
                for c, (f, w) in enumerate(FCH):
                    pe.wait_ge(*at_group(gelu_done, it, c + 1))
                    pe.matmul(HID_BANKS[c][0:w, :], w_up[:, f:f + w], xg[:], start=True, stop=True).then_inc(ups_done, 1)

            def down(it):
                pe.wait_ge(*loads(w_down_in, it, 2))
                if it.has(7):
                    pe.wait_ge(*at(y1_done, it, 1, -7))
                pe.wait_ge(*at_group(gated, it, 3))
                for j in range(GROUP):
                    for c, (f, w) in enumerate(FCH):
                        m = pe.matmul(FB[:, j * P:(j + 1) * P], gate[0:w, c, j * P:(j + 1) * P], w_down[0:w, c, :],
                                      start=(c == 0), stop=(c == 2))
                m.then_inc(down_done, 1)

            pe.wait_ge(zeroed, 7)
            pipeline(pe, 0, UNITS, U, [
                (3, project(2)), (10, by_group(turn_y1)), (6, turn_p), (5, score(0)), (5, score(1)), (3, project(3)),
                (6, attend(0)), (3, project(4)), (6, attend(1)), (11, by_group(turn_xn)), (3, project(5)),
                (2, project(0)), (6, project_out), (4, turn_qk(0)), (2, project(1)), (10, by_group(turn_shifted)),
                (12, by_group(ups)), (4, turn_qk(1)), (13, by_group(down)), (4, turn_qk(2)), (0, by_group(turn_x)),
                (4, turn_qk(3)), (11, by_group(gates))])

        @block.scalar
        def _(act):
            seed(act, [squared, v_in, qk_in, k_prev, exped, p_spread_a, o_in, x_shifted, y1_shifted, gained, gelu_done, high_taken])

            def shift_in(buf, ring, turned, read, out_sem):
                def do(it):
                    g = it.slot // GROUP % ring
                    act.wait_ge(*at_group(turned, it, 1))
                    act.wait_ge(*read(it))
                    act.wait_ge(*at_group(out_sem, it, 3, 1))
                    act.activation(buf[64:P, g, 0:1], buf[64:P, (g - 1) % ring, GROUP * P:GROUP * P + 1], ACT.Identity,
                                   scale=keep_carry[64:P, bass.ds(it.t % TPB, 1)]).then_inc(out_sem, 1)
                    act.activation(buf[0:64, g, 0:GROUP * P], FB[0:64, :], ACT.Copy).then_inc(out_sem, 1)
                    act.wait_ge(*at_group(out_sem, it, 1))
                    act.activation(buf[64:P, g, 1:GROUP * P + 1], FB[64:P, :], ACT.Copy).then_inc(out_sem, 1)
                return do

            shift_x = shift_in(shifted, 1, x_turned, lambda it: at_group(low_taken, it, 1, 1), x_shifted)
            shift_y1 = shift_in(f_shift, 2, y1_turned, lambda it: at_group(shift_turned, it, 1, 2), y1_shifted)

            def take_high(it):
                g = it.slot // GROUP
                act.wait_ge(*at_group(x_shifted, it, 3))
                act.wait_ge(*at(projected, it, 6, 5))
                act.activation(x_high[:, g, :], shifted[:, 0, 0:GROUP * P], ACT.Copy).then_inc(high_taken, 1)

            def square(c):
                def do(it):
                    act.wait_ge(*at(projected, it, c + 1))
                    act.wait_ge(*at(ss_done, it, c + 1, 1))
                    act.activation(squares[:, c, :], ATT[c % 2], ACT.Square).then_inc(squared, 1)
                return do

            def take_v(c):
                def do(it):
                    act.wait_ge(*at(projected, it, 5 + c))
                    act.wait_ge(*at(attended, it, 2, 3))
                    act.activation(V[:, it.slot % 4, 512 * c:512 * c + 512], ATT[c], ACT.Copy).then_inc(v_in, 1)
                return do

            def carry_k(it):
                b = it.slot % 2
                act.wait_ge(*at(scored, it, 2, 2))
                act.wait_ge(*at(qk_in, it, 4, 1))
                act.wait_ge(*at(k_prev, it, 1, 1))
                act.sem_inc(held, 1)
                act.activation(kT[:, b, :, 0:WIN], kT[:, 1 - b, :, P:P + WIN], ACT.Identity,
                               scale=keep_carry[:, bass.ds(it.t % TPB, 1)]).then_inc(k_prev, 1)

            def take_qk(n):
                def do(it):
                    if n == 0:
                        act.wait_ge(*at(scored, it, 2, 1))
                    act.wait_ge(*at(qk_turned, it, n + 1))
                    dst = qT[:, 4 * n:4 * n + 4, :] if n < 2 else kT[:, it.slot % 2, 4 * n - 8:4 * n - 4, WIN:]
                    act.activation(dst, TR[:, n % 2, :].rearrange("p (a q) -> p a q", a=4), ACT.Copy).then_inc(qk_in, 1)
                return do

            def exps(c):
                def do(it):
                    act.wait_ge(*at(shifted_max, it, c + 1))
                    s = sc[:, it.slot % 2, c, :]
                    act.activation(s, s, ACT.Exp).then_inc(exped, 1)
                return do

            def spread_a(it):
                act.wait_ge(*at(p_turned, it, 1))
                act.wait_ge(*at(attended, it, 2, 1))
                spread(act.activation, it, 0, p_spread_a)

            def take_o(c):
                def do(it):
                    act.wait_ge(*at(out_projected, it, 1, 1))
                    act.wait_ge(*at(attended, it, c + 1))
                    act.activation(oT[:, 4 * c:4 * c + 4, :],
                                   OB.rearrange("p (a q) -> p a q", a=4), ACT.Copy).then_inc(o_in, 1)
                return do

            def gain(it):
                act.wait_ge(*loads(cols_in, it))
                act.wait_ge(*at_group(xn_turned, it, 1))
                act.wait_ge(*at_group(ups_done, it, 3, 1))
                act.activation(xg[:], FB, ACT.Identity, scale=cols[:, 6:7], bias=cols[:, 7:8]).then_inc(gained, 1)

            def gelu(it):
                act.wait_ge(*at_group(down_done, it, 1, 1))
                for c, (f, w) in enumerate(FCH):
                    act.wait_ge(*at_group(gates_done, it, c + 1))
                    act.activation(gate[0:w, c, :], HID_BANKS[c][0:w, :], ACT.Gelu,
                                   bias=cols[0:w, 3 + c:4 + c]).then_inc(gelu_done, 1)

            act.wait_ge(consts, 48)
            act.wait_ge(zeroed, 7)
            pipeline(act, 0, UNITS, U, [
                (6, spread_a), (10, by_group(shift_y1)), (3, square(2)), (3, square(3)), (5, exps(0)),
                (6, take_o(0)), (3, take_v(0)), (6, take_o(1)), (11, by_group(gain)), (5, exps(1)), (3, take_v(1)),
                (2, square(0)), (2, square(1)), (4, take_qk(0)), (4, carry_k), (4, take_qk(1)), (4, take_qk(2)),
                (4, take_qk(3)), (11, by_group(gelu)), (0, by_group(shift_x)), (0, by_group(take_high))])

        @block.vector
        def _(dve):
            seed(dve, [roped, ss_done, rs_step, masked, maxed, summed, inverted, p_spread_d, y1_done,
                       stats_step, xn_done, gated, y_done])

            def rotate(c, half):
                def do(it):
                    table = rope[:, it.slot % 2, 2 * (c % 2):2 * (c % 2) + 2, :].unsqueeze(1)
                    if half == 0:
                        dve.wait_ge(*at(squared, it, c + 1))
                        if c == 0:
                            dve.wait_ge(*at(table_made, it, 1))
                            dve.wait_ge(*at(qk_turned, it, 4, 4))
                        dve.tensor_tensor(qk[:, it.slot % 4, c, :].rearrange("p (h d) -> p h d", h=8),
                                          ATT[c % 2].rearrange("p (h d) -> p h d", h=8),
                                          table[:, :, 0, :].to_broadcast([P, 8, HD]), ALU.mult).then_inc(roped, 1)
                    else:
                        dve.wait_ge(*(at(rope_added, it, c - 1) if c >= 2 else at(rope_added, it, c + 3, 1)))
                        sin = table[:, :, 1, :].to_broadcast([P, 8, HD]).rearrange("p h (r d) -> p h r d", r=2)
                        x = ATT[c % 2].rearrange("p (h r d) -> p h r d", h=8, r=2)
                        dve.tensor_tensor(rotated[:, c % 2, :].rearrange("p (h r d) -> p h r d", h=8, r=2),
                                          x[:, :, ::-1, :], sin, ALU.mult).then_inc(roped, 1)
                return do

            def sum_squares(c):
                def do(it):
                    if c == 0:
                        dve.wait_ge(*at(rs_step, it, 12, 2))
                    dve.wait_ge(*at(squared, it, c + 1))
                    dve.tensor_reduce(ss[:, it.slot % 2, 8 * c:8 * c + 8],
                                      squares[:, c, :].rearrange("p (h d) -> p h d", h=8),
                                      AX.X, ALU.add).then_inc(ss_done, 1)
                return do

            def inverse_norm(n):
                def do(it):
                    b = it.slot % 2
                    half, t, y = ss[:, b, :], rs_a[:], rs_y[:, b, :]
                    if n == 0:
                        dve.wait_ge(*at(ss_done, it, 4))
                        dve.wait_ge(*at(qk_normed, it, 4, 2))
                        i = dve.tensor_scalar(half, half, 1e-24, 0.5, ALU.max, ALU.mult)
                    else:
                        dve.wait_ge(*at(rs_step, it, n))
                        if n == 1:
                            i = dve.tensor_scalar(rs_b[:].bitcast(I32), half.bitcast(I32), 1, None, ALU.logical_shift_right)
                        elif n == 2:
                            i = dve.tensor_scalar(y.bitcast(I32), rs_b[:].bitcast(I32), -1.0, RSQRT_SEED, ALU.mult, ALU.add)
                        elif n % 3 == 0:
                            i = dve.tensor_tensor(t, y, y, ALU.mult)
                        elif n % 3 == 1:
                            i = dve.tensor_tensor(t, t, half, ALU.mult)
                        else:
                            i = dve.scalar_tensor_tensor(out=y, in0=t, scalar=-1.5, in1=y, op0=ALU.add, op1=ALU.mult)
                    i.then_inc(rs_step, 1)
                return do

            def mask_scores(c):
                def do(it):
                    dve.wait_ge(*at(scored, it, c + 1))
                    dve.wait_ge(*at(p_turned, it, 1, 2))
                    m = mask[:, bass.ds(it.t % TPB, 1), :].to_broadcast([P, 8, 2 * WIN])
                    dve.scalar_tensor_tensor(out=sc[:, it.slot % 2, c, :].rearrange("p (h k) -> p h k", h=8),
                                             in0=SC[c].rearrange("p (h k) -> p h k", h=8), scalar=QK_SCALE,
                                             in1=m, op0=ALU.mult, op1=ALU.add).then_inc(masked, 1)
                return do

            def find_max(c):
                def do(it):
                    b = it.slot % 2
                    dve.wait_ge(*at(masked, it, c + 1))
                    dve.wait_ge(*at(shifted_max, it, c + 1, 2))
                    dve.tensor_reduce(mx[:, b, 8 * c:8 * c + 8], sc[:, b, c, :].rearrange("p (h k) -> p h k", h=8),
                                      AX.X, ALU.max).then_inc(maxed, 1)
                return do

            def sum_p(c):
                def do(it):
                    b = it.slot % 2
                    dve.wait_ge(*at(exped, it, c + 1))
                    dve.tensor_reduce(sm[:, b, 8 * c:8 * c + 8], sc[:, b, c, :].rearrange("p (h k) -> p h k", h=8),
                                      AX.X, ALU.add).then_inc(summed, 1)
                return do

            def invert_sum(c):
                def do(it):
                    b, h = it.slot % 2, slice(8 * c, 8 * c + 8)
                    dve.wait_ge(*at(summed, it, c + 1))
                    dve.wait_ge(*at(p_scaled, it, c + 1, 2))
                    dve.reciprocal(rsum[:, b, h], sm[:, b, h]).then_inc(inverted, 1)
                return do

            def spread_d(it):
                dve.wait_ge(*at(p_turned, it, 1))
                dve.wait_ge(*at(attended, it, 2, 1))
                spread(dve.tensor_copy, it, 1, p_spread_d)

            def residual(it):
                dve.wait_ge(*at(out_projected, it, 1))
                dve.wait_ge(*at_group(y_done, it, 1, 2))
                dve.tensor_tensor(y1[:, it.slot // GROUP, it.slot % GROUP, :], FB[:, 0:C],
                                  Y[:, bass.ds(it.t % NT, 1), :].rearrange("p o c -> p (o c)"), ALU.add).then_inc(y1_done, 1)

            def ffn_stats(it):
                dve.wait_ge(*at_group(shift_turned, it, 1))
                dve.wait_ge(*at_group(xn_turned, it, 1, 1))
                dve.tensor_copy(xn[:].rearrange("p t c -> p (t c)"), FB).then_inc(stats_step, 1)
                dve.wait_ge(*at_group(stats_step, it, 1))
                dve.sem_inc(held, 1)
                for j in range(GROUP):
                    dve.bn_stats(stats[:, j, :], xn[:, j, :]).then_inc(stats_step, 1)
                dve.wait_ge(*at_group(stats_step, it, 5))
                dve.sem_inc(held, 1)
                for j in range(GROUP):
                    dve.bn_aggr(mv[:, j, :], stats[:, j, :]).then_inc(stats_step, 1)
                dve.wait_ge(*at_group(stats_step, it, 9))
                dve.tensor_scalar(veps[:], mv[:, :, 1:2].rearrange("p t o -> p (t o)"), 1e-5, None,
                                  ALU.add).then_inc(stats_step, 1)

            def ffn_norm(it):
                dve.wait_ge(*at_group(rstd_done, it, 1))
                for j in range(GROUP):
                    dve.tensor_scalar(xn[:, j, :], xn[:, j, :], mv[:, j, 0:1], rstd[:, j:j + 1],
                                      ALU.subtract, ALU.mult).then_inc(xn_done, 1)

            def ffn_gated(it):
                for c, (f, w) in enumerate(FCH):
                    dve.wait_ge(*at_group(ups_done, it, c + 1))
                    dve.scalar_tensor_tensor(out=gate[0:w, c, :], in0=HID_BANKS[c][0:w, :],
                                             scalar=cols[0:w, c:c + 1], in1=gate[0:w, c, :],
                                             op0=ALU.add, op1=ALU.mult).then_inc(gated, 1)

            def ffn_sum(it):
                dve.wait_ge(*at_group(down_done, it, 1))
                dve.wait_ge(*at_group(biased, it, 1))
                dve.tensor_tensor(Y[:, bass.ds(it.t % NT, GROUP), :], FB.rearrange("p (t c) -> p t c", t=GROUP),
                                  y1[:, it.slot // GROUP, :, :], ALU.add).then_inc(y_done, 1)

            dve.wait_ge(consts, 48)
            dve.wait_ge(zeroed, 7)
            newton = [(4, inverse_norm(n)) for n in range(12)]
            pipeline(dve, 0, UNITS, U, [
                (3, rotate(0, 0)), newton[0], (3, rotate(0, 1)), newton[1], newton[2], (11, by_group(ffn_stats)),
                (3, rotate(1, 0)), (14, by_group(ffn_sum)), newton[3], newton[4], (6, spread_d), newton[5],
                (3, rotate(1, 1)), (5, mask_scores(0)), newton[6], (5, find_max(0)), newton[7], newton[8],
                (3, rotate(2, 0)), (3, rotate(2, 1)), (3, rotate(3, 0)), newton[9], newton[10], (3, rotate(3, 1)),
                (11, by_group(ffn_norm)), newton[11], (5, mask_scores(1)), (5, find_max(1)), (3, sum_squares(0)),
                (3, sum_squares(1)), (5, sum_p(0)), (5, invert_sum(0)), (3, sum_squares(3)), (5, sum_p(1)),
                (3, sum_squares(2)), (5, invert_sum(1)), (6, residual), (12, by_group(ffn_gated))])

        @block.gpsimd
        def _(pool):
            seed(pool, [table_made, rope_added, qk_normed, shifted_max, p_scaled, staged, rstd_done, biased, low_taken])

            def stage(it):
                pool.wait_ge(*at_group(y_done, it, 1, GROUPS_PER_LAYER))
                pool.wait_ge(*at_group(x_turned, it, 1, 1))
                pool.sem_inc(held, 1)
                pool.tensor_copy(y_in[:], Y[:, bass.ds(it.t % NT, GROUP), :]).then_inc(staged, 1)

            def take_low(it):
                g = it.slot // GROUP
                pool.wait_ge(*at_group(high_taken, it, 1))
                pool.tensor_tensor(x_low[:, g, :], shifted[:, 0, 0:GROUP * P], x_high[:, g, :].bitcast(F32),
                                   ALU.subtract).then_inc(low_taken, 1)

            def make_table(it):
                pool.wait_ge(*loads(scales_in, it))
                pool.wait_ge(*at(roped, it, 8, 2))
                pool.sem_inc(held, 1)
                pool.tensor_tensor(rope[:, it.slot % 2, :, :].unsqueeze(1), rope_base[:, bass.ds(it.t % TPB, 1), :, :],
                                   scales[:].rearrange("p (o a d) -> p o a d", o=1, a=4), ALU.mult).then_inc(table_made, 1)

            def add_rotated(c):
                def do(it):
                    pool.wait_ge(*at(roped, it, 2 * c + 2))
                    dst = qk[:, it.slot % 4, c, :]
                    pool.tensor_tensor(dst, dst, rotated[:, c % 2, :], ALU.add).then_inc(rope_added, 1)
                return do

            def norm(n):
                def do(it):
                    b, c = it.slot % 2, TURN_ORDER[n]
                    if n == 0:
                        pool.wait_ge(*at(rs_step, it, 12))
                        pool.wait_ge(*at(rope_added, it, 4))
                    dst = qk[:, it.slot % 4, c, :].rearrange("p (h d) -> p h d", h=8)
                    r = rs_y[:, b, 8 * c:8 * c + 8].unsqueeze(2).to_broadcast([P, 8, HD])
                    pool.tensor_tensor(dst, dst, r, ALU.mult).then_inc(qk_normed, 1)
                return do

            def subtract_max(c):
                def do(it):
                    b = it.slot % 2
                    pool.wait_ge(*at(maxed, it, c + 1))
                    s = sc[:, b, c, :].rearrange("p (h k) -> p h k", h=8)
                    pool.tensor_tensor(s, s, mx[:, b, 8 * c:8 * c + 8].unsqueeze(2).to_broadcast([P, 8, 2 * WIN]),
                                       ALU.subtract).then_inc(shifted_max, 1)
                return do

            def scale_p(c):
                def do(it):
                    b = it.slot % 2
                    pool.wait_ge(*at(inverted, it, c + 1))
                    s = sc[:, b, c, :].rearrange("p (h k) -> p h k", h=8)
                    pool.tensor_tensor(s, s, rsum[:, b, 8 * c:8 * c + 8].unsqueeze(2).to_broadcast([P, 8, 2 * WIN]),
                                       ALU.mult).then_inc(p_scaled, 1)
                return do

            def ffn_rstd(it):
                pool.wait_ge(*at_group(stats_step, it, 10))
                pool.tensor_tensor(rstd[:], veps[:], minus_half[:], ALU.pow).then_inc(rstd_done, 1)

            def ffn_bias(it):
                pool.wait_ge(*loads(bias_in, it))
                pool.wait_ge(*at_group(y1_turned, it, 1))
                y = y1[:, it.slot // GROUP, :, :]
                pool.tensor_tensor(y, y, bias_row[:].unsqueeze(1).to_broadcast([P, GROUP, C]), ALU.add).then_inc(biased, 1)

            pool.wait_ge(consts, 48)
            pool.wait_ge(zeroed, 7)
            pipeline(pool, 0, UNITS, U, [
                (11, by_group(ffn_rstd)), (3, add_rotated(0)), (3, add_rotated(1)), (2, make_table),
                (5, subtract_max(0)), (3, add_rotated(2)), (3, add_rotated(3)), (0, by_group(stage)),
                (5, subtract_max(1)), (4, norm(0)), (4, norm(1)), (5, scale_p(0)), (4, norm(2)), (4, norm(3)),
                (5, scale_p(1)), (12, by_group(ffn_bias)), (0, by_group(take_low))])


def sandwich_kernel(nc, A, out):
    with ExitStack() as ctx:
        x = ctx.enter_context(nc.sbuf_tensor("x", [P, NT, C], F32))
        y = ctx.enter_context(nc.sbuf_tensor("y", [P, NT, C], F32))
        ident = ctx.enter_context(nc.sbuf_tensor("ident", [P, P], F32))
        psum = ctx.enter_context(nc.psum_tensor("psum", [P, 8, 512], F32))
        x_loaded = ctx.enter_context(nc.semaphore("x_loaded"))
        out_stored = ctx.enter_context(nc.semaphore("out_stored"))
        scratch = nc.dram_tensor("router_weights_dram", (NT, P), F32).ap()
        for part in ("Wqkv_high", "Wqkv_low"):
            A[part] = nc.dram_tensor(part + "_dram", (DEPTH, P, QKV), F32).ap()
        norms = Normalizer(nc, ctx)

        with nc.Block() as block:
            @block.sync
            def _(sp):
                sp.dma_start(x[:], A["x"].rearrange("b (t p) c -> p (b t) c", p=P)).then_inc(x_loaded, 16)
                sp.dma_start(ident[:], A["ident"]).then_inc(x_loaded, 16)
                sp.wait_ge(x_loaded, 32)

        def norm_x():
            norms.run(x, y, LN_EPS)

        def norm_branch_and_x():
            norms.run(y, y, LN_EPS, residual=x)
            norms.run(x, y, LN_EPS)

        causal_attention(nc, A, y, y, ident, psum, norm_x)
        routed_block(nc, A, y, y, ident, psum, scratch, norm_branch_and_x)
        linear_attention(nc, A, y, y, ident, psum, norm_branch_and_x)
        local_transformer(nc, A, y, ident, psum, norm_branch_and_x)
        norms.run(y, y, LN_EPS, residual=x)

        with nc.Block() as block:
            @block.sync
            def _(sp):
                sp.dma_start(out.rearrange("b (t p) c -> p (b t) c", p=P), x[:]).then_inc(out_stored, 16)
                sp.wait_ge(out_stored, 16)


def _lay_out(inputs):
    import numpy as np
    f = np.float32
    d = {k: np.asarray(v) for k, v in inputs.items()}
    masked = f(-3e38)
    a = {"x": d["L0_attn_x"], "ident": np.eye(P, dtype=f)}

    for k in ("w_kv_down", "w_kv_up", "w_q", "w_out"):
        a[k] = d["L0_attn_" + k]
    a["causal"] = np.where(np.tril(np.ones((P, P), bool)), f(0), masked).astype(f)

    for k in ("attention_mask", "position_ids", "router_w", "router_b", "wq", "wk", "wv", "wo", "w1", "w2", "ln1", "ln2"):
        a[k] = d["L0_ffn_" + k]
    positions = a.pop("position_ids")
    positions = np.concatenate([positions, np.repeat(positions[:, -1:], T - positions.shape[1], 1)], 1)
    a["pos"] = positions.reshape(B, TPB, P).transpose(2, 0, 1)
    token, column = np.arange(P)[:, None], np.arange(2 * T - P)[None]
    a["from_here"] = (column - (T - P) >= token).astype(f)
    slot = np.arange(P)
    a["slots"] = np.tile(np.where(slot < P - 1, slot, -1).astype(f), (P, 1))
    a["spare"] = np.tile(np.where(slot < P - 1, f(0), masked).astype(f), (P, 1))
    all_last = np.zeros((P, P), f)
    all_last[:, P - 1] = 1
    a["last_row"] = np.stack([np.eye(P, dtype=f), all_last], 1)
    a["halves_sign"] = np.tile(np.array([-1, 1], f), (P, 1))
    a["inv_freq"] = np.tile(f(1) / f(10000) ** (np.arange(0, 8, 2, dtype=f) / f(8)), (P, 1)).astype(f)
    a["head_cols"] = (np.arange(P)[:, None] // 8 == np.arange(16)[None]).astype(f)

    a["head_blocks"] = np.repeat(a["head_cols"], 8, 1)

    a["la_wT"] = np.stack([d["L1_attn_" + k].T for k in ("Wq", "Wk", "Wv", "Wo")], 1)
    a["la_bias_cols"] = np.stack([d["L1_attn_bq"], d["L1_attn_bk"]], 1)
    a["la_bias_rows"] = np.stack([d["L1_attn_bv"], d["L1_attn_bo"]], 0)
    a["la_PT"] = d["L1_attn_P"].T

    for k in ("Wqkv", "Wo", "W1", "W2"):
        a[k] = d["L1_ffn_" + k]
    b1 = d["L1_ffn_b1"]
    cols = np.zeros((DEPTH, P, 8), b1.dtype)
    for k, (lo, w) in enumerate(FCH):
        cols[:, :w, k] = b1[:, lo:lo + w]
        cols[:, :w, 3 + k] = b1[:, FF + lo:FF + lo + w]
    cols[:, :, 6], cols[:, :, 7] = d["L1_ffn_ln_g"], d["L1_ffn_ln_b"]
    a["cols"] = cols

    def rotated(v):
        return np.concatenate([v[:, HD // 2:], v[:, :HD // 2]], 1)
    q, k = d["L1_ffn_q_scale"], d["L1_ffn_k_scale"]
    a["rows"] = np.concatenate([d["L1_ffn_b2"], q, rotated(q), k, rotated(k)], 1)
    half = np.arange(0, HD, 2, dtype=f)
    inv_freq = f(1) / (f(10000) ** (half / f(HD))).astype(f)
    position = np.arange(T, dtype=f)
    freqs = (position[:, None] * inv_freq[None]).astype(f)
    base = ((half + f(0.4 * HD)) / f(1.4 * HD)).astype(f)
    scale = (base[None] ** ((position - T // 2) / f(WIN // 2)).astype(f)[:, None]).astype(f)
    freqs, scale = np.concatenate([freqs, freqs], 1), np.concatenate([scale, scale], 1)
    sign = np.concatenate([-np.ones(HD // 2, f), np.ones(HD // 2, f)])
    table = np.stack([np.cos(freqs) * scale, np.sin(freqs) * sign * scale,
                      np.cos(freqs) * (f(1) / scale), np.sin(freqs) * sign * (f(1) / scale)], 1)
    a["rope_base"] = table.reshape(TPB, P, 4, HD).transpose(1, 0, 2, 3).astype(f)
    row, column = np.arange(P)[:, None] % WIN, np.arange(2 * WIN)[None]
    window = np.where((column >= row) & (column <= row + WIN), f(0), masked).astype(f)
    window = np.repeat(window[:, None], TPB, 1)
    window[0:WIN, 0, 0:WIN] = masked
    a["win_mask"] = window
    keep = np.ones((P, TPB), f)
    keep[:, 0] = 0
    a["keep_carry"] = keep
    return {k: np.ascontiguousarray(v) for k, v in a.items()}


def kernel(**inputs):
    import concourse.bacc as bacc
    from concourse.bass_utils import run_bass_kernel_spmd

    nc = bacc.Bacc("TRN2", target_bir_lowering=False, num_devices=1)
    arrays, aps = {}, {}
    for name, a in _lay_out(inputs).items():
        arrays[f"in_{name}_dram"] = a
        aps[name] = nc.dram_tensor(f"in_{name}_dram", a.shape, mybir.dt.from_np(a.dtype), kind="ExternalInput").ap()
    out = nc.dram_tensor("out_dram", (B, T, C), F32, kind="ExternalOutput").ap()
    sandwich_kernel(nc, aps, out)
    result = run_bass_kernel_spmd(nc, [arrays], core_ids=[0])
    return result.results[0]["out_dram"]
```
